# Optimizing a Trainium2 kernel written in Bass

```python
import numpy as np
import jax
import jax.numpy as jnp

def _softmax(x, axis=-1):
    return jax.nn.softmax(x, axis=axis)

def _gelu(x):
    return jax.nn.gelu(x, approximate=True)

def _silu(x):
    return jax.nn.silu(x)

def _sigmoid(x):
    return jax.nn.sigmoid(x)

def _layernorm(x, axis=-1, eps=1e-05):
    m = jnp.mean(x, axis=axis, keepdims=True)
    v = jnp.var(x, axis=axis, keepdims=True)
    return (x - m) / jnp.sqrt(v + eps)

def _scatter_add(tgt, idx, src, axis=0):
    return tgt.at[idx].add(src)

def _segment_sum(src, seg, n):
    return jax.ops.segment_sum(src, seg, n)
kernel_name = 'mk_seq_postln_d2_jaxref_r8_389827'

def setup_inputs(seed: int=0):
    np.random.seed(seed)
    _w = jnp.asarray

    def _L0_attn_setup():
        import jax, jax.numpy as jnp
        import numpy as np
        C = 128
        H = 8
        MAX_SAMPLES = 32
        HALF_S = MAX_SAMPLES // 2
        S = 2 * HALF_S
        K = 64
        MAX_FREQ = 16.0
        MIN_FREQ = 1.0
        MAX_RECEPTIVE = HALF_S * MAX_FREQ
        B, L = (2, 128)

        def _gather_conv(x, wave_w, wave_b, kernel_w, kernel_b, out_w):
            Bx, Lx, Cx = x.shape
            D = Cx // H
            wave = (x @ wave_w.T + wave_b).reshape(Bx, Lx, H, 2)
            freq = MIN_FREQ + jax.nn.sigmoid(wave[..., 0]) * (MAX_FREQ - MIN_FREQ)
            phase = jnp.tanh(wave[..., 1]) * freq
            taps = jnp.arange(S, dtype=x.dtype) - HALF_S + 0.5
            offs = phase[..., None] + freq[..., None] * taps
            pos = jnp.arange(Lx, dtype=x.dtype)[None, :, None, None] + offs
            pos = jnp.clip(pos, 0.0, Lx - 1)
            i0f = jnp.floor(pos)
            frac = pos - i0f
            i0 = i0f.astype(jnp.int32)
            i1 = jnp.minimum(i0 + 1, Lx - 1)
            xh = x.reshape(Bx, Lx, H, D)
            b_idx = jnp.arange(Bx)[:, None, None, None]
            h_idx = jnp.arange(H)[None, None, :, None]
            g0 = xh[b_idx, i0, h_idx]
            g1 = xh[b_idx, i1, h_idx]
            gathered = g0 + frac[..., None] * (g1 - g0)
            kmat = (x @ kernel_w.T + kernel_b).reshape(Bx, Lx, H, K)
            bins = jnp.clip(jnp.floor((offs + MAX_RECEPTIVE) / (2.0 * MAX_RECEPTIVE) * K).astype(jnp.int32), 0, K - 1)
            w = jnp.take_along_axis(kmat, bins, axis=3)
            y = jnp.einsum('blhs,blhsd->blhd', w, gathered).reshape(Bx, Lx, Cx)
            return y @ out_w.T
        key = jax.random.key(seed)
        k1, k2, k3, k4 = jax.random.split(key, 4)
        x = jax.random.normal(k1, (B, L, C), dtype=jnp.float32)
        wave_w = 0.02 * jax.random.normal(k2, (2 * H, C), dtype=jnp.float32)
        wave_b = jnp.zeros((2 * H,), dtype=jnp.float32)
        lim_k = 0.1 * np.sqrt(6.0 / (H * K + C))
        kernel_w = jax.random.uniform(k3, (H * K, C), dtype=jnp.float32, minval=-lim_k, maxval=lim_k)
        kernel_b = jnp.zeros((H * K,), dtype=jnp.float32)
        lim_o = 0.1 * np.sqrt(6.0 / (C + C))
        out_w = jax.random.uniform(k4, (C, C), dtype=jnp.float32, minval=-lim_o, maxval=lim_o)
        return {'x': x, 'wave_w': wave_w, 'wave_b': wave_b, 'kernel_w': kernel_w, 'kernel_b': kernel_b, 'out_w': out_w}
    _L0_attn_in = _L0_attn_setup()

    def _L0_ffn_setup():
        import jax, jax.numpy as jnp
        import numpy as np
        from jax.scipy.linalg import expm
        B, S, D, E, K, NROT = (2, 256, 128, 8, 2, 3)
        DF = 4 * D
        EPS = 1e-05
        key = jax.random.key(seed)
        ks = jax.random.split(key, 8)
        s = lambda d: 1.0 / np.sqrt(d)
        return {'x': jax.random.normal(ks[0], (B, S, D), jnp.float32), 'ln_g': jnp.ones((D,), jnp.float32), 'ln_b': jnp.zeros((D,), jnp.float32), 'abel_w': jax.random.normal(ks[1], (D, D), jnp.float32) * s(D), 'abel_b': jnp.zeros((D,), jnp.float32), 'gate_w_moe': jax.random.normal(ks[2], (D, E), jnp.float32) * s(D), 'gate_b_moe': jnp.zeros((E,), jnp.float32), 'w1': jax.random.normal(ks[3], (E, D, DF), jnp.float32) * s(D), 'b1': jnp.zeros((E, DF), jnp.float32), 'w2': jax.random.normal(ks[4], (E, DF, D), jnp.float32) * s(DF), 'b2': jnp.zeros((E, D), jnp.float32), 'gens': jax.random.normal(ks[5], (NROT, D, D), jnp.float32) * 0.02, 'mix_w': jax.random.normal(ks[6], (2 * D, 1), jnp.float32) * s(2 * D), 'mix_b': jnp.zeros((1,), jnp.float32)}
    _L0_ffn_in = _L0_ffn_setup()

    def _L1_attn_setup():
        import jax, jax.numpy as jnp
        import numpy as np
        B, N, C = (2, 256, 128)
        H = 16
        HD = C // H
        key = jax.random.key(seed)
        ks = jax.random.split(key, 5)
        s = 0.02
        return {'x': jax.random.normal(ks[0], (B, N, C), dtype=jnp.float32), 'qkv_w': jax.random.normal(ks[1], (3 * C, C), dtype=jnp.float32) * s, 'qkv_b': jax.random.normal(ks[2], (3 * C,), dtype=jnp.float32) * s, 'proj_w': jax.random.normal(ks[3], (C, C), dtype=jnp.float32) * s, 'proj_b': jax.random.normal(ks[4], (C,), dtype=jnp.float32) * s}
    _L1_attn_in = _L1_attn_setup()

    def _L1_ffn_setup():
        import jax, jax.numpy as jnp
        import numpy as np
        E = 8
        TOP_K = 2
        DIM = 128
        HID = 256
        key = jax.random.key(seed)
        k1, k2, k3, k4, k5 = jax.random.split(key, 5)
        s = 0.02
        x = jax.random.normal(k1, (2, 256, DIM), dtype=jnp.float32)
        Wg = jax.random.normal(k2, (DIM, E), dtype=jnp.float32) * s
        W1 = jax.random.normal(k3, (E, DIM, HID), dtype=jnp.float32) * s
        W2 = jax.random.normal(k4, (E, DIM, HID), dtype=jnp.float32) * s
        W3 = jax.random.normal(k5, (E, HID, DIM), dtype=jnp.float32) * s
        return {'x': x, 'Wg': Wg, 'W1': W1, 'W2': W2, 'W3': W3}
    _L1_ffn_in = _L1_ffn_setup()
    _d = {'L0_attn_x': _L0_attn_in['x'], 'L0_attn_wave_w': _L0_attn_in['wave_w'], 'L0_attn_wave_b': _L0_attn_in['wave_b'], 'L0_attn_kernel_w': _L0_attn_in['kernel_w'], 'L0_attn_kernel_b': _L0_attn_in['kernel_b'], 'L0_attn_out_w': _L0_attn_in['out_w'], 'L0_ffn_ln_g': _L0_ffn_in['ln_g'], 'L0_ffn_ln_b': _L0_ffn_in['ln_b'], 'L0_ffn_abel_w': _L0_ffn_in['abel_w'], 'L0_ffn_abel_b': _L0_ffn_in['abel_b'], 'L0_ffn_gate_w_moe': _L0_ffn_in['gate_w_moe'], 'L0_ffn_gate_b_moe': _L0_ffn_in['gate_b_moe'], 'L0_ffn_w1': _L0_ffn_in['w1'], 'L0_ffn_b1': _L0_ffn_in['b1'], 'L0_ffn_w2': _L0_ffn_in['w2'], 'L0_ffn_b2': _L0_ffn_in['b2'], 'L0_ffn_gens': _L0_ffn_in['gens'], 'L0_ffn_mix_w': _L0_ffn_in['mix_w'], 'L0_ffn_mix_b': _L0_ffn_in['mix_b'], 'L1_attn_qkv_w': _L1_attn_in['qkv_w'], 'L1_attn_qkv_b': _L1_attn_in['qkv_b'], 'L1_attn_proj_w': _L1_attn_in['proj_w'], 'L1_attn_proj_b': _L1_attn_in['proj_b'], 'L1_ffn_Wg': _L1_ffn_in['Wg'], 'L1_ffn_W1': _L1_ffn_in['W1'], 'L1_ffn_W2': _L1_ffn_in['W2'], 'L1_ffn_W3': _L1_ffn_in['W3']}
    _x0 = _d['L0_attn_x']
    _d['L0_attn_x'] = jax.random.normal(jax.random.fold_in(jax.random.key(seed), 1), (8, 256, 128), dtype=_x0.dtype)
    del _x0
    return _d

def reference(L0_attn_x, L0_attn_wave_w, L0_attn_wave_b, L0_attn_kernel_w, L0_attn_kernel_b, L0_attn_out_w, L0_ffn_ln_g, L0_ffn_ln_b, L0_ffn_abel_w, L0_ffn_abel_b, L0_ffn_gate_w_moe, L0_ffn_gate_b_moe, L0_ffn_w1, L0_ffn_b1, L0_ffn_w2, L0_ffn_b2, L0_ffn_gens, L0_ffn_mix_w, L0_ffn_mix_b, L1_attn_qkv_w, L1_attn_qkv_b, L1_attn_proj_w, L1_attn_proj_b, L1_ffn_Wg, L1_ffn_W1, L1_ffn_W2, L1_ffn_W3):

    def _L0_attn_ref(x, wave_w, wave_b, kernel_w, kernel_b, out_w):
        import jax, jax.numpy as jnp
        import numpy as np
        C = 128
        H = 8
        MAX_SAMPLES = 32
        HALF_S = MAX_SAMPLES // 2
        S = 2 * HALF_S
        K = 64
        MAX_FREQ = 16.0
        MIN_FREQ = 1.0
        MAX_RECEPTIVE = HALF_S * MAX_FREQ
        B, L = (2, 128)

        def _gather_conv(x, wave_w, wave_b, kernel_w, kernel_b, out_w):
            Bx, Lx, Cx = x.shape
            D = Cx // H
            wave = (x @ wave_w.T + wave_b).reshape(Bx, Lx, H, 2)
            freq = MIN_FREQ + jax.nn.sigmoid(wave[..., 0]) * (MAX_FREQ - MIN_FREQ)
            phase = jnp.tanh(wave[..., 1]) * freq
            taps = jnp.arange(S, dtype=x.dtype) - HALF_S + 0.5
            offs = phase[..., None] + freq[..., None] * taps
            pos = jnp.arange(Lx, dtype=x.dtype)[None, :, None, None] + offs
            pos = jnp.clip(pos, 0.0, Lx - 1)
            i0f = jnp.floor(pos)
            frac = pos - i0f
            i0 = i0f.astype(jnp.int32)
            i1 = jnp.minimum(i0 + 1, Lx - 1)
            xh = x.reshape(Bx, Lx, H, D)
            b_idx = jnp.arange(Bx)[:, None, None, None]
            h_idx = jnp.arange(H)[None, None, :, None]
            g0 = xh[b_idx, i0, h_idx]
            g1 = xh[b_idx, i1, h_idx]
            gathered = g0 + frac[..., None] * (g1 - g0)
            kmat = (x @ kernel_w.T + kernel_b).reshape(Bx, Lx, H, K)
            bins = jnp.clip(jnp.floor((offs + MAX_RECEPTIVE) / (2.0 * MAX_RECEPTIVE) * K).astype(jnp.int32), 0, K - 1)
            w = jnp.take_along_axis(kmat, bins, axis=3)
            y = jnp.einsum('blhs,blhsd->blhd', w, gathered).reshape(Bx, Lx, Cx)
            return y @ out_w.T
        return _gather_conv(x, wave_w, wave_b, kernel_w, kernel_b, out_w)

    def _L0_ffn_ref(x, ln_g, ln_b, abel_w, abel_b, gate_w_moe, gate_b_moe, w1, b1, w2, b2, gens, mix_w, mix_b):
        import jax, jax.numpy as jnp
        import numpy as np
        from jax.scipy.linalg import expm
        B, S, D, E, K, NROT = (2, 256, 128, 8, 2, 3)
        DF = 4 * D
        EPS = 1e-05
        residual = x
        mu = jnp.mean(x, axis=-1, keepdims=True)
        var = jnp.mean((x - mu) ** 2, axis=-1, keepdims=True)
        xn = (x - mu) * jax.lax.rsqrt(var + EPS) * ln_g + ln_b
        abel = jax.nn.gelu(xn @ abel_w + abel_b, approximate=False)
        logits = xn @ gate_w_moe + gate_b_moe
        tw, ti = jax.lax.top_k(logits, K)
        tw = jax.nn.softmax(tw, axis=-1)
        onehot = (ti[..., None] == jnp.arange(E)).astype(tw.dtype)
        wdense = jnp.sum(tw[..., None] * onehot, axis=2)
        h = jax.nn.gelu(jnp.einsum('bsd,edf->besf', xn, w1) + b1[None, :, None, :], approximate=False)
        eo = jnp.einsum('besf,efd->besd', h, w2) + b2[None, :, None, :]
        moe = jnp.einsum('besd,bse->bsd', eo, wdense)
        rot = expm(gens[0])
        for i in range(1, NROT):
            rot = rot @ expm(gens[i])
        nonabel = moe @ rot
        combined = jnp.concatenate([abel, nonabel], axis=-1)
        g = jax.nn.sigmoid(combined @ mix_w + mix_b)
        return residual + abel * (1.0 - g) + nonabel * g

    def _L1_attn_ref(x, qkv_w, qkv_b, proj_w, proj_b):
        import jax, jax.numpy as jnp
        import numpy as np
        B, N, C = (2, 256, 128)
        H = 16
        HD = C // H
        b, n, c = x.shape
        qkv = x @ qkv_w.T + qkv_b
        qkv = qkv.reshape(b, n, 3, H, HD)
        qkv = jnp.transpose(qkv, (2, 0, 3, 1, 4))
        q, k, v = (qkv[0], qkv[1], qkv[2])
        scale = 1.0 / np.sqrt(HD).astype(np.float32)
        attn = jnp.einsum('bhqd,bhkd->bhqk', q, k) * scale
        attn = jax.nn.softmax(attn, axis=-1)
        out = jnp.einsum('bhqk,bhkd->bhqd', attn, v)
        out = jnp.transpose(out, (0, 2, 1, 3)).reshape(b, n, c)
        return out @ proj_w.T + proj_b

    def _L1_ffn_ref(x, Wg, W1, W2, W3):
        import jax, jax.numpy as jnp
        import numpy as np
        E = 8
        TOP_K = 2
        DIM = 128
        HID = 256
        B, T, C = x.shape
        xf = x.reshape(-1, C)
        logits = xf @ Wg
        top_w, top_i = jax.lax.top_k(logits, TOP_K)
        top_w = jax.nn.softmax(top_w, axis=-1)
        one_hot = jax.nn.one_hot(top_i, E, dtype=xf.dtype)
        combine = jnp.einsum('nk,nke->ne', top_w, one_hot)
        h = jnp.einsum('nc,ech->enh', xf, W1)
        g = jnp.einsum('nc,ech->enh', xf, W2)
        y = jnp.einsum('enh,ehc->enc', jax.nn.silu(h) * g, W3)
        out = jnp.einsum('enc,ne->nc', y, combine)
        return out.reshape(B, T, C)
    x = L0_attn_x
    x = _layernorm(x + _L0_attn_ref(x, L0_attn_wave_w, L0_attn_wave_b, L0_attn_kernel_w, L0_attn_kernel_b, L0_attn_out_w), axis=-1)
    x = _layernorm(x + _L0_ffn_ref(x, L0_ffn_ln_g, L0_ffn_ln_b, L0_ffn_abel_w, L0_ffn_abel_b, L0_ffn_gate_w_moe, L0_ffn_gate_b_moe, L0_ffn_w1, L0_ffn_b1, L0_ffn_w2, L0_ffn_b2, L0_ffn_gens, L0_ffn_mix_w, L0_ffn_mix_b), axis=-1)
    x = _layernorm(x + _L1_attn_ref(x, L1_attn_qkv_w, L1_attn_qkv_b, L1_attn_proj_w, L1_attn_proj_b), axis=-1)
    x = _layernorm(x + _L1_ffn_ref(x, L1_ffn_Wg, L1_ffn_W1, L1_ffn_W2, L1_ffn_W3), axis=-1)
    return x

_drawn_inputs = setup_inputs


def setup_inputs(seed=0):
    import zlib

    import numpy as np

    out = dict(_drawn_inputs(seed))
    spreads = {'L0_attn_wave_b': (0.0, 0.1),
     'L0_attn_kernel_b': (0.0, 0.1),
     'L0_ffn_ln_g': (1.0, 0.2),
     'L0_ffn_ln_b': (0.0, 0.1),
     'L0_ffn_abel_b': (0.0, 0.536),
     'L0_ffn_gate_b_moe': (0.0, 0.1),
     'L0_ffn_b1': (0.0, 0.497),
     'L0_ffn_b2': (0.0, 0.365)}
    factors = {'L1_attn_qkv_w': 8.0,
     'L1_attn_qkv_b': 8.0,
     'L1_attn_proj_w': 8.0,
     'L1_attn_proj_b': 2.781,
     'L1_ffn_Wg': 8.0,
     'L1_ffn_W1': 8.0,
     'L1_ffn_W2': 8.0,
     'L1_ffn_W3': 8.0}
    for name, (base, spread) in spreads.items():
        noise = np.random.default_rng([zlib.crc32(name.encode()), seed]).standard_normal(out[name].shape)
        drawn = base * np.exp(spread * noise) if base else spread * noise
        out[name] = jnp.asarray(drawn.astype(out[name].dtype))
    for name, factor in factors.items():
        out[name] = (out[name] * factor).astype(out[name].dtype)
    return out
```

```python
from contextlib import ExitStack

import concourse.bass as bass
from concourse import mybir

F32 = mybir.dt.float32
U32 = mybir.dt.uint32
ALU = mybir.AluOpType
ACT = mybir.ActivationFunctionType
AX = mybir.AxisListType.X

P = 128
B, L, C = 8, 256, 128
TOK = B * L
NT = TOK // P
H0, D0, BINS, TAPS = 8, 16, 64, 32
R8 = 8
A32 = L // R8
GB = 4
NBLK = L // R8 + 1
VW = NBLK * R8
AW = VW + R8
E = 8
DF = 512
HID = 256
NH, HD = 16, 8
CH = 512
TC = CH // P
EPS = 1e-5
MAGIC = 12582912.0
DELTA = 2.0 ** -17
SQUARINGS, DEGREE = 8, 8
NE_ = BINS + 1 + 2


def V(nc, own, eng):
    sem, state = own

    def link(ins):
        state[0] += 1
        ins.then_inc(sem, 1)
        eng.wait_ge(sem, state[0])
    return link


def loop_link(sem, eng, it, per):
    state = [0]

    def link(ins):
        state[0] += 1
        ins.then_inc(sem, 1)
        eng.wait_ge(sem, it * per + state[0])
    link.state = state
    return link


def bc(ap, axis, n):
    d = [list(x) for x in ap.ap]
    d.insert(axis, [0, n])
    return bass.AP(ap.tensor, ap.offset, d)


def build(nc, x_tok, x_T, x_conv, kw, kbias, outwT, cst, edges, ident_d, ln_gb, abel_w, abel_b, gate_w, gate_b,
          w1, b1, w2, b2, gens, mix_w, mix_b, wqkv, bqkv, wv, bv, proj_w, proj_b, wg, w31, w32, w33, kd, out):
    top = ExitStack()

    def alloc(ctx):
        def sb(name, shape, dt=F32):
            return ctx.enter_context(nc.sbuf_tensor(name, shape, dt))

        def ps(name, shape):
            return ctx.enter_context(nc.psum_tensor(name, shape, F32))

        def sem(name):
            s = ctx.enter_context(nc.semaphore(name))
            if "dve" not in name:
                started.append(s)
            return s
        return sb, ps, sem

    started = []

    def start_at_one(eng):
        for s in started:
            eng.sem_inc(s, 1)
        started.clear()

    with top:
        sb, _, _ = alloc(top)
        ident = sb("ident", [P, P])
        ones_row = sb("ones_row", [1, P])
        eps_t = sb("eps_t", [P, 1])
        sT = sb("sT", [P, TOK])
        rot = sb("rot", [P, P])

        par_ctx = ExitStack()
        psb, _, _ = alloc(par_ctx)
        wave = psb("wave", [P, NT, 2 * H0])
        par = psb("par", [P, 8, NT, H0])
        FR, INV, INV2, CE, CO, F2, O0, TMP = range(8)
        cst_s = psb("cst_s", [P, VW + 1])
        edges_s = psb("edges_s", [P, R8, NE_])
        with ExitStack() as ctx:
            sb, ps, sem = alloc(ctx)
            kw_s = sb("kw_s", [P, H0 * BINS + 2 * H0])
            kb_s = sb("kb_s", [1, H0 * BINS + 2 * H0])
            xs = [sb(f"xs{u}", [P, P]) for u in range(2)]
            kst = [sb(f"kst{u}", [P, H0 * BINS]) for u in range(2)]
            kps = [ps(f"kps{u}", [P, 512]) for u in range(2)]
            wps = [ps(f"wps{u}", [P, 512]) for u in range(2)]
            loaded, x_in = sem("loaded"), [sem(f"x_in{u}") for u in range(2)]
            mm = [sem(f"mm{u}") for u in range(2)]
            k_out = [sem(f"k_out{u}") for u in range(2)]
            w_out = [sem(f"w_out{u}") for u in range(2)]
            k_dma = [sem(f"k_dma{u}") for u in range(2)]
            wave_done, act_done, dve = sem("wave_done"), sem("act_done"), sem("dve")
            ones_set = sem("ones_set")
            block = ctx.enter_context(nc.Block())
            NK = H0 * BINS

            @block.sync
            def _(sp):
                start_at_one(sp)
                for dst, src in ((kw_s, kw), (kb_s, kbias), (ident, ident_d), (cst_s, cst), (edges_s, edges)):
                    sp.dma_start(dst[:], src).then_inc(loaded, 16)
                with sp.Fori(0, NT // 2) as r:
                    for u in range(2):
                        sp.wait_ge(mm[u], 1 + r)
                        sp.dma_start(xs[u][:], x_conv[bass.ds(r * 2 + u, 1), :, :].rearrange("o c p -> (o c) p"))\
                            .then_inc(x_in[u], 16)
                sp.wait_ge(loaded, 1 + 80)

            @block.tensor
            def _(pe):
                pe.wait_ge(loaded, 1 + 80)
                pe.wait_ge(ones_set, 1 + 1)
                with pe.Fori(0, NT // 2) as r:
                    for u in range(2):
                        pe.wait_ge(x_in[u], 1 + r * 16 + 16)
                        pe.wait_ge(k_out[u], 1 + r)
                        pe.wait_ge(w_out[u], 1 + r)
                        nc.tensor.matmul(kps[u][:, 0:NK], xs[u][:], kw_s[:, 0:NK], start=True, stop=False)
                        nc.tensor.matmul(kps[u][:, 0:NK], ones_row[:], kb_s[:, 0:NK], start=False, stop=True)
                        nc.tensor.matmul(wps[u][:, 0:16], xs[u][:], kw_s[:, NK:NK + 16], start=True, stop=False)
                        nc.tensor.matmul(wps[u][:, 0:16], ones_row[:], kb_s[:, NK:NK + 16], start=False, stop=True)\
                            .then_inc(mm[u], 1)

            @block.scalar
            def _(act):
                with act.Fori(0, NT // 2) as r:
                    for u in range(2):
                        act.wait_ge(mm[u], 1 + r + 1)
                        act.wait_ge(k_dma[u], 1 + r * 16)
                        nc.scalar.copy(kst[u][:], kps[u][:]).then_inc(k_out[u], 1)
                        act.wait_ge(k_out[u], 1 + r + 1)
                        act.dma_start(kd[bass.ds(r * 2 + u, 1), :, :].rearrange("o p n -> (o p) n"), kst[u][:])\
                            .then_inc(k_dma[u], 16)
                for u in range(2):
                    act.wait_ge(k_dma[u], 1 + 8 * 16)
                act.wait_ge(wave_done, 1 + 1)
                nc.scalar.activation(par[:, FR], wave[:, :, 0:H0], ACT.Sigmoid).then_inc(act_done, 1)
                nc.scalar.activation(par[:, TMP], wave[:, :, H0:], ACT.Tanh).then_inc(act_done, 1)

            @block.gpsimd
            def _(pool):
                nc.gpsimd.memset(eps_t[:], EPS)
                nc.gpsimd.memset(ones_row[:], 1.0).then_inc(ones_set, 1)

            @block.vector
            def _(v):
                with v.Fori(0, NT // 2) as r:
                    for u in range(2):
                        v.wait_ge(mm[u], 1 + r + 1)
                        nc.vector.tensor_copy(wave[:, bass.ds(r * 2 + u, 1), :],
                                              bc(wps[u][:, 0:16], 1, 1)).then_inc(w_out[u], 1)
                for u in range(2):
                    v.wait_ge(w_out[u], 1 + NT // 2)
                nc.vector.memset(sT[:, 0:1], 0.0).then_inc(wave_done, 1)
                v.wait_ge(act_done, 1 + 2)
                v.wait_ge(loaded, 1 + 80)
                link = V(nc, (dve, [0]), v)
                G = lambda k: par[:, k].rearrange("p n h -> p (n h)")
                link(nc.vector.tensor_scalar(G(FR), G(FR), 15.0, 1.0, ALU.mult, ALU.add))
                link(nc.vector.tensor_tensor(G(TMP), G(TMP), G(FR), ALU.mult))
                link(nc.vector.reciprocal(G(INV), G(FR)))
                link(nc.vector.tensor_scalar(G(INV2), G(INV), 0.5, None, ALU.mult))
                link(nc.vector.tensor_scalar(G(F2), G(FR), 2.0, None, ALU.mult))
                link(nc.vector.scalar_tensor_tensor(G(O0), G(FR), -(TAPS // 2 - 0.5), G(TMP), ALU.mult, ALU.add))
                link(nc.vector.tensor_scalar(G(CE), G(O0), cst_s[:, VW:VW + 1], -1.0, ALU.add, ALU.mult))
                link(nc.vector.tensor_tensor(G(CE), G(CE), G(INV2), ALU.mult))
                link(nc.vector.tensor_scalar(G(CO), G(CE), -0.5, None, ALU.add))

        with ExitStack() as ctx:
            sb, ps, sem = alloc(ctx)
            gs = sb("gs", [P, 6, P])
            Rk = sb("Rk", [P, 3, P])
            Y = sb("Y", [P, 6, P])
            r01 = sb("r01", [P, P])
            r01T = sb("r01T", [P, P])
            gp = ps("gp", [P, 2, 512])
            gp2 = ps("gp2", [P, 2, 512])
            g_in, pe_done, dve, = sem("g_in"), sem("e_pe"), sem("e_dve")
            block = ctx.enter_context(nc.Block())
            x2d = lambda t, a, b: t[:, a:b, :].rearrange("p m n -> p (m n)")

            started.clear()

            @block.sync
            def _(sp):
                for m in range(6):
                    sp.dma_start(gs[:, m, :], gens[m]).then_inc(g_in, 16)
                sp.wait_ge(g_in, 96)

            @block.vector
            def _(v):
                v.wait_ge(g_in, 96)
                link = V(nc, (dve, [0]), v)
                link(nc.vector.tensor_scalar(x2d(gs, 0, 6), x2d(gs, 0, 6), 2.0 ** -SQUARINGS, None, ALU.mult))
                link(nc.vector.tensor_copy(x2d(Rk, 0, 3), x2d(gs, 0, 3)))
                n = 0
                for k in range(DEGREE, 1, -1):
                    n += 1
                    v.wait_ge(pe_done, n)
                    link(nc.vector.scalar_tensor_tensor(x2d(Rk, 0, 3), gp[:, 0, 0:384], 1.0 / k, x2d(gs, 0, 3),
                                                        ALU.mult, ALU.add))
                n += 1
                v.wait_ge(pe_done, n)
                link(nc.vector.tensor_copy(x2d(Y, 0, 3), x2d(Rk, 0, 3)))
                link(nc.vector.tensor_copy(x2d(Y, 3, 6), gp[:, 1, 0:384]))
                for _ in range(SQUARINGS):
                    n += 1
                    v.wait_ge(pe_done, n)
                    for half in range(2):
                        link(nc.vector.scalar_tensor_tensor(x2d(Y, 3 * half, 3 * half + 3),
                                                            x2d(Y, 3 * half, 3 * half + 3), 2.0,
                                                            gp2[:, half, 0:384], ALU.mult, ALU.add))
                n += 1
                v.wait_ge(pe_done, n)
                link(nc.vector.tensor_tensor(r01[:], gp[:, 0, 0:P], Y[:, 0, :], ALU.add))
                link(nc.vector.tensor_tensor(r01[:], r01[:], Y[:, 1, :], ALU.add))
                n += 1
                v.wait_ge(pe_done, n)
                link(nc.vector.tensor_copy(r01T[:], gp[:, 1, 0:P]))
                n += 1
                v.wait_ge(pe_done, n)
                link(nc.vector.tensor_tensor(rot[:], gp2[:, 0, 0:P], r01[:], ALU.add))
                link(nc.vector.tensor_tensor(rot[:], rot[:], Y[:, 2, :], ALU.add))
                link(nc.vector.tensor_tensor(rot[:], rot[:], ident[:], ALU.add))

            @block.tensor
            def _(pe):
                d = 2
                for k in range(DEGREE, 1, -1):
                    pe.wait_ge(dve, d)
                    for m in range(3):
                        last = nc.tensor.matmul(gp[:, 0, m * P:(m + 1) * P], gs[:, 3 + m, :], Rk[:, m, :],
                                                start=True, stop=True)
                    last.then_inc(pe_done, 1)
                    d += 1
                pe.wait_ge(dve, d)
                for m in range(3):
                    last = nc.tensor.transpose(gp[:, 1, m * P:(m + 1) * P], Rk[:, m, :], ident[:])
                last.then_inc(pe_done, 1)
                d += 2
                for _ in range(SQUARINGS):
                    pe.wait_ge(dve, d)
                    for m in range(3):
                        nc.tensor.matmul(gp2[:, 0, m * P:(m + 1) * P], Y[:, 3 + m, :], Y[:, m, :],
                                         start=True, stop=True)
                    for m in range(3):
                        last = nc.tensor.matmul(gp2[:, 1, m * P:(m + 1) * P], Y[:, m, :], Y[:, 3 + m, :],
                                                start=True, stop=True)
                    last.then_inc(pe_done, 1)
                    d += 2
                pe.wait_ge(dve, d)
                nc.tensor.matmul(gp[:, 0, 0:P], Y[:, 3, :], Y[:, 1, :], start=True, stop=True).then_inc(pe_done, 1)
                d += 2
                pe.wait_ge(dve, d)
                nc.tensor.transpose(gp[:, 1, 0:P], r01[:], ident[:]).then_inc(pe_done, 1)
                d += 1
                pe.wait_ge(dve, d)
                nc.tensor.matmul(gp2[:, 0, 0:P], r01T[:], Y[:, 2, :], start=True, stop=True).then_inc(pe_done, 1)

        with ExitStack() as ctx:
            sb, ps, sem = alloc(ctx)
            xn = sb("xn", [P, NT, P])
            XM = sb("XM", [P, NT, H0, P])
            XT = sb("XT", [P, TOK])
            ow = sb("ow", [P, P])
            Ks = [sb(f"Ks{u}", [P, H0, NBLK]) for u in range(2)]
            Kr = [sb(f"Kr{u}", [P, H0, BINS]) for u in range(2)]
            tts = [sb(f"tt{u}", [P, 2, H0, VW]) for u in range(2)]
            cls = [sb(f"cl{u}", [P, 2, H0, VW]) for u in range(2)]
            Ams = [sb(f"Am{u}", [P, H0, AW]) for u in range(2)]
            AT = sb("AT", [P, 2 * H0, P])
            yS = sb("yS", [P, P])
            t67 = sb("t67", [P, H0, NE_])
            nl = sb("nl", [P, H0, A32 + 2])
            dl = sb("dl", [P, H0, A32 + 1])
            ends = sb("ends", [P, H0, 2])
            ea = sb("ea", [P, 2, H0, 2])
            eg = sb("eg", [P, H0, 2])
            sm = sb("sm", [P, 3, H0])
            map_s = sb("map_s", [P, 2, 3, H0])
            spare = sb("spare", [P, 2])
            map_set = sem("map_set")
            q1 = sb("q1", [P, 2, H0, NBLK])
            q2 = sb("q2", [P, 2, H0, NBLK])
            dW = sb("dW", [P, H0, NBLK])
            tp = [ps(f"tp{k}", [P, 512]) for k in range(4)]
            yps = ps("yps", [P, 512])
            ops = ps("ops", [P, 512])
            ld, kin = sem("ld"), [sem(f"kin{u}") for u in range(2)]
            xm_set, xm_done, const_set = sem("xm_set"), sem("xm_done"), sem("const_set")
            t_ready, c_ready, g_ready, a_ready = sem("t_ready"), sem("c_ready"), sem("g_ready"), sem("a_ready")
            tp_ready, at_ready, y_ready, ys_ready = sem("tp_ready"), sem("at_ready"), sem("y_ready"), sem("ys_ready")
            o_ready, o_used, A_ready = sem("o_ready"), sem("o_used"), sem("A_ready")
            dve = sem("g_dve")
            block = ctx.enter_context(nc.Block())
            flat = lambda ap: ap.rearrange("p a h v -> p (a h v)")

            def in_turn(eng, tile):
                tile(0, 0, 0, None)
                with eng.Fori(0, R8 - 1) as k:
                    tile(2 * k + 1, k, 1, (2 * k, k, 0))
                    tile(2 * k + 2, k + 1, 0, (2 * k + 1, k, 1))
                tile(NT - 1, R8 - 1, 1, (NT - 2, R8 - 1, 0))

            @block.sync
            def _(sp):
                start_at_one(sp)
                sp.dma_start(xn[:], x_tok.rearrange("(n p) c -> p n c", p=P)).then_inc(ld, 16)
                sp.dma_start(XT[:], x_T).then_inc(ld, 16)
                sp.dma_start(ow[:], outwT).then_inc(ld, 16)
                sp.wait_ge(ld, 1 + 48)

                def tile(n, r, g, before):
                    if before:
                        sp.wait_ge(A_ready, n)
                    row = H0 * BINS
                    base = kd[0:1, 0:1, 0:1]
                    off = n * (P * row)
                    for b in range(GB):
                        sp.dma_start(
                            Ks[g][b * A32:(b + 1) * A32, :, :],
                            bass.AP(base.tensor, off + b * A32 * row + A32 - 1,
                                    [[row - 1, A32], [BINS, H0], [1, NBLK]])).then_inc(kin[g], 16)
                    sp.dma_start(Kr[g][:].rearrange("p h k -> p (h k)"),
                                 bass.AP(base.tensor, off, [[row, P], [1, row]])).then_inc(kin[g], 16)

                in_turn(sp, tile)

            @block.gpsimd
            def _(pool):
                nc.gpsimd.memset(spare[:], 0.0)
                nc.gpsimd.memset(XM[:].rearrange("p n h c -> p (n h c)"), 0.0).then_inc(xm_set, 1)
                for u in range(2):
                    nc.gpsimd.memset(Ams[u][:].rearrange("p h v -> p (h v)"), 0.0)
                nc.gpsimd.memset(ea[:].rearrange("p a h v -> p (a h v)"), 2.0)
                nc.gpsimd.memset(eg[:, :, 0:1], 1.0)
                nc.gpsimd.memset(eg[:, :, 1:2], -1.0).then_inc(const_set, 1)
                pool.wait_ge(xm_set, 1 + 1)
                pool.wait_ge(ld, 1 + 48)
                xm0 = XM[:, 0, 0, 0:D0]
                for n in range(NT):
                    dst = bass.AP(xm0.tensor, xm0.offset + n * H0 * P,
                                  [list(xm0.ap[0]), [P + D0, H0], [1, D0]])
                    nc.gpsimd.tensor_copy(dst, xn[:, n, :].rearrange("p (h c) -> p h c", h=H0)).then_inc(xm_done, 1)

                def tile(n, r, g, before):
                    if before:
                        pool.wait_ge(A_ready, n)
                    nc.gpsimd.tensor_copy(map_s[:, g], par[:, INV2:CO + 1, bass.ds(n, 1), :].rearrange(
                        "p k a h -> p k (a h)")).then_inc(map_set, 1)
                    pool.wait_ge(map_set, 1 + n + 1)
                    nc.gpsimd.tensor_tensor(spare[:, g:g + 1], spare[:, g:g + 1], spare[:, g:g + 1], ALU.add)
                    for h in range(H0):
                        for odd in range(2):
                            last = nc.gpsimd.tensor_scalar(tts[g][:, odd, h, :], cst_s[:, 0:VW],
                                                           map_s[:, g, 0, h:h + 1], map_s[:, g, 1 + odd, h:h + 1],
                                                           ALU.mult, ALU.add)
                    last.then_inc(t_ready, 1)

                in_turn(pool, tile)

            @block.scalar
            def _(act):
                def transposed(n, r, g):
                    act.wait_ge(tp_ready, 1 + n + 1)
                    act.wait_ge(y_ready, 1 + n)
                    for k in range(4):
                        last = nc.scalar.copy(AT[:, 4 * k:4 * k + 4, :].rearrange("p a b -> p (a b)"), tp[k][:])
                    last.then_inc(at_ready, 1)

                def mixed(n, r, g):
                    act.wait_ge(y_ready, 1 + n + 1)
                    act.wait_ge(o_ready, 1 + n)
                    nc.scalar.copy(yS[:], yps[:, 0:P]).then_inc(ys_ready, 1)

                def tile(n, r, g, before):
                    act.wait_ge(t_ready, 1 + n + 1)
                    act.wait_ge(A_ready, n) if before else None
                    nc.scalar.activation(flat(cls[g][:]), flat(tts[g][:]), ACT.Relu).then_inc(c_ready, 1)
                    if before:
                        transposed(*before)
                    act.wait_ge(g_ready, 1 + n + 1)
                    for h in range(H0):
                        last = nc.scalar.activation(
                            tts[g][:, :, h, :], cls[g][:, :, h, :], ACT.Abs,
                            scale=par[:, F2, bass.ds(n, 1), h:h + 1].rearrange("p a b -> p (a b)"))
                    last.then_inc(a_ready, 1)
                    if before:
                        mixed(*before)

                act.wait_ge(xm_done, 1 + NT)
                in_turn(act, tile)
                transposed(NT - 1, R8 - 1, 1)
                mixed(NT - 1, R8 - 1, 1)

            @block.tensor
            def _(pe):
                pe.wait_ge(xm_done, 1 + NT)
                pe.wait_ge(ld, 1 + 48)
                with pe.Fori(0, R8) as r:
                    for g in range(2):
                        n = r * 2 + g
                        pe.wait_ge(A_ready, 1 + n + 1)
                        pe.wait_ge(at_ready, 1 + n)
                        for k in range(4):
                            for j in range(4):
                                h, jc = (4 * k + j) // 2, j % 2
                                last = nc.tensor.transpose(tp[k][:, j * P:(j + 1) * P],
                                                           Ams[g][:, h, R8 + jc * P:R8 + (jc + 1) * P], ident[:])
                        last.then_inc(tp_ready, 1)
                        pe.wait_ge(at_ready, 1 + n + 1)
                        pe.wait_ge(ys_ready, 1 + n)
                        for b in range(GB):
                            for q in range(2 * H0):
                                h, jc = q // 2, q % 2
                                last = nc.tensor.matmul(yps[:, b * A32:(b + 1) * A32],
                                                        XM[:, (g * GB + b) * 2 + jc, h, :],
                                                        AT[:, q, b * A32:(b + 1) * A32],
                                                        start=(q == 0), stop=(q == 2 * H0 - 1))
                        last.then_inc(y_ready, 1)
                        pe.wait_ge(ys_ready, 1 + n + 1)
                        pe.wait_ge(o_used, 1 + n)
                        nc.tensor.matmul(ops[:, 0:P], ow[:], yS[:], start=True, stop=True).then_inc(o_ready, 1)

            @block.vector
            def _(v):
                v.wait_ge(const_set, 1 + 1)
                v.wait_ge(ld, 1 + 48)
                PER = 37

                def add_residual(n, r, g):
                    v.wait_ge(o_ready, 1 + n + 1)
                    dst = sT[:, g * GB * L:(g + 1) * GB * L].rearrange("p (b a e) -> p b a e", b=GB, e=R8)
                    src = XT[:, g * GB * L:(g + 1) * GB * L].rearrange("p (b a e) -> p b a e", b=GB, e=R8)
                    nc.vector.tensor_tensor(
                        dst[:, :, :, bass.ds(r, 1)].rearrange("p b a e -> p b (a e)"),
                        src[:, :, :, bass.ds(r, 1)].rearrange("p b a e -> p b (a e)"),
                        ops[:, 0:P].rearrange("p (b a) -> p b a", b=GB), ALU.subtract).then_inc(o_used, 1)

                def tile(n, r, g, before):
                    tt_, cl, Am = tts[g], cls[g], Ams[g]
                    link = loop_link(dve, v, n, PER)
                    pr = lambda k: par[:, k, bass.ds(n, 1), :].rearrange("p a h -> p (a h)")

                    v.wait_ge(c_ready, 1 + n + 1)
                    link(nc.vector.tensor_scalar(flat(cl[:]), flat(cl[:]), float(TAPS // 2 - 1), MAGIC,
                                                 ALU.min, ALU.add))
                    nc.vector.scalar_tensor_tensor(flat(cl[:]), flat(cl[:]), MAGIC, flat(tt_[:]),
                                                   ALU.subtract, ALU.subtract).then_inc(g_ready, 1)
                    ed = bc(edges_s[:, bass.ds(r, 1), :].rearrange("p a e -> p (a e)"), 1, H0)
                    link(nc.vector.tensor_tensor(t67[:], ed, bc(pr(O0), 2, NE_), ALU.subtract))
                    link(nc.vector.tensor_tensor(t67[:], t67[:], bc(pr(INV), 2, NE_), ALU.mult))
                    t67f = t67[:].rearrange("p h e -> p (h e)")
                    link(nc.vector.tensor_scalar(t67f, t67f, 0.5 - DELTA, 0.0, ALU.add, ALU.max))
                    link(nc.vector.tensor_scalar(t67f, t67f, float(TAPS), MAGIC, ALU.min, ALU.add))
                    link(nc.vector.tensor_scalar(t67f, t67f, -MAGIC, None, ALU.add))
                    N0, NL = t67[:, :, BINS + 1], t67[:, :, BINS + 2]
                    N0b = bc(t67[:, :, BINS + 1:BINS + 2].rearrange("p h a -> p (h a)"), 2, A32 + 2)
                    NLb = bc(t67[:, :, BINS + 2:BINS + 3].rearrange("p h a -> p (h a)"), 2, A32 + 2)
                    v.wait_ge(kin[g], 1 + (r + 1) * 80)
                    link(nc.vector.tensor_tensor(nl[:], t67[:, :, 0:A32 + 2], N0b, ALU.min))
                    link(nc.vector.tensor_tensor(dl[:], nl[:, :, 1:], nl[:, :, 0:A32 + 1], ALU.subtract))
                    link(nc.vector.tensor_tensor(dl[:], dl[:], Kr[g][:, :, 0:A32 + 1], ALU.mult))
                    link(nc.vector.tensor_reduce(ends[:, :, 0:1], dl[:], AX, ALU.add))
                    link(nc.vector.tensor_tensor(nl[:], t67[:, :, A32 - 1:BINS + 1], NLb, ALU.max))
                    link(nc.vector.tensor_tensor(dl[:], nl[:, :, 1:], nl[:, :, 0:A32 + 1], ALU.subtract))
                    link(nc.vector.tensor_tensor(dl[:], dl[:], Kr[g][:, :, A32 - 1:BINS], ALU.mult))
                    link(nc.vector.tensor_reduce(ends[:, :, 1:2], dl[:], AX, ALU.add))
                    wide = lambda ap: bass.AP(ap.tensor, ap.offset, [list(ap.ap[0]), [0, H0]])
                    e_first = edges_s[:, bass.ds(r, 1), BINS + 1:BINS + 2].rearrange("p a e -> p (a e)")
                    e_last = edges_s[:, bass.ds(r, 1), BINS + 2:BINS + 3].rearrange("p a e -> p (a e)")
                    for side, cnt, add, edge, cmp, lim in ((0, N0, 0.0, e_first, ALU.is_ge, TAPS - 0.5),
                                                           (1, NL, -1.0, e_last, ALU.is_le, 0.5)):
                        link(nc.vector.scalar_tensor_tensor(sm[:, 0, :], cnt, add, pr(FR), ALU.add, ALU.mult))
                        link(nc.vector.tensor_tensor(sm[:, 1, :], sm[:, 0, :], wide(edge), ALU.subtract))
                        link(nc.vector.tensor_tensor(sm[:, 1, :], sm[:, 1, :], pr(O0), ALU.add))
                        link(nc.vector.scalar_tensor_tensor(sm[:, 1, :], sm[:, 1, :], -1.0, sm[:, 1, :],
                                                            ALU.mult, ALU.max))
                        link(nc.vector.tensor_scalar(sm[:, 0, :], cnt, lim, 4.0, cmp, ALU.mult))
                        link(nc.vector.tensor_tensor(ea[:, 0, :, side], sm[:, 1, :], sm[:, 0, :], ALU.add))

                    link(nc.vector.tensor_tensor(dW[:, :, 1:], Ks[g][:, :, 0:NBLK - 1], Ks[g][:, :, 1:],
                                                 ALU.subtract))
                    v.wait_ge(a_ready, 1 + n + 1)
                    ta = tt_[:, :, :, bass.ds(R8 - r, 1)]
                    tg = cl[:, 0, :, bass.ds(R8 - r, 1)]
                    d4 = [list(x) for x in ta.ap]
                    d3 = [list(x) for x in tg.ap]
                    nc.vector.memset(sm[:, 2, 0:1], 0.0)
                    link(nc.vector.tensor_copy(bass.AP(ta.tensor, ta.offset, d4[:-1] + [[L - 1, 2]]), ea[:]))
                    nc.vector.memset(sm[:, 2, 0:1], 0.0)
                    link(nc.vector.tensor_copy(bass.AP(tg.tensor, tg.offset, d3[:-1] + [[L - 1, 2]]), eg[:]))
                    blk = lambda t: t[:].rearrange("p a h (c q) -> p (a h c) q", q=R8)[:, :, 0:1]\
                        .rearrange("p c q -> p (c q)")
                    q1f, q2f = (t[:].rearrange("p a h c -> p (a h c)") for t in (q1, q2))
                    link(nc.vector.tensor_scalar(q1f, blk(tt_), 1.0, -1.0, ALU.min, ALU.add))
                    link(nc.vector.scalar_tensor_tensor(q2f, blk(cl), 0.0, q1f, ALU.is_lt, ALU.mult))
                    link(nc.vector.tensor_tensor(q1[:, 0], q2[:, 0], q2[:, 1], ALU.add))
                    link(nc.vector.tensor_tensor(q1[:, 1, :, 1:], q1[:, 0, :, 1:], dW[:, :, 1:], ALU.mult))
                    tE = tt_[:, 0].rearrange("p h v -> p (h v)")
                    tO = tt_[:, 1].rearrange("p h v -> p (h v)")
                    link(nc.vector.tensor_scalar(tO, tO, 1.0, -2.0, ALU.min, ALU.add))
                    link(nc.vector.scalar_tensor_tensor(tE, tE, 1.0, tO, ALU.min, ALU.add))
                    if before:
                        v.wait_ge(tp_ready, n)
                    link(nc.vector.tensor_tensor(
                        Am[:, :, bass.ds(r, VW)].rearrange("p h (c q) -> p h c q", q=R8),
                        tt_[:, 0].rearrange("p h (c q) -> p h c q", q=R8),
                        bc(Ks[g][:], 3, R8), ALU.mult))
                    a8 = Am[:, :, bass.ds(r + R8, 1)]
                    d3 = [list(x) for x in a8.ap]
                    a8 = bass.AP(a8.tensor, a8.offset, d3[:-1] + [[R8, NBLK - 1]])
                    link(nc.vector.tensor_tensor(a8, a8, q1[:, 1, :, 1:], ALU.add))
                    ab = Am[:, :, R8:R8 + 1]
                    ab = bass.AP(ab.tensor, ab.offset, [list(x) for x in ab.ap][:-1] + [[L - 1, 2]])
                    nc.vector.tensor_tensor(ab, ab, ends[:], ALU.subtract).then_inc(A_ready, 1)
                    if before:
                        add_residual(*before)
                    assert link.state[0] == PER, link.state[0]

                in_turn(v, tile)
                add_residual(NT - 1, R8 - 1, 1)

        par_ctx.close()
        sb, _, _ = alloc(top)
        xs_all = sb("xs_all", [P, NT, P])
        xT_all = sb("xT_all", [P, TOK])
        return finish(nc, alloc, start_at_one, ident, ones_row, eps_t, sT, rot, xs_all, xT_all, ln_gb, abel_w, abel_b, gate_w, gate_b,
                      w1, b1, w2, b2, mix_w, mix_b, wqkv, bqkv, wv, bv, proj_w, proj_b, wg, w31, w32, w33, out)


def finish(nc, alloc, start_at_one, ident, ones_row, eps_t, sT, rot, xs_all, xT_all, ln_gb, abel_w, abel_b, gate_w, gate_b,
           w1, b1, w2, b2, mix_w, mix_b, wqkv, bqkv, wv, bv, proj_w, proj_b, wg, w31, w32, w33, out):
    def norm_link(link, v, src, dst, mv, stats, std, sqrt_go, sqrt_done, n, count, done=None):
        for t in range(count):
            ins = nc.vector.bn_stats(stats[:, t, :], src[:, t, :])
        link(ins)
        one = lambda k: stats[:, 0:count, k:k + 1]
        link(nc.vector.tensor_tensor(mv[:, 0:count, 0:1], one(1), one(4), ALU.add))
        link(nc.vector.tensor_tensor(one(0), one(1), one(4), ALU.subtract))
        link(nc.vector.tensor_tensor(one(2), one(2), one(5), ALU.add))
        link(nc.vector.scalar_tensor_tensor(one(0), one(0), C / 4.0, one(0), ALU.mult, ALU.mult))
        link(nc.vector.tensor_scalar(mv[:, 0:count, 0:1], mv[:, 0:count, 0:1], 0.5, None, ALU.mult))
        nc.vector.tensor_tensor(mv[:, 0:count, 1:2], one(2), one(0), ALU.add).then_inc(sqrt_go, 1)
        v.wait_ge(sqrt_done, 1 + n + 1)
        link(nc.vector.reciprocal(std[:, 0:count], std[:, 0:count]))
        for t in range(count):
            ins = nc.vector.tensor_scalar(dst[:, t, :], src[:, t, :], mv[:, t, 0:1], std[:, t:t + 1],
                                          ALU.subtract, ALU.mult)
        link(ins) if done is None else ins.then_inc(done, 1)

    def route_link(link, v, lg_ps, lg, m8, i8, i8f, dd, wd, it8, exp_go, exp_done, n):
        link(nc.vector.tensor_copy(lg[:], lg_ps))
        nc.vector.memset(dd[:, 0, 0:1], 0.0)
        for t in range(TC):
            ins = nc.vector.max(m8[:, t, :], lg[:, t, :])
        link(ins)
        nc.vector.memset(dd[:, 0, 0:1], 0.0)
        for t in range(TC):
            ins = nc.vector.max_index(i8[:, t, :], m8[:, t, :], lg[:, t, :])
        link(ins)
        link(nc.vector.tensor_copy(i8f[:], i8[:, :, 0:2]))
        nc.vector.tensor_tensor(dd[:, :, 0:1], m8[:, :, 1:2], m8[:, :, 0:1], ALU.subtract).then_inc(exp_go, 1)
        v.wait_ge(exp_done, 1 + n + 1)
        link(nc.vector.tensor_scalar(dd[:, :, 1:2], dd[:, :, 0:1], 1.0, None, ALU.add))
        link(nc.vector.reciprocal(dd[:, :, 1:2], dd[:, :, 1:2]))
        link(nc.vector.tensor_tensor(dd[:, :, 0:1], dd[:, :, 0:1], dd[:, :, 1:2], ALU.mult))
        for t in range(TC):
            link(nc.vector.tensor_scalar(wd[:, t, :], it8[:], i8f[:, t, 0:1], dd[:, t, 1:2],
                                         ALU.is_equal, ALU.mult))
            link(nc.vector.tensor_scalar(lg[:, t, :], it8[:], i8f[:, t, 1:2], dd[:, t, 0:1],
                                         ALU.is_equal, ALU.mult))
        link(nc.vector.tensor_tensor(wd[:], wd[:], lg[:], ALU.add))

    flat2 = lambda ap: ap.rearrange("p a b -> p (a b)")

    with ExitStack() as ctx:
        sb, ps, sem = alloc(ctx)
        w1s = sb("w1s", [P, E, DF])
        w2s = sb("w2s", [P, E, 4, C])
        b1s = sb("b1s", [P, E * 4])
        b2s = sb("b2s", [E, C])
        aw = sb("aw", [P, C])
        abr = sb("abr", [1, C])
        gw = sb("gw", [P, E])
        gbr = sb("gbr", [1, E])
        gb = sb("gb", [P, 2])
        mixs = sb("mixs", [P, 2, C])
        mb = sb("mb", [P, 1])
        it8 = sb("it8", [P, E])
        sS = sb("sS", [P, CH])
        x1 = sb("x1", [P, TC, C])
        xh = sb("xh", [P, TC, C])
        xnT = sb("xnT", [P, CH])
        stats = sb("stats", [P, TC, 6])
        mv = sb("mv", [P, TC, 2])
        std = sb("std", [P, TC])
        lg = sb("lg", [P, TC, E])
        m8 = sb("m8", [P, TC, 8])
        i8 = sb("i8", [P, TC, 8], U32)
        i8f = sb("i8f", [P, TC, 2])
        dd = sb("dd", [P, TC, 2])
        wd = sb("wd", [P, TC, E])
        wT = sb("wT", [E, CH])
        abel = sb("abel", [P, TC, C])
        hT = [sb(f"hT{u}", [P, 4, CH]) for u in range(2)]
        moe = sb("moe", [P, TC, C])
        moeT = sb("moeT", [P, CH])
        nona = sb("nona", [P, TC, C])
        junk = sb("junk", [P, C])
        z = sb("z", [P, TC, 2])
        y = sb("y", [P, TC, C])
        tpa, lps, eo = ps("tpa", [P, 512]), ps("lps", [P, 512]), [ps(f"eo{u}", [P, 512]) for u in range(2)]
        hps = [ps(f"hps{u}", [P, 512]) for u in range(2)]
        ab_ps = ps("ab_ps", [P, 512])
        wt_ps = ps("wt_ps", [P, 512])
        wl_iota = sem("wl_iota")
        wl, staged, dve = sem("wl"), sem("staged"), sem("f_dve")
        tp_s, tp_x, tp_w, tp_m, tp_y = (sem(f"tp_{k}") for k in "sxwmy")
        sqrt_go, sqrt_done, exp_go, exp_done = sem("sqrt_go"), sem("sqrt_done"), sem("exp_go"), sem("exp_done")
        xn_ready, lg_ready, wT_ready, ab_ready, ab_act = (sem(k) for k in ("xn_ready", "lg_ready", "wT_ready",
                                                                            "ab_ready", "ab_act"))
        bias_ready, h_ps, h_ready, e_ready, e_used = (sem(k) for k in ("bias_ready", "h_ps", "h_ready", "e_ready", "e_used"))
        moe_ready, moeT_ready, rot_ready, z_go, z_done = (sem(k) for k in ("moe_ready", "moeT_ready", "rot_ready",
                                                                           "z_go", "z_done"))
        x2_ready, x2T_done = sem("x2_ready"), sem("x2T_done")
        block = ctx.enter_context(nc.Block())

        @block.sync
        def _(sp):
            start_at_one(sp)
            for dst, src in ((w1s[:], w1.rearrange("e d f -> d e f")),
                             (w2s[:], w2.rearrange("e (k f) d -> f e k d", f=P)),
                             (b1s[:], b1), (b2s[:], b2), (aw[:], abel_w), (abr[:], abel_b), (gw[:], gate_w),
                             (gbr[:], gate_b), (gb[:], ln_gb), (mixs[:].rearrange("p a c -> p (a c)"), mix_w),
                             (mb[:], mix_b)):
                sp.dma_start(dst, src).then_inc(wl, 16)
            sp.wait_ge(wl, 1 + 176)

        @block.gpsimd
        def _(pool):
            nc.gpsimd.iota(it8[:], pattern=[[1, E]], base=0, channel_multiplier=0,
                           allow_small_or_imprecise_dtypes=True).then_inc(wl_iota, 1)
            with pool.Fori(0, TOK // CH) as q:
                pool.wait_ge(tp_s, 1 + q)
                nc.gpsimd.tensor_copy(sS[:], sT[:, bass.ds(q * CH, CH)]).then_inc(staged, 1)

        @block.tensor
        def _(pe):
            pe.wait_ge(wl, 1 + 176)
            with pe.Fori(0, TOK // CH) as q:
                pe.wait_ge(staged, 1 + q + 1)
                for t in range(TC):
                    last = nc.tensor.transpose(tpa[:, t * P:(t + 1) * P], sS[:, t * P:(t + 1) * P], ident[:])
                last.then_inc(tp_s, 1)
                pe.wait_ge(sqrt_go, 1 + 3 * q + 2)
                pe.wait_ge(bias_ready, 1 + 2 * q + 1)
                for t in range(TC):
                    last = nc.tensor.transpose(tpa[:, t * P:(t + 1) * P], xh[:, t, :], ident[:])
                last.then_inc(tp_x, 1)
                pe.wait_ge(xn_ready, 1 + q + 1)
                for t in range(TC):
                    tok = xnT[:, t * P:(t + 1) * P]
                    nc.tensor.matmul(lps[:, t * E:(t + 1) * E], tok, gw[:], start=True, stop=False)
                    last = nc.tensor.matmul(lps[:, t * E:(t + 1) * E], ones_row[:], gbr[:], start=False, stop=True)
                last.then_inc(lg_ready, 1)
                for t in range(TC):
                    tok = xnT[:, t * P:(t + 1) * P]
                    nc.tensor.matmul(ab_ps[:, t * C:(t + 1) * C], tok, aw[:], start=True, stop=False)
                    last = nc.tensor.matmul(ab_ps[:, t * C:(t + 1) * C], ones_row[:], abr[:], start=False, stop=True)
                last.then_inc(ab_ready, 1)

                def up(e):
                    for k in range(4):
                        m = e * 4 + k
                        if m >= 2:
                            pe.wait_ge(h_ready, 1 + q * 32 + m - 1)
                        else:
                            pe.wait_ge(h_ready, 1 + q * 32)
                        nc.tensor.matmul(hps[m % 2][:], w1s[:, e, k * P:(k + 1) * P], xnT[:], start=True, stop=True)\
                            .then_inc(h_ps, 1)

                def down(e):
                    pe.wait_ge(h_ready, 1 + q * 32 + 4 * e + 4)
                    pe.wait_ge(e_used, 1 + q * E + e - 1) if e >= 1 else pe.wait_ge(e_used, 1 + q * E)
                    for t in range(TC):
                        for k in range(4):
                            last = nc.tensor.matmul(eo[e % 2][:, t * C:(t + 1) * C], hT[e % 2][:, k, t * P:(t + 1) * P],
                                                    w2s[:, e, k, :], start=(k == 0), stop=(k == 3))
                    last.then_inc(e_ready, 1)

                up(0)
                pe.wait_ge(bias_ready, 1 + 2 * q + 2)
                for t in range(TC):
                    last = nc.tensor.matmul(wt_ps[0:E, t * P:(t + 1) * P], wd[:, t, :], ident[:], start=True, stop=True)
                last.then_inc(tp_w, 1)
                pe.wait_ge(wT_ready, 1 + q + 1)
                for t in range(TC):
                    last = nc.tensor.matmul(tpa[:, t * C:(t + 1) * C], wT[:, t * P:(t + 1) * P], b2s[:],
                                            start=True, stop=True)
                last.then_inc(tp_w, 1)
                for e in range(1, E):
                    up(e)
                    down(e - 1)
                down(E - 1)
                pe.wait_ge(moe_ready, 1 + q + 1)
                for t in range(TC):
                    last = nc.tensor.transpose(tpa[:, t * P:(t + 1) * P], moe[:, t, :], ident[:])
                last.then_inc(tp_m, 1)
                pe.wait_ge(moeT_ready, 1 + q + 1)
                for t in range(TC):
                    last = nc.tensor.matmul(ab_ps[:, t * C:(t + 1) * C], moeT[:, t * P:(t + 1) * P], rot[:],
                                            start=True, stop=True)
                last.then_inc(rot_ready, 1)
                pe.wait_ge(x2_ready, 1 + q + 1)
                for t in range(TC):
                    last = nc.tensor.transpose(tpa[:, t * P:(t + 1) * P], y[:, t, :], ident[:])
                last.then_inc(tp_y, 1)
                pe.wait_ge(x2T_done, 1 + 2 * q + 2)

        @block.scalar
        def _(act):
            act.wait_ge(wl, 1 + 176)
            with act.Fori(0, TOK // CH) as q:
                def root(n):
                    act.wait_ge(sqrt_go, 1 + 3 * q + n + 1)
                    nc.scalar.activation(std[:], mv[:, :, 1], ACT.Sqrt, bias=eps_t[:], scale=1.0 / C).then_inc(sqrt_done, 1)
                root(0)
                root(1)
                act.wait_ge(exp_go, 1 + q + 1)
                nc.scalar.activation(dd[:, :, 0:1], dd[:, :, 0:1], ACT.Exp).then_inc(exp_done, 1)
                act.wait_ge(ab_ready, 1 + q + 1)
                nc.scalar.activation(flat2(abel[:]), ab_ps[:], ACT.Gelu).then_inc(ab_act, 1)
                for m in range(32):
                    e, k = m // 4, m % 4
                    act.wait_ge(h_ps, 1 + q * 32 + m + 1)
                    if k == 0:
                        act.wait_ge(e_ready, 1 + q * E + e - 1) if e >= 1 else act.wait_ge(e_ready, 1 + q * E)
                    nc.scalar.activation(hT[e % 2][:, k, :], hps[m % 2][:], ACT.Gelu, bias=b1s[:, m:m + 1])\
                        .then_inc(h_ready, 1)
                act.wait_ge(z_go, 1 + q + 1)
                nc.scalar.activation(z[:, :, 0:1], z[:, :, 0:1], ACT.Exp, scale=-1.0).then_inc(z_done, 1)
                root(2)
                act.wait_ge(tp_y, 1 + q + 1)
                nc.scalar.copy(xT_all[:, bass.ds(q * CH, CH)], tpa[:]).then_inc(x2T_done, 1)

        @block.vector
        def _(v):
            PER = 0
            v.wait_ge(wl_iota, 1 + 1)
            v.wait_ge(wl, 1 + 176)
            with v.Fori(0, TOK // CH) as q:
                link = loop_link(dve, v, q, FFN0_LINKS)
                v.wait_ge(tp_s, 1 + q + 1)
                s3 = tpa[:].rearrange("p (t c) -> p t c", t=TC)
                norm_link(link, v, s3, x1, mv, stats, std, sqrt_go, sqrt_done, 3 * q, TC)
                norm_link(link, v, x1, xh, mv, stats, std, sqrt_go, sqrt_done, 3 * q + 1, TC, bias_ready)
                v.wait_ge(tp_x, 1 + q + 1)
                nc.vector.tensor_scalar(xnT[:], tpa[:], gb[:, 0:1], gb[:, 1:2], ALU.mult, ALU.add)\
                    .then_inc(xn_ready, 1)
                v.wait_ge(lg_ready, 1 + q + 1)
                route_link(link, v, lps[:, 0:TC * E].rearrange("p (t e) -> p t e", t=TC), lg, m8, i8, i8f, dd, wd,
                           it8, exp_go, exp_done, q)
                nc.vector.memset(junk[:, 0:1], 0.0).then_inc(bias_ready, 1)
                v.wait_ge(tp_w, 1 + 2 * q + 1)
                nc.vector.tensor_copy(wT[:], wt_ps[0:E, :]).then_inc(wT_ready, 1)
                v.wait_ge(tp_w, 1 + 2 * q + 2)
                link(nc.vector.tensor_copy(flat2(moe[:]), tpa[:]))
                for e in range(E):
                    v.wait_ge(e_ready, 1 + q * E + e + 1)
                    for t in range(TC):
                        ins = nc.vector.scalar_tensor_tensor(moe[:, t, :], eo[e % 2][:, t * C:(t + 1) * C],
                                                             wd[:, t, e:e + 1], moe[:, t, :], ALU.mult, ALU.add)
                        if t < TC - 1:
                            link(ins)
                        else:
                            ins.then_inc(e_used, 1)
                            v.wait_ge(e_used, 1 + q * E + e + 1)
                nc.vector.memset(junk[:, 0:1], 0.0).then_inc(moe_ready, 1)
                v.wait_ge(tp_m, 1 + q + 1)
                nc.vector.tensor_copy(moeT[:], tpa[:]).then_inc(moeT_ready, 1)
                v.wait_ge(rot_ready, 1 + q + 1)
                link(nc.vector.tensor_copy(flat2(nona[:]), ab_ps[:]))
                v.wait_ge(ab_act, 1 + q + 1)
                for t in range(TC):
                    for a, src in ((0, abel), (1, nona)):
                        link(nc.vector.scalar_tensor_tensor(junk[:], src[:, t, :], 1.0, mixs[:, a, :], ALU.mult,
                                                            ALU.mult, accum_out=z[:, t, a:a + 1]))
                link(nc.vector.tensor_tensor(z[:, :, 0:1], z[:, :, 0:1], z[:, :, 1:2], ALU.add))
                nc.vector.tensor_scalar(z[:, :, 0:1], z[:, :, 0:1], mb[:], None, ALU.add).then_inc(z_go, 1)
                v.wait_ge(z_done, 1 + q + 1)
                link(nc.vector.tensor_scalar(z[:, :, 1:2], z[:, :, 0:1], 1.0, None, ALU.add))
                link(nc.vector.reciprocal(z[:, :, 1:2], z[:, :, 1:2]))
                link(nc.vector.tensor_tensor(flat2(nona[:]), flat2(nona[:]), flat2(abel[:]), ALU.subtract))
                for t in range(TC):
                    link(nc.vector.scalar_tensor_tensor(nona[:, t, :], nona[:, t, :], z[:, t, 1:2], abel[:, t, :],
                                                        ALU.mult, ALU.add))
                link(nc.vector.scalar_tensor_tensor(flat2(xh[:]), flat2(x1[:]), 2.0, flat2(nona[:]),
                                                    ALU.mult, ALU.add))
                norm_link(link, v, xh, y, mv, stats, std, sqrt_go, sqrt_done, 3 * q + 2, TC, x2_ready)
                v.wait_ge(x2_ready, 1 + q + 1)
                nc.vector.memset(junk[:, 0:1], 0.0)
                nc.vector.tensor_copy(xs_all[:, bass.ds(q * TC, TC), :], y[:]).then_inc(x2T_done, 1)
                assert link.state[0] == FFN0_LINKS, link.state[0]

    with ExitStack() as ctx:
        sb, ps, sem = alloc(ctx)
        wqk = sb("wqk", [P, 2, 4, P])
        bqk = sb("bqk", [P, 2, 4])
        wvs = sb("wvs", [P, C])
        bvr = sb("bvr", [1, C])
        pw = sb("pw", [P, C])
        pbr = sb("pbr", [1, C])
        xb = sb("xb", [P, L])
        qk = sb("qk", [P, 2, 4, L])
        va = sb("va", [P, 2, NH, HD + 1])
        mx = sb("mx", [P, 2, NH])
        mxx = sb("mxx", [P, 2, 4, 4, 32])
        pt = [sb(f"pt{u}", [P, 2, 2, L]) for u in range(4)]
        o = sb("o", [P, 2, C])
        den = sb("den", [P, 2, NH])
        oT = sb("oT", [P, L])
        x3 = sb("x3", [P, 2, C])
        y = sb("y5", [P, 2, C])
        stats = sb("stats5", [P, 2, 6])
        mv = sb("mv5", [P, 2, 2])
        std = sb("std5", [P, 2])
        qk_ps = [ps(f"qk_ps{u}", [P, 512]) for u in range(2)]
        s_ps = [ps(f"s_ps{u}", [P, 512]) for u in range(4)]
        o_ps = ps("o_ps", [P, 512])
        v_ps = ps("v_ps", [P, 512])
        names = ("wl5 staged5 qk_ready qk_used v_ready v_used sc_ready sc_used mx_ready mt_ready qa_ready st_ready "
                 "p_ready pv_ready o_ready5 ot_ready oT_done pj_ready x3_ready xt_ready xT_done dve5 sq_go sq_done "
                 "pz").split()
        S = {k: sem(k) for k in names}
        block = ctx.enter_context(nc.Block())
        SCALE = float(HD) ** -0.5

        @block.sync
        def _(sp):
            start_at_one(sp)
            for dst, src in ((wqk[:].rearrange("p a b c -> p (a b c)"), wqkv), (bqk[:].rearrange("p a b -> p (a b)"), bqkv),
                             (wvs[:], wv), (bvr[:], bv), (pw[:], proj_w), (pbr[:], proj_b)):
                sp.dma_start(dst, src).then_inc(S["wl5"], 16)
            sp.wait_ge(S["wl5"], 1 + 96)

        @block.gpsimd
        def _(pool):
            nc.gpsimd.memset(mxx[:].rearrange("p t g s c -> p (t g s c)"), 0.0)
            nc.gpsimd.memset(va[:].rearrange("p t h d -> p (t h d)"), 1.0).then_inc(S["pz"], 1)
            with pool.Fori(0, B) as b:
                pool.wait_ge(S["v_ready"], 1 + b)
                pool.wait_ge(S["qk_ready"], 1 + 8 * b)
                nc.gpsimd.tensor_copy(xb[:], xT_all[:, bass.ds(b * L, L)]).then_inc(S["staged5"], 1)

        @block.tensor
        def _(pe):
            pe.wait_ge(S["wl5"], 1 + 96)
            with pe.Fori(0, B) as b:
                pe.wait_ge(S["staged5"], 1 + b + 1)
                pe.wait_ge(S["p_ready"], 1 + 16 * b)
                for i in range(8):
                    if i >= 2:
                        pe.wait_ge(S["qk_used"], 1 + 8 * b + i - 1)
                    else:
                        pe.wait_ge(S["qk_used"], 1 + 8 * b)
                    nc.tensor.matmul(qk_ps[i % 2][:, 0:L], wqk[:, i // 4, i % 4, :], xb[:], start=True, stop=True)\
                        .then_inc(S["qk_ready"], 1)
                pe.wait_ge(S["v_used"], 1 + b)
                for t in range(2):
                    nc.tensor.matmul(v_ps[:, t * C:(t + 1) * C], xb[:, t * P:(t + 1) * P], wvs[:], start=True, stop=False)
                    last = nc.tensor.matmul(v_ps[:, t * C:(t + 1) * C], ones_row[:], bvr[:], start=False, stop=True)
                last.then_inc(S["v_ready"], 1)
                pe.wait_ge(S["qk_used"], 1 + 8 * b + 8)
                for h in range(NH):
                    g, s = h // 4, h % 4
                    rows = slice(32 * s, 32 * s + 32)
                    if h >= 4:
                        pe.wait_ge(S["sc_used"], 1 + 16 * b + h - 3)
                    for t in range(2):
                        last = nc.tensor.matmul(s_ps[h % 4][:, t * L:(t + 1) * L], qk[rows, 0, g, t * P:(t + 1) * P],
                                                qk[rows, 1, g, :], start=True, stop=True, tile_position=(32 * s, 0))
                    last.then_inc(S["sc_ready"], 1)
                pe.wait_ge(S["mx_ready"], 1 + b + 1)
                for g in range(4):
                    for t in range(2):
                        last = nc.tensor.matmul(qk_ps[g // 2][:, (g % 2) * L + t * P:(g % 2) * L + (t + 1) * P],
                                                mxx[:, t, g, :, :].rearrange("p s c -> p (s c)"), ident[:],
                                                start=True, stop=True)
                last.then_inc(S["mt_ready"], 1)
                pe.wait_ge(S["qa_ready"], 1 + 4 * b + 4)

                def scores_t(h):
                    g, s = h // 4, h % 4
                    rows = slice(32 * s, 32 * s + 32)
                    if h >= 4:
                        pe.wait_ge(S["p_ready"], 1 + 16 * b + h - 3)
                    for t in range(2):
                        last = nc.tensor.matmul(s_ps[h % 4][:, t * L:(t + 1) * L], qk[rows, 1, g, t * P:(t + 1) * P],
                                                qk[rows, 0, g, :], start=True, stop=True, tile_position=(32 * s, 0))
                    last.then_inc(S["st_ready"], 1)

                def values(h):
                    pe.wait_ge(S["p_ready"], 1 + 16 * b + h + 1)
                    for tq in range(2):
                        for tk in range(2):
                            last = nc.tensor.matmul(
                                o_ps[:, (tq * NH + h) * (HD + 1):(tq * NH + h + 1) * (HD + 1)],
                                pt[h % 4][:, 0, tk, tq * P:(tq + 1) * P], va[:, tk, h, :],
                                start=(tk == 0), stop=(tk == 1))
                    last.then_inc(S["pv_ready"], 1)

                for h in range(2):
                    scores_t(h)
                for h in range(NH):
                    if h + 2 < NH:
                        scores_t(h + 2)
                    values(h)
                pe.wait_ge(S["o_ready5"], 1 + b + 1)
                for t in range(2):
                    last = nc.tensor.transpose(v_ps[:, t * P:(t + 1) * P], o[:, t, :], ident[:])
                last.then_inc(S["ot_ready"], 1)
                pe.wait_ge(S["oT_done"], 1 + b + 1)
                for t in range(2):
                    nc.tensor.matmul(v_ps[:, t * C:(t + 1) * C], oT[:, t * P:(t + 1) * P], pw[:], start=True, stop=False)
                    last = nc.tensor.matmul(v_ps[:, t * C:(t + 1) * C], ones_row[:], pbr[:], start=False, stop=True)
                last.then_inc(S["pj_ready"], 1)
                pe.wait_ge(S["x3_ready"], 1 + b + 1)
                for t in range(2):
                    last = nc.tensor.transpose(qk_ps[0][:, t * P:(t + 1) * P], y[:, t, :], ident[:])
                last.then_inc(S["xt_ready"], 1)
                pe.wait_ge(S["xT_done"], 1 + b + 1)

        @block.scalar
        def _(act):
            act.wait_ge(S["wl5"], 1 + 96)
            with act.Fori(0, B) as b:
                for i in range(8):
                    act.wait_ge(S["qk_ready"], 1 + 8 * b + i + 1)
                    nc.scalar.activation(qk[:, i // 4, i % 4, :], qk_ps[i % 2][:, 0:L], ACT.Identity,
                                         bias=bqk[:, i // 4, i % 4:i % 4 + 1]).then_inc(S["qk_used"], 1)
                for h in range(NH):
                    act.wait_ge(S["st_ready"], 1 + 16 * b + h + 1)
                    if h >= 4:
                        act.wait_ge(S["pv_ready"], 1 + 16 * b + h - 3)
                    nc.scalar.activation(pt[h % 4][:, 0, :, :].rearrange("p t q -> p (t q)"), s_ps[h % 4][:],
                                         ACT.Exp, scale=SCALE).then_inc(S["p_ready"], 1)
                act.wait_ge(S["sq_go"], 1 + b + 1)
                nc.scalar.activation(std[:], mv[:, :, 1], ACT.Sqrt, bias=eps_t[:], scale=1.0 / C).then_inc(S["sq_done"], 1)
                act.wait_ge(S["xt_ready"], 1 + b + 1)
                nc.scalar.copy(xT_all[:, bass.ds(b * L, L)], qk_ps[0][:, 0:L]).then_inc(S["xT_done"], 1)

        @block.vector
        def _(v):
            v.wait_ge(S["wl5"], 1 + 96)
            v.wait_ge(S["pz"], 1 + 1)
            with v.Fori(0, B) as b:
                link = loop_link(S["dve5"], v, b, ATT_LINKS)
                v.wait_ge(S["v_ready"], 1 + b + 1)
                nc.vector.tensor_copy(va[:, :, :, 0:HD], v_ps[:, 0:2 * C].rearrange("p (t h d) -> p t h d", t=2, h=NH))\
                    .then_inc(S["v_used"], 1)
                for h in range(NH):
                    v.wait_ge(S["sc_ready"], 1 + 16 * b + h + 1)
                    ins = nc.vector.tensor_reduce(mx[:, :, h:h + 1], s_ps[h % 4][:].rearrange("p (t k) -> p t k", t=2),
                                                  AX, ALU.max)
                    ins.then_inc(S["sc_used"], 1)
                v.wait_ge(S["sc_used"], 1 + 16 * b + 16)
                for t in range(2):
                    ins = nc.vector.tensor_scalar(mxx[:, t, :, :, HD:HD + 1].rearrange("p g s c -> p (g s) c"),
                                                  bc(mx[:, t, :], 2, 1), -1.0, None, ALU.mult)
                    if t == 0:
                        link(ins)
                    else:
                        ins.then_inc(S["mx_ready"], 1)
                v.wait_ge(S["mt_ready"], 1 + b + 1)
                for g in range(4):
                    nc.vector.tensor_tensor(qk[:, 0, g, :], qk[:, 0, g, :], qk_ps[g // 2][:, (g % 2) * L:(g % 2 + 1) * L],
                                            ALU.add).then_inc(S["qa_ready"], 1)
                v.wait_ge(S["pv_ready"], 1 + 16 * b + 16)
                o4 = o_ps[:, 0:2 * NH * (HD + 1)].rearrange("p (t h d) -> p t h d", t=2, h=NH)
                link(nc.vector.reciprocal(den[:], o4[:, :, :, HD:HD + 1].rearrange("p t h d -> p t (h d)")))
                ins = nc.vector.tensor_tensor(o[:].rearrange("p t (h d) -> p t h d", h=NH), o4[:, :, :, 0:HD],
                                              bc(den[:], 3, HD), ALU.mult)
                ins.then_inc(S["o_ready5"], 1)
                v.wait_ge(S["ot_ready"], 1 + b + 1)
                nc.vector.tensor_copy(oT[:], v_ps[:, 0:L]).then_inc(S["oT_done"], 1)
                v.wait_ge(S["pj_ready"], 1 + b + 1)
                link(nc.vector.tensor_tensor(x3[:], v_ps[:, 0:2 * C].rearrange("p (t c) -> p t c", t=2),
                                             xs_all[:, bass.ds(b * 2, 2), :], ALU.add))
                norm_link(link, v, x3, y, mv, stats, std, S["sq_go"], S["sq_done"], b, 2)
                nc.vector.memset(den[:, 0, 0:1], 0.0)
                nc.vector.tensor_copy(xs_all[:, bass.ds(b * 2, 2), :], y[:]).then_inc(S["x3_ready"], 1)
                assert link.state[0] == ATT_LINKS, link.state[0]

    with ExitStack() as ctx:
        sb, ps, sem = alloc(ctx)
        wgs = sb("wgs", [P, E])
        wa = sb("wa", [P, E, HID])
        wb = sb("wb", [P, E, HID])
        wc = sb("wc", [P, E, 2, C])
        it8 = sb("it86", [P, E])
        xc = sb("xc", [P, CH])
        lg = sb("lg6", [P, TC, E])
        m8 = sb("m86", [P, TC, 8])
        i8 = sb("i86", [P, TC, 8], U32)
        i8f = sb("i8f6", [P, TC, 2])
        dd = sb("dd6", [P, TC, 2])
        wd = sb("wd6", [P, TC, E])
        act_h = [sb(f"act_h{u}", [P, 2, CH]) for u in range(2)]
        hid = [sb(f"hid{u}", [P, 2, CH]) for u in range(2)]
        moe = sb("moe6", [P, TC, C])
        y = sb("y6", [P, TC, C])
        stats = sb("stats6", [P, TC, 6])
        mv = sb("mv6", [P, TC, 2])
        std = sb("std6", [P, TC])
        lps = ps("lps6", [P, 512])
        h_ps = [ps(f"h_ps{u}", [P, 512]) for u in range(2)]
        g_ps = [ps(f"g_ps{u}", [P, 512]) for u in range(2)]
        eo = [ps(f"eo6{u}", [P, 512]) for u in range(2)]
        names = ("wl6 it8_set staged6 lg_ready6 exp_go6 exp_done6 h_ready6 g_ready6 silu_done hid_done e_ready6 e_used6 "
                 "sq_go6 sq_done6 y_ready6 stored dve6 x_set").split()
        S = {k: sem(k) for k in names}
        block = ctx.enter_context(nc.Block())

        @block.sync
        def _(sp):
            start_at_one(sp)
            for dst, src in ((wgs[:], wg), (wa[:], w31.rearrange("e d f -> d e f")),
                             (wb[:], w32.rearrange("e d f -> d e f")),
                             (wc[:], w33.rearrange("e (k f) d -> f e k d", f=P))):
                sp.dma_start(dst, src).then_inc(S["wl6"], 16)
            sp.wait_ge(S["wl6"], 1 + 64)
            with sp.Fori(0, TOK // CH) as q:
                sp.wait_ge(S["y_ready6"], 1 + q + 1)
                sp.dma_start(out[bass.ds(q * CH, CH), :].rearrange("(t p) c -> p t c", p=P), y[:])\
                    .then_inc(S["stored"], 16)
            sp.wait_ge(S["stored"], 1 + 16 * (TOK // CH))

        @block.gpsimd
        def _(pool):
            nc.gpsimd.iota(it8[:], pattern=[[1, E]], base=0, channel_multiplier=0,
                           allow_small_or_imprecise_dtypes=True).then_inc(S["it8_set"], 1)
            with pool.Fori(0, TOK // CH) as q:
                pool.wait_ge(S["e_ready6"], 1 + q * E)
                nc.gpsimd.tensor_copy(xc[:], xT_all[:, bass.ds(q * CH, CH)]).then_inc(S["staged6"], 1)

        @block.tensor
        def _(pe):
            pe.wait_ge(S["wl6"], 1 + 64)
            with pe.Fori(0, TOK // CH) as q:
                pe.wait_ge(S["staged6"], 1 + q + 1)
                for t in range(TC):
                    last = nc.tensor.matmul(lps[:, t * E:(t + 1) * E], xc[:, t * P:(t + 1) * P], wgs[:],
                                            start=True, stop=True)
                last.then_inc(S["lg_ready6"], 1)

                def up(e):
                    for k in range(2):
                        pe.wait_ge(S["hid_done"], 1 + q * 16 + 2 * e + k - 1) if e + k >= 1 else \
                            pe.wait_ge(S["hid_done"], 1 + q * 16)
                        nc.tensor.matmul(h_ps[k][:], wa[:, e, k * P:(k + 1) * P], xc[:], start=True, stop=True)\
                            .then_inc(S["h_ready6"], 1)
                        nc.tensor.matmul(g_ps[k][:], wb[:, e, k * P:(k + 1) * P], xc[:], start=True, stop=True)\
                            .then_inc(S["g_ready6"], 1)

                def down(e):
                    pe.wait_ge(S["hid_done"], 1 + q * 16 + 2 * e + 2)
                    pe.wait_ge(S["e_used6"], 1 + q * E + e - 1) if e >= 1 else pe.wait_ge(S["e_used6"], 1 + q * E)
                    for t in range(TC):
                        for k in range(2):
                            last = nc.tensor.matmul(eo[e % 2][:, t * C:(t + 1) * C], hid[e % 2][:, k, t * P:(t + 1) * P],
                                                    wc[:, e, k, :], start=(k == 0), stop=(k == 1))
                    last.then_inc(S["e_ready6"], 1)

                up(0)
                for e in range(1, E):
                    up(e)
                    down(e - 1)
                down(E - 1)

        @block.scalar
        def _(act):
            with act.Fori(0, TOK // CH) as q:
                act.wait_ge(S["exp_go6"], 1 + q + 1)
                nc.scalar.activation(dd[:, :, 0:1], dd[:, :, 0:1], ACT.Exp).then_inc(S["exp_done6"], 1)
                for m in range(16):
                    e, k = m // 2, m % 2
                    act.wait_ge(S["h_ready6"], 1 + q * 16 + m + 1)
                    if m >= 4:
                        act.wait_ge(S["hid_done"], 1 + q * 16 + m - 3)
                    nc.scalar.activation(act_h[e % 2][:, k, :], h_ps[k][:], ACT.Silu).then_inc(S["silu_done"], 1)
                act.wait_ge(S["sq_go6"], 1 + q + 1)
                nc.scalar.activation(std[:], mv[:, :, 1], ACT.Sqrt, bias=eps_t[:], scale=1.0 / C).then_inc(S["sq_done6"], 1)

        @block.vector
        def _(v):
            v.wait_ge(S["it8_set"], 1 + 1)
            with v.Fori(0, TOK // CH) as q:
                link = loop_link(S["dve6"], v, q, FFN1_LINKS)
                v.wait_ge(S["lg_ready6"], 1 + q + 1)
                route_link(link, v, lps[:, 0:TC * E].rearrange("p (t e) -> p t e", t=TC), lg, m8, i8, i8f, dd, wd,
                           it8, S["exp_go6"], S["exp_done6"], q)
                nc.vector.memset(dd[:, 0, 0:1], 0.0)
                link(nc.vector.tensor_copy(moe[:], xs_all[:, bass.ds(q * TC, TC), :]))

                def gated(e):
                    for k in range(2):
                        m = 2 * e + k
                        v.wait_ge(S["silu_done"], 1 + q * 16 + m + 1)
                        v.wait_ge(S["g_ready6"], 1 + q * 16 + m + 1)
                        if e >= 1:
                            v.wait_ge(S["e_ready6"], 1 + q * E + e - 1)
                        nc.vector.tensor_tensor(hid[e % 2][:, k, :], act_h[e % 2][:, k, :], g_ps[k][:], ALU.mult)\
                            .then_inc(S["hid_done"], 1)

                def combine(e):
                    v.wait_ge(S["e_ready6"], 1 + q * E + e + 1)
                    for t in range(TC):
                        ins = nc.vector.scalar_tensor_tensor(moe[:, t, :], eo[e % 2][:, t * C:(t + 1) * C],
                                                             wd[:, t, e:e + 1], moe[:, t, :], ALU.mult, ALU.add)
                        if t < TC - 1:
                            link(ins)
                        else:
                            ins.then_inc(S["e_used6"], 1)
                            v.wait_ge(S["e_used6"], 1 + q * E + e + 1)
                gated(0)
                for e in range(1, E):
                    gated(e)
                    combine(e - 1)
                combine(E - 1)
                v.wait_ge(S["stored"], 1 + 16 * q)
                norm_link(link, v, moe, y, mv, stats, std, S["sq_go6"], S["sq_done6"], q, TC, S["y_ready6"])
                assert link.state[0] == FFN1_LINKS, link.state[0]


FFN0_LINKS, ATT_LINKS, FFN1_LINKS = 81, 11, 48


def kernel(**inputs):
    import numpy as np
    import concourse.bacc as bacc
    from concourse.bass_utils import run_bass_kernel_spmd

    a = {k: np.asarray(v) for k, v in inputs.items()}
    x = a["L0_attn_x"].reshape(TOK, C)
    f32 = np.float32
    ar = {}
    ar["x_tok"] = x
    ar["x_T"] = x.T
    ar["x_conv"] = x.reshape(2, GB, A32, R8, C).transpose(3, 0, 4, 1, 2).reshape(NT, C, P)
    ww = a["L0_attn_wave_w"].reshape(H0, 2, C).transpose(2, 1, 0).reshape(C, 2 * H0)
    ar["kw"] = np.concatenate([a["L0_attn_kernel_w"].T, ww], axis=1)
    ar["kbias"] = np.concatenate([a["L0_attn_kernel_b"],
                                  a["L0_attn_wave_b"].reshape(H0, 2).T.reshape(-1)]).reshape(1, -1)
    ar["outwT"] = a["L0_attn_out_w"].T
    cst = np.zeros((P, VW + 1), f32)
    cst[:, :VW] = np.arange(VW) - R8
    cst[:, VW] = R8 * (np.arange(P) % A32)
    ar["cst"] = cst
    edges = np.zeros((P, R8, NE_), f32)
    edges[:, :, :BINS + 1] = np.arange(BINS + 1) * R8 - L
    edges[:, :, 0], edges[:, :, BINS] = -1e6, 1e6
    pos = R8 * (np.arange(P) % A32)[:, None] + np.arange(R8)[None, :]
    edges[:, :, BINS + 1] = -pos
    edges[:, :, BINS + 2] = L - 1 - pos
    ar["edges"] = edges
    ar["ident_d"] = np.eye(P, dtype=f32)
    ar["ln_gb"] = np.stack([a["L0_ffn_ln_g"], a["L0_ffn_ln_b"]], axis=1)
    ar["abel_w"], ar["abel_b"] = a["L0_ffn_abel_w"], a["L0_ffn_abel_b"].reshape(1, C)
    ar["gate_w"], ar["gate_b"] = a["L0_ffn_gate_w_moe"], a["L0_ffn_gate_b_moe"].reshape(1, E)
    ar["w1"], ar["b1"] = a["L0_ffn_w1"], a["L0_ffn_b1"].reshape(E * 4, P).T
    ar["w2"], ar["b2"] = a["L0_ffn_w2"], a["L0_ffn_b2"]
    gens = a["L0_ffn_gens"]
    ar["gens"] = np.concatenate([gens, gens.transpose(0, 2, 1)], axis=0)
    ar["mix_w"] = np.broadcast_to(a["L0_ffn_mix_w"].reshape(1, 2 * C), (P, 2 * C))
    ar["mix_b"] = np.broadcast_to(a["L0_ffn_mix_b"].reshape(1, 1), (P, 1))
    wq = a["L1_attn_qkv_w"][:2 * C].reshape(2, 4, 4, HD, C)
    wqk = np.zeros((C, 2, 4, 4, 32), f32)
    wqk[..., :HD] = wq.transpose(4, 0, 1, 2, 3)
    ar["wqkv"] = wqk.reshape(C, 2 * 4 * P)
    bqk = np.zeros((4, 32, 2, 4), f32)
    bqk[:, :HD] = a["L1_attn_qkv_b"][:2 * C].reshape(2, 4, 4, HD).transpose(2, 3, 0, 1)
    bqk[:, HD, 1, :] = 1.0
    ar["bqkv"] = bqk.reshape(P, 8)
    ar["wv"], ar["bv"] = a["L1_attn_qkv_w"][2 * C:].T, a["L1_attn_qkv_b"][2 * C:].reshape(1, C)
    ar["proj_w"], ar["proj_b"] = a["L1_attn_proj_w"].T, a["L1_attn_proj_b"].reshape(1, C)
    ar["wg"], ar["w31"], ar["w32"], ar["w33"] = (a[f"L1_ffn_{k}"] for k in ("Wg", "W1", "W2", "W3"))

    nc = bacc.Bacc("TRN2", target_bir_lowering=False, num_devices=1)
    args, arrays = {}, {}
    for name, arr in ar.items():
        arrays[f"in_{name}"] = np.ascontiguousarray(arr)
        args[name] = nc.dram_tensor(f"in_{name}", arr.shape, F32, kind="ExternalInput").ap()
    kd = nc.dram_tensor("kd", (NT, P, H0 * BINS), F32, kind="Internal").ap()
    out = nc.dram_tensor("out_0", (TOK, C), F32, kind="ExternalOutput").ap()
    build(nc, kd=kd, out=out, **args)
    r = run_bass_kernel_spmd(nc, [arrays], core_ids=[0])
    return r.results[0]["out_0"].reshape(B, L, C)
```

```python
from contextlib import ExitStack

import concourse.bass as bass
from concourse import mybir

F32 = mybir.dt.float32
F32R = mybir.dt.float32r
U32 = mybir.dt.uint32
ALU = mybir.AluOpType
ACT = mybir.ActivationFunctionType
AX = mybir.AxisListType.X

P = 128
B, L, C = 8, 256, 128
TOK = B * L
NT = TOK // P
H0, D0, BINS, TAPS = 8, 16, 64, 32
R8 = 8
A32 = L // R8
GB = 4
NBLK = L // R8 + 1
VW = NBLK * R8
AW = VW + R8
E = 8
DF = 512
HID = 256
NH, HD = 16, 8
CH = 512
TC = CH // P
EPS = 1e-5
MAGIC = 12582912.0
DELTA = 2.0 ** -17
SQUARINGS, DEGREE = 8, 8
NE_ = BINS + 1 + 2


def V(nc, own, eng):
    sem, state = own

    def link(ins):
        state[0] += 1
        ins.then_inc(sem, 1)
        eng.wait_ge(sem, state[0])
    return link


def loop_link(sem, eng, it, per):
    state = [0]

    def link(ins):
        state[0] += 1
        ins.then_inc(sem, 1)
        eng.wait_ge(sem, it * per + state[0])
    link.state = state
    return link


def bc(ap, axis, n):
    d = [list(x) for x in ap.ap]
    d.insert(axis, [0, n])
    return bass.AP(ap.tensor, ap.offset, d)


def build(nc, x_tok, x_T, x_conv, kw, kbias, outwT, cst, edges, ident_d, ln_gb, abel_w, abel_b, gate_w, gate_b,
          w1, b1, w2, b2, gens, mix_w, mix_b, wqkv, bqkv, wv, bv, proj_w, proj_b, wg, w31, w32, w33, kd, out):
    top = ExitStack()

    def alloc(ctx):
        def sb(name, shape, dt=F32):
            return ctx.enter_context(nc.sbuf_tensor(name, shape, dt))

        def ps(name, shape):
            return ctx.enter_context(nc.psum_tensor(name, shape, F32))

        def sem(name):
            s = ctx.enter_context(nc.semaphore(name))
            if "dve" not in name:
                started.append(s)
            return s
        return sb, ps, sem

    started = []

    def start_at_one(eng):
        for s in started:
            eng.sem_inc(s, 1)
        started.clear()

    with top:
        sb, _, _ = alloc(top)
        ident = sb("ident", [P, P])
        ones_row = sb("ones_row", [1, P])
        eps_t = sb("eps_t", [P, 1])
        sT = sb("sT", [P, TOK])
        rot = sb("rot", [P, P])

        par_ctx = ExitStack()
        psb, _, _ = alloc(par_ctx)
        wave = psb("wave", [P, NT, 2 * H0])
        par = psb("par", [P, 8, NT, H0])
        FR, INV, INV2, CE, CO, F2, O0, TMP = range(8)
        cst_s = psb("cst_s", [P, VW + 1])
        edges_s = psb("edges_s", [P, R8, NE_])
        with ExitStack() as ctx:
            sb, ps, sem = alloc(ctx)
            kw_s = sb("kw_s", [P, H0 * BINS + 2 * H0])
            kb_s = sb("kb_s", [1, H0 * BINS + 2 * H0])
            xs = [sb(f"xs{u}", [P, P]) for u in range(2)]
            kst = [sb(f"kst{u}", [P, H0 * BINS]) for u in range(2)]
            kps = [ps(f"kps{u}", [P, 512]) for u in range(2)]
            wps = [ps(f"wps{u}", [P, 512]) for u in range(2)]
            loaded, x_in = sem("loaded"), [sem(f"x_in{u}") for u in range(2)]
            mm = [sem(f"mm{u}") for u in range(2)]
            k_out = [sem(f"k_out{u}") for u in range(2)]
            w_out = [sem(f"w_out{u}") for u in range(2)]
            k_dma = [sem(f"k_dma{u}") for u in range(2)]
            wave_done, act_done, dve = sem("wave_done"), sem("act_done"), sem("dve")
            ones_set = sem("ones_set")
            block = ctx.enter_context(nc.Block())
            NK = H0 * BINS

            @block.sync
            def _(sp):
                start_at_one(sp)
                for dst, src in ((kw_s, kw), (kb_s, kbias), (ident, ident_d), (cst_s, cst), (edges_s, edges)):
                    sp.dma_start(dst[:], src).then_inc(loaded, 16)
                with sp.Fori(0, NT // 2) as r:
                    for u in range(2):
                        sp.wait_ge(mm[u], 1 + r)
                        sp.dma_start(xs[u][:], x_conv[bass.ds(r * 2 + u, 1), :, :].rearrange("o c p -> (o c) p"))\
                            .then_inc(x_in[u], 16)
                sp.wait_ge(loaded, 1 + 80)

            @block.tensor
            def _(pe):
                pe.wait_ge(loaded, 1 + 80)
                pe.wait_ge(ones_set, 1 + 1)
                with pe.Fori(0, NT // 2) as r:
                    for u in range(2):
                        pe.wait_ge(x_in[u], 1 + r * 16 + 16)
                        pe.wait_ge(k_out[u], 1 + r)
                        pe.wait_ge(w_out[u], 1 + r)
                        nc.tensor.matmul(kps[u][:, 0:NK], xs[u][:], kw_s[:, 0:NK], start=True, stop=False)
                        nc.tensor.matmul(kps[u][:, 0:NK], ones_row[:], kb_s[:, 0:NK], start=False, stop=True)
                        nc.tensor.matmul(wps[u][:, 0:16], xs[u][:], kw_s[:, NK:NK + 16], start=True, stop=False)
                        nc.tensor.matmul(wps[u][:, 0:16], ones_row[:], kb_s[:, NK:NK + 16], start=False, stop=True)\
                            .then_inc(mm[u], 1)

            @block.scalar
            def _(act):
                with act.Fori(0, NT // 2) as r:
                    for u in range(2):
                        act.wait_ge(mm[u], 1 + r + 1)
                        act.wait_ge(k_dma[u], 1 + r * 16)
                        nc.scalar.copy(kst[u][:], kps[u][:]).then_inc(k_out[u], 1)
                        act.wait_ge(k_out[u], 1 + r + 1)
                        act.dma_start(kd[bass.ds(r * 2 + u, 1), :, :].rearrange("o p n -> (o p) n"), kst[u][:])\
                            .then_inc(k_dma[u], 16)
                for u in range(2):
                    act.wait_ge(k_dma[u], 1 + 8 * 16)
                act.wait_ge(wave_done, 1 + 1)
                nc.scalar.activation(par[:, FR], wave[:, :, 0:H0], ACT.Sigmoid).then_inc(act_done, 1)
                nc.scalar.activation(par[:, TMP], wave[:, :, H0:], ACT.Tanh).then_inc(act_done, 1)

            @block.gpsimd
            def _(pool):
                nc.gpsimd.memset(eps_t[:], EPS)
                nc.gpsimd.memset(ones_row[:], 1.0).then_inc(ones_set, 1)

            @block.vector
            def _(v):
                with v.Fori(0, NT // 2) as r:
                    for u in range(2):
                        v.wait_ge(mm[u], 1 + r + 1)
                        nc.vector.tensor_copy(wave[:, bass.ds(r * 2 + u, 1), :],
                                              bc(wps[u][:, 0:16], 1, 1)).then_inc(w_out[u], 1)
                for u in range(2):
                    v.wait_ge(w_out[u], 1 + NT // 2)
                nc.vector.memset(sT[:, 0:1], 0.0).then_inc(wave_done, 1)
                v.wait_ge(act_done, 1 + 2)
                v.wait_ge(loaded, 1 + 80)
                link = V(nc, (dve, [0]), v)
                G = lambda k: par[:, k].rearrange("p n h -> p (n h)")
                link(nc.vector.tensor_scalar(G(FR), G(FR), 15.0, 1.0, ALU.mult, ALU.add))
                link(nc.vector.tensor_tensor(G(TMP), G(TMP), G(FR), ALU.mult))
                link(nc.vector.reciprocal(G(INV), G(FR)))
                link(nc.vector.tensor_scalar(G(INV2), G(INV), 0.5, None, ALU.mult))
                link(nc.vector.tensor_scalar(G(F2), G(FR), 2.0, None, ALU.mult))
                link(nc.vector.scalar_tensor_tensor(G(O0), G(FR), -(TAPS // 2 - 0.5), G(TMP), ALU.mult, ALU.add))
                link(nc.vector.tensor_scalar(G(CE), G(O0), cst_s[:, VW:VW + 1], -1.0, ALU.add, ALU.mult))
                link(nc.vector.tensor_tensor(G(CE), G(CE), G(INV2), ALU.mult))
                link(nc.vector.tensor_scalar(G(CO), G(CE), -0.5, None, ALU.add))

        with ExitStack() as ctx:
            sb, ps, sem = alloc(ctx)
            gs = sb("gs", [P, 6, P])
            Rk = sb("Rk", [P, 3, P])
            Y = sb("Y", [P, 6, P])
            r01 = sb("r01", [P, P])
            r01T = sb("r01T", [P, P])
            gp = ps("gp", [P, 2, 512])
            gp2 = ps("gp2", [P, 2, 512])
            g_in, pe_done, dve, = sem("g_in"), sem("e_pe"), sem("e_dve")
            block = ctx.enter_context(nc.Block())
            x2d = lambda t, a, b: t[:, a:b, :].rearrange("p m n -> p (m n)")

            started.clear()

            @block.sync
            def _(sp):
                for m in range(6):
                    sp.dma_start(gs[:, m, :], gens[m]).then_inc(g_in, 16)
                sp.wait_ge(g_in, 96)

            @block.vector
            def _(v):
                v.wait_ge(g_in, 96)
                link = V(nc, (dve, [0]), v)
                link(nc.vector.tensor_scalar(x2d(gs, 0, 6), x2d(gs, 0, 6), 2.0 ** -SQUARINGS, None, ALU.mult))
                link(nc.vector.tensor_copy(x2d(Rk, 0, 3), x2d(gs, 0, 3)))
                n = 0
                for k in range(DEGREE, 1, -1):
                    n += 1
                    v.wait_ge(pe_done, n)
                    link(nc.vector.scalar_tensor_tensor(x2d(Rk, 0, 3), gp[:, 0, 0:384], 1.0 / k, x2d(gs, 0, 3),
                                                        ALU.mult, ALU.add))
                n += 1
                v.wait_ge(pe_done, n)
                link(nc.vector.tensor_copy(x2d(Y, 0, 3), x2d(Rk, 0, 3)))
                link(nc.vector.tensor_copy(x2d(Y, 3, 6), gp[:, 1, 0:384]))
                for _ in range(SQUARINGS):
                    n += 1
                    v.wait_ge(pe_done, n)
                    for half in range(2):
                        link(nc.vector.scalar_tensor_tensor(x2d(Y, 3 * half, 3 * half + 3),
                                                            x2d(Y, 3 * half, 3 * half + 3), 2.0,
                                                            gp2[:, half, 0:384], ALU.mult, ALU.add))
                n += 1
                v.wait_ge(pe_done, n)
                link(nc.vector.tensor_tensor(r01[:], gp[:, 0, 0:P], Y[:, 0, :], ALU.add))
                link(nc.vector.tensor_tensor(r01[:], r01[:], Y[:, 1, :], ALU.add))
                n += 1
                v.wait_ge(pe_done, n)
                link(nc.vector.tensor_copy(r01T[:], gp[:, 1, 0:P]))
                n += 1
                v.wait_ge(pe_done, n)
                link(nc.vector.tensor_tensor(rot[:], gp2[:, 0, 0:P], r01[:], ALU.add))
                link(nc.vector.tensor_tensor(rot[:], rot[:], Y[:, 2, :], ALU.add))
                link(nc.vector.tensor_tensor(rot[:], rot[:], ident[:], ALU.add))

            @block.tensor
            def _(pe):
                d = 2
                for k in range(DEGREE, 1, -1):
                    pe.wait_ge(dve, d)
                    for m in range(3):
                        last = nc.tensor.matmul(gp[:, 0, m * P:(m + 1) * P], gs[:, 3 + m, :], Rk[:, m, :],
                                                start=True, stop=True)
                    last.then_inc(pe_done, 1)
                    d += 1
                pe.wait_ge(dve, d)
                for m in range(3):
                    last = nc.tensor.transpose(gp[:, 1, m * P:(m + 1) * P], Rk[:, m, :], ident[:])
                last.then_inc(pe_done, 1)
                d += 2
                for _ in range(SQUARINGS):
                    pe.wait_ge(dve, d)
                    for m in range(3):
                        nc.tensor.matmul(gp2[:, 0, m * P:(m + 1) * P], Y[:, 3 + m, :], Y[:, m, :],
                                         start=True, stop=True)
                    for m in range(3):
                        last = nc.tensor.matmul(gp2[:, 1, m * P:(m + 1) * P], Y[:, m, :], Y[:, 3 + m, :],
                                                start=True, stop=True)
                    last.then_inc(pe_done, 1)
                    d += 2
                pe.wait_ge(dve, d)
                nc.tensor.matmul(gp[:, 0, 0:P], Y[:, 3, :], Y[:, 1, :], start=True, stop=True).then_inc(pe_done, 1)
                d += 2
                pe.wait_ge(dve, d)
                nc.tensor.transpose(gp[:, 1, 0:P], r01[:], ident[:]).then_inc(pe_done, 1)
                d += 1
                pe.wait_ge(dve, d)
                nc.tensor.matmul(gp2[:, 0, 0:P], r01T[:], Y[:, 2, :], start=True, stop=True).then_inc(pe_done, 1)

        with ExitStack() as ctx:
            sb, ps, sem = alloc(ctx)
            xn = sb("xn", [P, NT, P])
            XM = sb("XM", [P, NT, H0, P])
            XT = sb("XT", [P, TOK])
            ow = sb("ow", [P, P])
            Ks = [sb(f"Ks{u}", [P, H0, NBLK]) for u in range(2)]
            Kr = [sb(f"Kr{u}", [P, H0, BINS]) for u in range(2)]
            tts = [sb(f"tt{u}", [P, 2, H0, VW]) for u in range(2)]
            cls = [sb(f"cl{u}", [P, 2, H0, VW]) for u in range(2)]
            Ams = [sb(f"Am{u}", [P, H0, AW]) for u in range(2)]
            AT = sb("AT", [P, 2 * H0, P])
            yS = sb("yS", [P, P])
            t67 = sb("t67", [P, H0, NE_])
            nl = sb("nl", [P, H0, A32 + 2])
            dl = sb("dl", [P, H0, A32 + 1])
            ends = sb("ends", [P, H0, 2])
            ea = sb("ea", [P, 2, H0, 2])
            eg = sb("eg", [P, H0, 2])
            sm = sb("sm", [P, 3, H0])
            map_s = sb("map_s", [P, 2, 3, H0])
            spare = sb("spare", [P, 2])
            map_set = sem("map_set")
            q1 = sb("q1", [P, 2, H0, NBLK])
            q2 = sb("q2", [P, 2, H0, NBLK])
            dW = sb("dW", [P, H0, NBLK])
            tp = [ps(f"tp{k}", [P, 512]) for k in range(4)]
            yps = ps("yps", [P, 512])
            ops = ps("ops", [P, 512])
            ld, kin = sem("ld"), [sem(f"kin{u}") for u in range(2)]
            xm_set, xm_done, const_set = sem("xm_set"), sem("xm_done"), sem("const_set")
            t_ready, c_ready, g_ready, a_ready = sem("t_ready"), sem("c_ready"), sem("g_ready"), sem("a_ready")
            tp_ready, at_ready, y_ready, ys_ready = sem("tp_ready"), sem("at_ready"), sem("y_ready"), sem("ys_ready")
            o_ready, o_used, A_ready = sem("o_ready"), sem("o_used"), sem("A_ready")
            dve = sem("g_dve")
            block = ctx.enter_context(nc.Block())
            flat = lambda ap: ap.rearrange("p a h v -> p (a h v)")

            def in_turn(eng, tile):
                tile(0, 0, 0, None)
                with eng.Fori(0, R8 - 1) as k:
                    tile(2 * k + 1, k, 1, (2 * k, k, 0))
                    tile(2 * k + 2, k + 1, 0, (2 * k + 1, k, 1))
                tile(NT - 1, R8 - 1, 1, (NT - 2, R8 - 1, 0))

            @block.sync
            def _(sp):
                start_at_one(sp)
                sp.dma_start(xn[:], x_tok.rearrange("(n p) c -> p n c", p=P)).then_inc(ld, 16)
                sp.dma_start(XT[:], x_T).then_inc(ld, 16)
                sp.dma_start(ow[:], outwT).then_inc(ld, 16)
                sp.wait_ge(ld, 1 + 48)

                def tile(n, r, g, before):
                    if before:
                        sp.wait_ge(A_ready, n)
                    row = H0 * BINS
                    base = kd[0:1, 0:1, 0:1]
                    off = n * (P * row)
                    for b in range(GB):
                        sp.dma_start(
                            Ks[g][b * A32:(b + 1) * A32, :, :],
                            bass.AP(base.tensor, off + b * A32 * row + A32 - 1,
                                    [[row - 1, A32], [BINS, H0], [1, NBLK]])).then_inc(kin[g], 16)
                    sp.dma_start(Kr[g][:].rearrange("p h k -> p (h k)"),
                                 bass.AP(base.tensor, off, [[row, P], [1, row]])).then_inc(kin[g], 16)

                in_turn(sp, tile)

            @block.gpsimd
            def _(pool):
                nc.gpsimd.memset(spare[:], 0.0)
                nc.gpsimd.memset(XM[:].rearrange("p n h c -> p (n h c)"), 0.0).then_inc(xm_set, 1)
                for u in range(2):
                    nc.gpsimd.memset(Ams[u][:].rearrange("p h v -> p (h v)"), 0.0)
                nc.gpsimd.memset(ea[:].rearrange("p a h v -> p (a h v)"), 2.0)
                nc.gpsimd.memset(eg[:, :, 0:1], 1.0)
                nc.gpsimd.memset(eg[:, :, 1:2], -1.0).then_inc(const_set, 1)
                pool.wait_ge(xm_set, 1 + 1)
                pool.wait_ge(ld, 1 + 48)
                xm0 = XM[:, 0, 0, 0:D0]
                for n in range(NT):
                    dst = bass.AP(xm0.tensor, xm0.offset + n * H0 * P,
                                  [list(xm0.ap[0]), [P + D0, H0], [1, D0]])
                    nc.gpsimd.tensor_copy(dst, xn[:, n, :].rearrange("p (h c) -> p h c", h=H0)).then_inc(xm_done, 1)

                def tile(n, r, g, before):
                    if before:
                        pool.wait_ge(A_ready, n)
                    nc.gpsimd.tensor_copy(map_s[:, g], par[:, INV2:CO + 1, bass.ds(n, 1), :].rearrange(
                        "p k a h -> p k (a h)")).then_inc(map_set, 1)
                    pool.wait_ge(map_set, 1 + n + 1)
                    nc.gpsimd.tensor_tensor(spare[:, g:g + 1], spare[:, g:g + 1], spare[:, g:g + 1], ALU.add)
                    for h in range(H0):
                        for odd in range(2):
                            last = nc.gpsimd.tensor_scalar(tts[g][:, odd, h, :], cst_s[:, 0:VW],
                                                           map_s[:, g, 0, h:h + 1], map_s[:, g, 1 + odd, h:h + 1],
                                                           ALU.mult, ALU.add)
                    last.then_inc(t_ready, 1)

                in_turn(pool, tile)

            @block.scalar
            def _(act):
                def transposed(n, r, g):
                    act.wait_ge(tp_ready, 1 + n + 1)
                    act.wait_ge(y_ready, 1 + n)
                    for k in range(4):
                        last = nc.scalar.copy(AT[:, 4 * k:4 * k + 4, :].rearrange("p a b -> p (a b)"), tp[k][:])
                    last.then_inc(at_ready, 1)

                def mixed(n, r, g):
                    act.wait_ge(y_ready, 1 + n + 1)
                    act.wait_ge(o_ready, 1 + n)
                    nc.scalar.copy(yS[:], yps[:, 0:P]).then_inc(ys_ready, 1)

                def tile(n, r, g, before):
                    act.wait_ge(t_ready, 1 + n + 1)
                    act.wait_ge(A_ready, n) if before else None
                    nc.scalar.activation(flat(cls[g][:]), flat(tts[g][:]), ACT.Relu).then_inc(c_ready, 1)
                    if before:
                        transposed(*before)
                    act.wait_ge(g_ready, 1 + n + 1)
                    for h in range(H0):
                        last = nc.scalar.activation(
                            tts[g][:, :, h, :], cls[g][:, :, h, :], ACT.Abs,
                            scale=par[:, F2, bass.ds(n, 1), h:h + 1].rearrange("p a b -> p (a b)"))
                    last.then_inc(a_ready, 1)
                    if before:
                        mixed(*before)

                act.wait_ge(xm_done, 1 + NT)
                in_turn(act, tile)
                transposed(NT - 1, R8 - 1, 1)
                mixed(NT - 1, R8 - 1, 1)

            @block.tensor
            def _(pe):
                pe.wait_ge(xm_done, 1 + NT)
                pe.wait_ge(ld, 1 + 48)
                with pe.Fori(0, R8) as r:
                    for g in range(2):
                        n = r * 2 + g
                        pe.wait_ge(A_ready, 1 + n + 1)
                        pe.wait_ge(at_ready, 1 + n)
                        for k in range(4):
                            for j in range(4):
                                h, jc = (4 * k + j) // 2, j % 2
                                last = nc.tensor.transpose(tp[k][:, j * P:(j + 1) * P],
                                                           Ams[g][:, h, R8 + jc * P:R8 + (jc + 1) * P], ident[:])
                        last.then_inc(tp_ready, 1)
                        pe.wait_ge(at_ready, 1 + n + 1)
                        pe.wait_ge(ys_ready, 1 + n)
                        for b in range(GB):
                            for q in range(2 * H0):
                                h, jc = q // 2, q % 2
                                last = nc.tensor.matmul(yps[:, b * A32:(b + 1) * A32],
                                                        XM[:, (g * GB + b) * 2 + jc, h, :],
                                                        AT[:, q, b * A32:(b + 1) * A32],
                                                        start=(q == 0), stop=(q == 2 * H0 - 1))
                        last.then_inc(y_ready, 1)
                        pe.wait_ge(ys_ready, 1 + n + 1)
                        pe.wait_ge(o_used, 1 + n)
                        nc.tensor.matmul(ops[:, 0:P], ow[:], yS[:], start=True, stop=True).then_inc(o_ready, 1)

            @block.vector
            def _(v):
                v.wait_ge(const_set, 1 + 1)
                v.wait_ge(ld, 1 + 48)
                PER = 37

                def add_residual(n, r, g):
                    v.wait_ge(o_ready, 1 + n + 1)
                    dst = sT[:, g * GB * L:(g + 1) * GB * L].rearrange("p (b a e) -> p b a e", b=GB, e=R8)
                    src = XT[:, g * GB * L:(g + 1) * GB * L].rearrange("p (b a e) -> p b a e", b=GB, e=R8)
                    nc.vector.tensor_tensor(
                        dst[:, :, :, bass.ds(r, 1)].rearrange("p b a e -> p b (a e)"),
                        src[:, :, :, bass.ds(r, 1)].rearrange("p b a e -> p b (a e)"),
                        ops[:, 0:P].rearrange("p (b a) -> p b a", b=GB), ALU.subtract).then_inc(o_used, 1)

                def tile(n, r, g, before):
                    tt_, cl, Am = tts[g], cls[g], Ams[g]
                    link = loop_link(dve, v, n, PER)
                    pr = lambda k: par[:, k, bass.ds(n, 1), :].rearrange("p a h -> p (a h)")

                    v.wait_ge(c_ready, 1 + n + 1)
                    link(nc.vector.tensor_scalar(flat(cl[:]), flat(cl[:]), float(TAPS // 2 - 1), MAGIC,
                                                 ALU.min, ALU.add))
                    nc.vector.scalar_tensor_tensor(flat(cl[:]), flat(cl[:]), MAGIC, flat(tt_[:]),
                                                   ALU.subtract, ALU.subtract).then_inc(g_ready, 1)
                    ed = bc(edges_s[:, bass.ds(r, 1), :].rearrange("p a e -> p (a e)"), 1, H0)
                    link(nc.vector.tensor_tensor(t67[:], ed, bc(pr(O0), 2, NE_), ALU.subtract))
                    link(nc.vector.tensor_tensor(t67[:], t67[:], bc(pr(INV), 2, NE_), ALU.mult))
                    t67f = t67[:].rearrange("p h e -> p (h e)")
                    link(nc.vector.tensor_scalar(t67f, t67f, 0.5 - DELTA, 0.0, ALU.add, ALU.max))
                    link(nc.vector.tensor_scalar(t67f, t67f, float(TAPS), MAGIC, ALU.min, ALU.add))
                    link(nc.vector.tensor_scalar(t67f, t67f, -MAGIC, None, ALU.add))
                    N0, NL = t67[:, :, BINS + 1], t67[:, :, BINS + 2]
                    N0b = bc(t67[:, :, BINS + 1:BINS + 2].rearrange("p h a -> p (h a)"), 2, A32 + 2)
                    NLb = bc(t67[:, :, BINS + 2:BINS + 3].rearrange("p h a -> p (h a)"), 2, A32 + 2)
                    v.wait_ge(kin[g], 1 + (r + 1) * 80)
                    link(nc.vector.tensor_tensor(nl[:], t67[:, :, 0:A32 + 2], N0b, ALU.min))
                    link(nc.vector.tensor_tensor(dl[:], nl[:, :, 1:], nl[:, :, 0:A32 + 1], ALU.subtract))
                    link(nc.vector.tensor_tensor(dl[:], dl[:], Kr[g][:, :, 0:A32 + 1], ALU.mult))
                    link(nc.vector.tensor_reduce(ends[:, :, 0:1], dl[:], AX, ALU.add))
                    link(nc.vector.tensor_tensor(nl[:], t67[:, :, A32 - 1:BINS + 1], NLb, ALU.max))
                    link(nc.vector.tensor_tensor(dl[:], nl[:, :, 1:], nl[:, :, 0:A32 + 1], ALU.subtract))
                    link(nc.vector.tensor_tensor(dl[:], dl[:], Kr[g][:, :, A32 - 1:BINS], ALU.mult))
                    link(nc.vector.tensor_reduce(ends[:, :, 1:2], dl[:], AX, ALU.add))
                    wide = lambda ap: bass.AP(ap.tensor, ap.offset, [list(ap.ap[0]), [0, H0]])
                    e_first = edges_s[:, bass.ds(r, 1), BINS + 1:BINS + 2].rearrange("p a e -> p (a e)")
                    e_last = edges_s[:, bass.ds(r, 1), BINS + 2:BINS + 3].rearrange("p a e -> p (a e)")
                    for side, cnt, add, edge, cmp, lim in ((0, N0, 0.0, e_first, ALU.is_ge, TAPS - 0.5),
                                                           (1, NL, -1.0, e_last, ALU.is_le, 0.5)):
                        link(nc.vector.scalar_tensor_tensor(sm[:, 0, :], cnt, add, pr(FR), ALU.add, ALU.mult))
                        link(nc.vector.tensor_tensor(sm[:, 1, :], sm[:, 0, :], wide(edge), ALU.subtract))
                        link(nc.vector.tensor_tensor(sm[:, 1, :], sm[:, 1, :], pr(O0), ALU.add))
                        link(nc.vector.scalar_tensor_tensor(sm[:, 1, :], sm[:, 1, :], -1.0, sm[:, 1, :],
                                                            ALU.mult, ALU.max))
                        link(nc.vector.tensor_scalar(sm[:, 0, :], cnt, lim, 4.0, cmp, ALU.mult))
                        link(nc.vector.tensor_tensor(ea[:, 0, :, side], sm[:, 1, :], sm[:, 0, :], ALU.add))

                    link(nc.vector.tensor_tensor(dW[:, :, 1:], Ks[g][:, :, 0:NBLK - 1], Ks[g][:, :, 1:],
                                                 ALU.subtract))
                    v.wait_ge(a_ready, 1 + n + 1)
                    ta = tt_[:, :, :, bass.ds(R8 - r, 1)]
                    tg = cl[:, 0, :, bass.ds(R8 - r, 1)]
                    d4 = [list(x) for x in ta.ap]
                    d3 = [list(x) for x in tg.ap]
                    nc.vector.memset(sm[:, 2, 0:1], 0.0)
                    link(nc.vector.tensor_copy(bass.AP(ta.tensor, ta.offset, d4[:-1] + [[L - 1, 2]]), ea[:]))
                    nc.vector.memset(sm[:, 2, 0:1], 0.0)
                    link(nc.vector.tensor_copy(bass.AP(tg.tensor, tg.offset, d3[:-1] + [[L - 1, 2]]), eg[:]))
                    blk = lambda t: t[:].rearrange("p a h (c q) -> p (a h c) q", q=R8)[:, :, 0:1]\
                        .rearrange("p c q -> p (c q)")
                    q1f, q2f = (t[:].rearrange("p a h c -> p (a h c)") for t in (q1, q2))
                    link(nc.vector.tensor_scalar(q1f, blk(tt_), 1.0, -1.0, ALU.min, ALU.add))
                    link(nc.vector.scalar_tensor_tensor(q2f, blk(cl), 0.0, q1f, ALU.is_lt, ALU.mult))
                    link(nc.vector.tensor_tensor(q1[:, 0], q2[:, 0], q2[:, 1], ALU.add))
                    link(nc.vector.tensor_tensor(q1[:, 1, :, 1:], q1[:, 0, :, 1:], dW[:, :, 1:], ALU.mult))
                    tE = tt_[:, 0].rearrange("p h v -> p (h v)")
                    tO = tt_[:, 1].rearrange("p h v -> p (h v)")
                    link(nc.vector.tensor_scalar(tO, tO, 1.0, -2.0, ALU.min, ALU.add))
                    link(nc.vector.scalar_tensor_tensor(tE, tE, 1.0, tO, ALU.min, ALU.add))
                    if before:
                        v.wait_ge(tp_ready, n)
                    link(nc.vector.tensor_tensor(
                        Am[:, :, bass.ds(r, VW)].rearrange("p h (c q) -> p h c q", q=R8),
                        tt_[:, 0].rearrange("p h (c q) -> p h c q", q=R8),
                        bc(Ks[g][:], 3, R8), ALU.mult))
                    a8 = Am[:, :, bass.ds(r + R8, 1)]
                    d3 = [list(x) for x in a8.ap]
                    a8 = bass.AP(a8.tensor, a8.offset, d3[:-1] + [[R8, NBLK - 1]])
                    link(nc.vector.tensor_tensor(a8, a8, q1[:, 1, :, 1:], ALU.add))
                    ab = Am[:, :, R8:R8 + 1]
                    ab = bass.AP(ab.tensor, ab.offset, [list(x) for x in ab.ap][:-1] + [[L - 1, 2]])
                    nc.vector.tensor_tensor(ab, ab, ends[:], ALU.subtract).then_inc(A_ready, 1)
                    if before:
                        add_residual(*before)
                    assert link.state[0] == PER, link.state[0]

                in_turn(v, tile)
                add_residual(NT - 1, R8 - 1, 1)

        par_ctx.close()
        sb, _, _ = alloc(top)
        xs_all = sb("xs_all", [P, NT, P])
        xT_all = sb("xT_all", [P, TOK])
        return finish(nc, alloc, start_at_one, ident, ones_row, eps_t, sT, rot, xs_all, xT_all, ln_gb, abel_w, abel_b, gate_w, gate_b,
                      w1, b1, w2, b2, mix_w, mix_b, wqkv, bqkv, wv, bv, proj_w, proj_b, wg, w31, w32, w33, out)


def finish(nc, alloc, start_at_one, ident, ones_row, eps_t, sT, rot, xs_all, xT_all, ln_gb, abel_w, abel_b, gate_w, gate_b,
           w1, b1, w2, b2, mix_w, mix_b, wqkv, bqkv, wv, bv, proj_w, proj_b, wg, w31, w32, w33, out):
    def norm_link(link, v, src, dst, mv, stats, std, sqrt_go, sqrt_done, n, count, done=None):
        for t in range(count):
            ins = nc.vector.bn_stats(stats[:, t, :], src[:, t, :])
        link(ins)
        one = lambda k: stats[:, 0:count, k:k + 1]
        link(nc.vector.tensor_tensor(mv[:, 0:count, 0:1], one(1), one(4), ALU.add))
        link(nc.vector.tensor_tensor(one(0), one(1), one(4), ALU.subtract))
        link(nc.vector.tensor_tensor(one(2), one(2), one(5), ALU.add))
        link(nc.vector.scalar_tensor_tensor(one(0), one(0), C / 4.0, one(0), ALU.mult, ALU.mult))
        link(nc.vector.tensor_scalar(mv[:, 0:count, 0:1], mv[:, 0:count, 0:1], 0.5, None, ALU.mult))
        nc.vector.tensor_tensor(mv[:, 0:count, 1:2], one(2), one(0), ALU.add).then_inc(sqrt_go, 1)
        v.wait_ge(sqrt_done, 1 + n + 1)
        link(nc.vector.reciprocal(std[:, 0:count], std[:, 0:count]))
        for t in range(count):
            ins = nc.vector.tensor_scalar(dst[:, t, :], src[:, t, :], mv[:, t, 0:1], std[:, t:t + 1],
                                          ALU.subtract, ALU.mult)
        link(ins) if done is None else ins.then_inc(done, 1)

    def route_link(link, v, lg_ps, lg, m8, i8, i8f, dd, wd, it8, exp_go, exp_done, n):
        link(nc.vector.tensor_copy(lg[:], lg_ps))
        nc.vector.memset(dd[:, 0, 0:1], 0.0)
        for t in range(TC):
            ins = nc.vector.max(m8[:, t, :], lg[:, t, :])
        link(ins)
        nc.vector.memset(dd[:, 0, 0:1], 0.0)
        for t in range(TC):
            ins = nc.vector.max_index(i8[:, t, :], m8[:, t, :], lg[:, t, :])
        link(ins)
        link(nc.vector.tensor_copy(i8f[:], i8[:, :, 0:2]))
        nc.vector.tensor_tensor(dd[:, :, 0:1], m8[:, :, 1:2], m8[:, :, 0:1], ALU.subtract).then_inc(exp_go, 1)
        v.wait_ge(exp_done, 1 + n + 1)
        link(nc.vector.tensor_scalar(dd[:, :, 1:2], dd[:, :, 0:1], 1.0, None, ALU.add))
        link(nc.vector.reciprocal(dd[:, :, 1:2], dd[:, :, 1:2]))
        link(nc.vector.tensor_tensor(dd[:, :, 0:1], dd[:, :, 0:1], dd[:, :, 1:2], ALU.mult))
        for t in range(TC):
            link(nc.vector.tensor_scalar(wd[:, t, :], it8[:], i8f[:, t, 0:1], dd[:, t, 1:2],
                                         ALU.is_equal, ALU.mult))
            link(nc.vector.tensor_scalar(lg[:, t, :], it8[:], i8f[:, t, 1:2], dd[:, t, 0:1],
                                         ALU.is_equal, ALU.mult))
        link(nc.vector.tensor_tensor(wd[:], wd[:], lg[:], ALU.add))

    flat2 = lambda ap: ap.rearrange("p a b -> p (a b)")

    with ExitStack() as ctx:
        sb, ps, sem = alloc(ctx)
        w1s = sb("w1s", [P, E, DF])
        w2s = sb("w2s", [P, E, 4, C])
        b1s = sb("b1s", [P, E * 4])
        b2s = sb("b2s", [E, C])
        aw = sb("aw", [P, C])
        abr = sb("abr", [1, C])
        gw = sb("gw", [P, E])
        gbr = sb("gbr", [1, E])
        gb = sb("gb", [P, 2])
        mixs = sb("mixs", [P, 2, C])
        mb = sb("mb", [P, 1])
        it8 = sb("it8", [P, E])
        sS = sb("sS", [P, CH])
        x1 = sb("x1", [P, TC, C])
        xh = sb("xh", [P, TC, C])
        xnT = sb("xnT", [P, CH])
        stats = sb("stats", [P, TC, 6])
        mv = sb("mv", [P, TC, 2])
        std = sb("std", [P, TC])
        lg = sb("lg", [P, TC, E])
        m8 = sb("m8", [P, TC, 8])
        i8 = sb("i8", [P, TC, 8], U32)
        i8f = sb("i8f", [P, TC, 2])
        dd = sb("dd", [P, TC, 2])
        wd = sb("wd", [P, TC, E])
        wT = sb("wT", [E, CH])
        abel = sb("abel", [P, TC, C])
        hT = [sb(f"hT{u}", [P, 4, CH]) for u in range(2)]
        moe = sb("moe", [P, TC, C])
        moeT = sb("moeT", [P, CH])
        nona = sb("nona", [P, TC, C])
        junk = sb("junk", [P, C])
        z = sb("z", [P, TC, 2])
        y = sb("y", [P, TC, C])
        tpa, lps, eo = ps("tpa", [P, 512]), ps("lps", [P, 512]), [ps(f"eo{u}", [P, 512]) for u in range(2)]
        hps = [ps(f"hps{u}", [P, 512]) for u in range(2)]
        ab_ps = ps("ab_ps", [P, 512])
        wt_ps = ps("wt_ps", [P, 512])
        wl_iota = sem("wl_iota")
        wl, staged, dve = sem("wl"), sem("staged"), sem("f_dve")
        tp_s, tp_x, tp_w, tp_m, tp_y = (sem(f"tp_{k}") for k in "sxwmy")
        sqrt_go, sqrt_done, exp_go, exp_done = sem("sqrt_go"), sem("sqrt_done"), sem("exp_go"), sem("exp_done")
        xn_ready, lg_ready, wT_ready, ab_ready, ab_act = (sem(k) for k in ("xn_ready", "lg_ready", "wT_ready",
                                                                            "ab_ready", "ab_act"))
        bias_ready, h_ps, h_ready, e_ready, e_used = (sem(k) for k in ("bias_ready", "h_ps", "h_ready", "e_ready", "e_used"))
        moe_ready, moeT_ready, rot_ready, z_go, z_done = (sem(k) for k in ("moe_ready", "moeT_ready", "rot_ready",
                                                                           "z_go", "z_done"))
        x2_ready, x2T_done = sem("x2_ready"), sem("x2T_done")
        block = ctx.enter_context(nc.Block())

        @block.sync
        def _(sp):
            start_at_one(sp)
            for dst, src in ((w1s[:], w1.rearrange("e d f -> d e f")),
                             (w2s[:], w2.rearrange("e (k f) d -> f e k d", f=P)),
                             (b1s[:], b1), (b2s[:], b2), (aw[:], abel_w), (abr[:], abel_b), (gw[:], gate_w),
                             (gbr[:], gate_b), (gb[:], ln_gb), (mixs[:].rearrange("p a c -> p (a c)"), mix_w),
                             (mb[:], mix_b)):
                sp.dma_start(dst, src).then_inc(wl, 16)
            sp.wait_ge(wl, 1 + 176)

        @block.gpsimd
        def _(pool):
            nc.gpsimd.iota(it8[:], pattern=[[1, E]], base=0, channel_multiplier=0,
                           allow_small_or_imprecise_dtypes=True).then_inc(wl_iota, 1)
            with pool.Fori(0, TOK // CH) as q:
                pool.wait_ge(tp_s, 1 + q)
                nc.gpsimd.tensor_copy(sS[:], sT[:, bass.ds(q * CH, CH)]).then_inc(staged, 1)

        @block.tensor
        def _(pe):
            pe.wait_ge(wl, 1 + 176)
            with pe.Fori(0, TOK // CH) as q:
                pe.wait_ge(staged, 1 + q + 1)
                for t in range(TC):
                    last = nc.tensor.transpose(tpa[:, t * P:(t + 1) * P], sS[:, t * P:(t + 1) * P], ident[:])
                last.then_inc(tp_s, 1)
                pe.wait_ge(sqrt_go, 1 + 3 * q + 2)
                pe.wait_ge(bias_ready, 1 + 2 * q + 1)
                for t in range(TC):
                    last = nc.tensor.transpose(tpa[:, t * P:(t + 1) * P], xh[:, t, :], ident[:])
                last.then_inc(tp_x, 1)
                pe.wait_ge(xn_ready, 1 + q + 1)
                for t in range(TC):
                    tok = xnT[:, t * P:(t + 1) * P]
                    nc.tensor.matmul(lps[:, t * E:(t + 1) * E], tok, gw[:], start=True, stop=False)
                    last = nc.tensor.matmul(lps[:, t * E:(t + 1) * E], ones_row[:], gbr[:], start=False, stop=True)
                last.then_inc(lg_ready, 1)
                for t in range(TC):
                    tok = xnT[:, t * P:(t + 1) * P]
                    nc.tensor.matmul(ab_ps[:, t * C:(t + 1) * C], tok, aw[:], start=True, stop=False)
                    last = nc.tensor.matmul(ab_ps[:, t * C:(t + 1) * C], ones_row[:], abr[:], start=False, stop=True)
                last.then_inc(ab_ready, 1)

                def up(e):
                    for k in range(4):
                        m = e * 4 + k
                        if m >= 2:
                            pe.wait_ge(h_ready, 1 + q * 32 + m - 1)
                        else:
                            pe.wait_ge(h_ready, 1 + q * 32)
                        nc.tensor.matmul(hps[m % 2][:], w1s[:, e, k * P:(k + 1) * P], xnT[:], start=True, stop=True)\
                            .then_inc(h_ps, 1)

                def down(e):
                    pe.wait_ge(h_ready, 1 + q * 32 + 4 * e + 4)
                    pe.wait_ge(e_used, 1 + q * E + e - 1) if e >= 1 else pe.wait_ge(e_used, 1 + q * E)
                    for t in range(TC):
                        for k in range(4):
                            last = nc.tensor.matmul(eo[e % 2][:, t * C:(t + 1) * C], hT[e % 2][:, k, t * P:(t + 1) * P],
                                                    w2s[:, e, k, :], start=(k == 0), stop=(k == 3))
                    last.then_inc(e_ready, 1)

                up(0)
                pe.wait_ge(bias_ready, 1 + 2 * q + 2)
                for t in range(TC):
                    last = nc.tensor.matmul(wt_ps[0:E, t * P:(t + 1) * P], wd[:, t, :], ident[:], start=True, stop=True)
                last.then_inc(tp_w, 1)
                pe.wait_ge(wT_ready, 1 + q + 1)
                for t in range(TC):
                    last = nc.tensor.matmul(tpa[:, t * C:(t + 1) * C], wT[:, t * P:(t + 1) * P], b2s[:],
                                            start=True, stop=True)
                last.then_inc(tp_w, 1)
                for e in range(1, E):
                    up(e)
                    down(e - 1)
                down(E - 1)
                pe.wait_ge(moe_ready, 1 + q + 1)
                for t in range(TC):
                    last = nc.tensor.transpose(tpa[:, t * P:(t + 1) * P], moe[:, t, :], ident[:])
                last.then_inc(tp_m, 1)
                pe.wait_ge(moeT_ready, 1 + q + 1)
                for t in range(TC):
                    last = nc.tensor.matmul(ab_ps[:, t * C:(t + 1) * C], moeT[:, t * P:(t + 1) * P], rot[:],
                                            start=True, stop=True)
                last.then_inc(rot_ready, 1)
                pe.wait_ge(x2_ready, 1 + q + 1)
                for t in range(TC):
                    last = nc.tensor.transpose(tpa[:, t * P:(t + 1) * P], y[:, t, :], ident[:])
                last.then_inc(tp_y, 1)
                pe.wait_ge(x2T_done, 1 + 2 * q + 2)

        @block.scalar
        def _(act):
            act.wait_ge(wl, 1 + 176)
            with act.Fori(0, TOK // CH) as q:
                def root(n):
                    act.wait_ge(sqrt_go, 1 + 3 * q + n + 1)
                    nc.scalar.activation(std[:], mv[:, :, 1], ACT.Sqrt, bias=eps_t[:], scale=1.0 / C).then_inc(sqrt_done, 1)
                root(0)
                root(1)
                act.wait_ge(exp_go, 1 + q + 1)
                nc.scalar.activation(dd[:, :, 0:1], dd[:, :, 0:1], ACT.Exp).then_inc(exp_done, 1)
                act.wait_ge(ab_ready, 1 + q + 1)
                nc.scalar.activation(flat2(abel[:]), ab_ps[:], ACT.Gelu).then_inc(ab_act, 1)
                for m in range(32):
                    e, k = m // 4, m % 4
                    act.wait_ge(h_ps, 1 + q * 32 + m + 1)
                    if k == 0:
                        act.wait_ge(e_ready, 1 + q * E + e - 1) if e >= 1 else act.wait_ge(e_ready, 1 + q * E)
                    nc.scalar.activation(hT[e % 2][:, k, :], hps[m % 2][:], ACT.Gelu, bias=b1s[:, m:m + 1])\
                        .then_inc(h_ready, 1)
                act.wait_ge(z_go, 1 + q + 1)
                nc.scalar.activation(z[:, :, 0:1], z[:, :, 0:1], ACT.Exp, scale=-1.0).then_inc(z_done, 1)
                root(2)
                act.wait_ge(tp_y, 1 + q + 1)
                nc.scalar.copy(xT_all[:, bass.ds(q * CH, CH)], tpa[:]).then_inc(x2T_done, 1)

        @block.vector
        def _(v):
            PER = 0
            v.wait_ge(wl_iota, 1 + 1)
            v.wait_ge(wl, 1 + 176)
            with v.Fori(0, TOK // CH) as q:
                link = loop_link(dve, v, q, FFN0_LINKS)
                v.wait_ge(tp_s, 1 + q + 1)
                s3 = tpa[:].rearrange("p (t c) -> p t c", t=TC)
                norm_link(link, v, s3, x1, mv, stats, std, sqrt_go, sqrt_done, 3 * q, TC)
                norm_link(link, v, x1, xh, mv, stats, std, sqrt_go, sqrt_done, 3 * q + 1, TC, bias_ready)
                v.wait_ge(tp_x, 1 + q + 1)
                nc.vector.tensor_scalar(xnT[:], tpa[:], gb[:, 0:1], gb[:, 1:2], ALU.mult, ALU.add)\
                    .then_inc(xn_ready, 1)
                v.wait_ge(lg_ready, 1 + q + 1)
                route_link(link, v, lps[:, 0:TC * E].rearrange("p (t e) -> p t e", t=TC), lg, m8, i8, i8f, dd, wd,
                           it8, exp_go, exp_done, q)
                nc.vector.memset(junk[:, 0:1], 0.0).then_inc(bias_ready, 1)
                v.wait_ge(tp_w, 1 + 2 * q + 1)
                nc.vector.tensor_copy(wT[:], wt_ps[0:E, :]).then_inc(wT_ready, 1)
                v.wait_ge(tp_w, 1 + 2 * q + 2)
                link(nc.vector.tensor_copy(flat2(moe[:]), tpa[:]))
                for e in range(E):
                    v.wait_ge(e_ready, 1 + q * E + e + 1)
                    for t in range(TC):
                        ins = nc.vector.scalar_tensor_tensor(moe[:, t, :], eo[e % 2][:, t * C:(t + 1) * C],
                                                             wd[:, t, e:e + 1], moe[:, t, :], ALU.mult, ALU.add)
                        if t < TC - 1:
                            link(ins)
                        else:
                            ins.then_inc(e_used, 1)
                            v.wait_ge(e_used, 1 + q * E + e + 1)
                nc.vector.memset(junk[:, 0:1], 0.0).then_inc(moe_ready, 1)
                v.wait_ge(tp_m, 1 + q + 1)
                nc.vector.tensor_copy(moeT[:], tpa[:]).then_inc(moeT_ready, 1)
                v.wait_ge(rot_ready, 1 + q + 1)
                link(nc.vector.tensor_copy(flat2(nona[:]), ab_ps[:]))
                v.wait_ge(ab_act, 1 + q + 1)
                for t in range(TC):
                    for a, src in ((0, abel), (1, nona)):
                        link(nc.vector.scalar_tensor_tensor(junk[:], src[:, t, :], 1.0, mixs[:, a, :], ALU.mult,
                                                            ALU.mult, accum_out=z[:, t, a:a + 1]))
                link(nc.vector.tensor_tensor(z[:, :, 0:1], z[:, :, 0:1], z[:, :, 1:2], ALU.add))
                nc.vector.tensor_scalar(z[:, :, 0:1], z[:, :, 0:1], mb[:], None, ALU.add).then_inc(z_go, 1)
                v.wait_ge(z_done, 1 + q + 1)
                link(nc.vector.tensor_scalar(z[:, :, 1:2], z[:, :, 0:1], 1.0, None, ALU.add))
                link(nc.vector.reciprocal(z[:, :, 1:2], z[:, :, 1:2]))
                link(nc.vector.tensor_tensor(flat2(nona[:]), flat2(nona[:]), flat2(abel[:]), ALU.subtract))
                for t in range(TC):
                    link(nc.vector.scalar_tensor_tensor(nona[:, t, :], nona[:, t, :], z[:, t, 1:2], abel[:, t, :],
                                                        ALU.mult, ALU.add))
                link(nc.vector.scalar_tensor_tensor(flat2(xh[:]), flat2(x1[:]), 2.0, flat2(nona[:]),
                                                    ALU.mult, ALU.add))
                norm_link(link, v, xh, y, mv, stats, std, sqrt_go, sqrt_done, 3 * q + 2, TC, x2_ready)
                v.wait_ge(x2_ready, 1 + q + 1)
                nc.vector.memset(junk[:, 0:1], 0.0)
                nc.vector.tensor_copy(xs_all[:, bass.ds(q * TC, TC), :], y[:]).then_inc(x2T_done, 1)
                assert link.state[0] == FFN0_LINKS, link.state[0]

    with ExitStack() as ctx:
        sb, ps, sem = alloc(ctx)
        wqk = sb("wqk", [P, 2, 4, P])
        bqk = sb("bqk", [P, 2, 4])
        lo_bias = sb("lo_bias", [P, 2, 4])
        lo_row = sb("lo_row", [P, 2])
        wvs = sb("wvs", [P, C])
        bvr = sb("bvr", [1, C])
        pw = sb("pw", [P, C])
        pbr = sb("pbr", [1, C])
        xb = sb("xb", [P, L])
        hi = [sb(f"hi{u}", [P, 2, L], F32R) for u in range(2)]
        qf = [sb(f"qf{u}", [P, 4, L], F32R) for u in range(2)]
        kf = [sb(f"kf{u}", [P, 4, L], F32R) for u in range(2)]
        va = [sb(f"va{u}", [P, 2, NH, 32]) for u in range(2)]
        mx = sb("mx", [P, 2, NH])
        mxx = sb("mxx", [P, 2, 4, 4, 32])
        pt = [sb(f"pt{u}", [P, 2, L]) for u in range(4)]
        os_ = sb("os_", [P, 2, 512])
        o = sb("o", [P, 2, C])
        den = sb("den", [P, 2, NH])
        oT = sb("oT", [P, L])
        qk_ps = [ps(f"qk_ps{u}", [P, 512]) for u in range(2)]
        s_ps = [ps(f"s_ps{u}", [P, 512]) for u in range(2)]
        st_ps = [ps(f"st_ps{u}", [P, 512]) for u in range(2)]
        o_ps = [ps(f"o_ps{u}", [P, 512]) for u in range(2)]
        v_ps, tail_ps = s_ps
        weights_in, staged = sem("weights_in"), sem("staged5")
        proj_ready, hi_ready, proj_used = sem("proj_ready"), sem("hi_ready"), sem("proj_used")
        v_ready, v_used, s_ready, s_used, max_ready = (sem(k) for k in ("v_ready", "v_used", "s_ready", "s_used",
                                                                         "max_ready"))
        st_ready, p_ready, pv_ready = sem("st_ready"), sem("p_ready"), sem("pv_ready")
        o_ready, ot_ready, oT_done, pj_ready, pj_used = (sem(k) for k in ("o_ready5", "ot_ready", "oT_done",
                                                                          "pj_ready", "pj_used"))
        os_ready, ob_ready = sem("os_ready"), sem("ob_ready")
        dve, pool_set = sem("dve5"), sem("pool_set")
        block = ctx.enter_context(nc.Block())
        SCALE = float(HD) ** -0.5
        PJ = 6

        def in_turn(eng, batch):
            batch(0, 0, None)
            with eng.Fori(0, B // 2 - 1) as k:
                batch(2 * k + 1, 1, 2 * k)
                batch(2 * k + 2, 0, 2 * k + 1)
            batch(B - 1, 1, B - 2)
            batch(None, 0, B - 1)

        @block.sync
        def _(sp):
            start_at_one(sp)
            for dst, src in ((wqk[:].rearrange("p a b c -> p (a b c)"), wqkv),
                             (bqk[:].rearrange("p a b -> p (a b)"), bqkv[:, 0:8]),
                             (lo_bias[:].rearrange("p a b -> p (a b)"), bqkv[:, 8:16]), (lo_row[:], bqkv[:, 16:18]),
                             (wvs[:], wv), (bvr[:], bv), (pw[:], proj_w), (pbr[:], proj_b)):
                sp.dma_start(dst, src).then_inc(weights_in, 16)
            sp.wait_ge(weights_in, 1 + 128)

        @block.gpsimd
        def _(pool):
            nc.gpsimd.memset(mxx[:].rearrange("p t g s c -> p (t g s c)"), 0.0)
            for u in range(2):
                nc.gpsimd.memset(va[u][:].rearrange("p t h d -> p (t h d)"), 0.0).then_inc(pool_set, 1)
            pool.wait_ge(pool_set, 1 + 2)
            for u in range(2):
                nc.gpsimd.memset(va[u][:, :, :, HD:HD + 1], 1.0).then_inc(pool_set, 1)
            with pool.Fori(0, B) as b:
                pool.wait_ge(proj_ready, 1 + PJ * b)
                nc.gpsimd.tensor_copy(xb[:], xT_all[:, bass.ds(b * L, L)]).then_inc(staged, 1)

        @block.tensor
        def _(pe):
            pe.wait_ge(weights_in, 1 + 128)

            def project(b, i, which, pair, waits=True):
                pe.wait_ge(proj_used, PJ * b + i) if waits else None
                for j in range(2):
                    g = 2 * pair + j
                    last = nc.tensor.matmul(qk_ps[i % 2][:, j * L:(j + 1) * L], wqk[:, which, g, :], xb[:],
                                            start=True, stop=(i < 4))
                    if i >= 4:
                        for t in range(2):
                            last = nc.tensor.matmul(qk_ps[i % 2][:, j * L + t * P:j * L + (t + 1) * P],
                                                    mxx[:, t, g, :, :].rearrange("p s c -> p (s c)"), ident[:],
                                                    start=False, stop=(t == 1))
                last.then_inc(proj_ready, 1)

            def scores(b, u, h, out_ps, stat, mov, ready):
                rows = slice(32 * (h % 4), 32 * (h % 4) + 32)
                for t in range(2):
                    last = nc.tensor.matmul(out_ps[h % 2][:, t * L:(t + 1) * L],
                                            stat[u][rows, h // 4, t * P:(t + 1) * P], mov[u][rows, h // 4, :],
                                            start=True, stop=True, tile_position=(32 * (h % 4), 0))
                last.then_inc(ready, 1)

            def values(b, u, h):
                pe.wait_ge(p_ready, 1 + 16 * b + h + 1)
                if h == 0:
                    pe.wait_ge(os_ready, 1 + b)
                slot = slice(32 * (h % 4), 32 * (h % 4) + 32)
                g = h // 4
                for tk in range(2):
                    last = nc.tensor.matmul(o_ps[g // 2][slot, (g % 2) * L:(g % 2 + 1) * L], va[u][:, tk, h, :],
                                            pt[h % 4][:, tk, :], start=(tk == 0), stop=(tk == 1),
                                            tile_position=(0, 32 * (h % 4)))
                last.then_inc(pv_ready, 1)

            def batch(b, u, before):
                if b is not None:
                    pe.wait_ge(staged, 1 + b + 1)
                    if before is not None:
                        pe.wait_ge(o_ready, 1 + before)
                    for i, (which, pair) in enumerate(((1, 0), (1, 1), (0, 0), (0, 1))):
                        project(b, i, which, pair, before is not None or i >= 2)
                    if before is not None:
                        pe.wait_ge(s_used, 1 + 16 * b)
                    for t in range(2):
                        nc.tensor.matmul(v_ps[:, t * C:(t + 1) * C], xb[:, t * P:(t + 1) * P], wvs[:],
                                         start=True, stop=False)
                        last = nc.tensor.matmul(v_ps[:, t * C:(t + 1) * C], ones_row[:], bvr[:],
                                                start=False, stop=True)
                    last.then_inc(v_ready, 1)
                if before is not None:
                    pe.wait_ge(proj_used, 1 + PJ * before + PJ)
                for h in range(NH + 2):
                    if before is not None and h < NH:
                        if h >= 2:
                            pe.wait_ge(p_ready, 1 + 16 * before + h - 1)
                        scores(before, 1 - u, h, st_ps, kf, qf, st_ready)
                    if b is not None and h < NH:
                        if h == 0:
                            pe.wait_ge(proj_used, 1 + PJ * b + 4)
                            pe.wait_ge(v_used, 1 + b + 1)
                        if h == 1 and before is not None:
                            pe.wait_ge(pj_used, 1 + before)
                        if h >= 2:
                            pe.wait_ge(s_used, 1 + 16 * b + h - 1)
                        scores(b, u, h, s_ps, qf, kf, s_ready)
                    if before is not None and h >= 2:
                        values(before, 1 - u, h - 2)
                if b is not None:
                    pe.wait_ge(max_ready, 1 + b + 1)
                    project(b, 4, 0, 0)
                    project(b, 5, 0, 1)
                if before is not None:
                    pe.wait_ge(os_ready, 1 + before + 1)
                    if b is not None:
                        pe.wait_ge(proj_used, 1 + PJ * b + 6)
                    for t in range(2):
                        for g in range(4):
                            last = nc.tensor.transpose(qk_ps[t][:, g * P:(g + 1) * P],
                                                       os_[:, g // 2, (g % 2) * L + t * P:(g % 2) * L + (t + 1) * P],
                                                       ident[:])
                    last.then_inc(ob_ready, 1)
                    pe.wait_ge(o_ready, 1 + before + 1)
                    for t in range(2):
                        last = nc.tensor.transpose(tail_ps[:, t * P:(t + 1) * P], o[:, t, :], ident[:])
                    last.then_inc(ot_ready, 1)
                    pe.wait_ge(oT_done, 1 + before + 1)
                    for t in range(2):
                        nc.tensor.matmul(tail_ps[:, L + t * C:L + (t + 1) * C], oT[:, t * P:(t + 1) * P], pw[:],
                                         start=True, stop=False)
                        last = nc.tensor.matmul(tail_ps[:, L + t * C:L + (t + 1) * C], ones_row[:], pbr[:],
                                                start=False, stop=True)
                    last.then_inc(pj_ready, 1)

            in_turn(pe, batch)

        @block.scalar
        def _(act):
            act.wait_ge(weights_in, 1 + 128)

            def high(b, i, which, pair):
                act.wait_ge(proj_ready, 1 + PJ * b + i + 1)
                for j in range(2):
                    g = 2 * pair + j
                    last = nc.scalar.activation(hi[i % 2][:, j, :], qk_ps[i % 2][:, j * L:(j + 1) * L], ACT.Identity,
                                                bias=lo_bias[:, which, g:g + 1], scale=lo_row[:, which:which + 1])
                last.then_inc(hi_ready, 1)

            def batch(b, u, before):
                if b is not None:
                    for i, (which, pair) in enumerate(((1, 0), (1, 1), (0, 0), (0, 1))):
                        high(b, i, which, pair)
                if before is not None:
                    for h in range(NH):
                        act.wait_ge(st_ready, 1 + 16 * before + h + 1)
                        if h >= 4:
                            act.wait_ge(pv_ready, 1 + 16 * before + h - 3)
                        nc.scalar.activation(pt[h % 4][:].rearrange("p t q -> p (t q)"), st_ps[h % 2][:],
                                             ACT.Exp, scale=SCALE).then_inc(p_ready, 1)
                    act.wait_ge(pv_ready, 1 + 16 * before + 16)
                    for j in range(2):
                        last = nc.scalar.copy(os_[:, j, :], o_ps[j][:])
                    last.then_inc(os_ready, 1)
                if b is not None:
                    high(b, 4, 0, 0)
                    high(b, 5, 0, 1)

            in_turn(act, batch)

        @block.vector
        def _(v):
            v.wait_ge(weights_in, 1 + 128)
            v.wait_ge(pool_set, 1 + 4)

            def split(b, i, u, which, pair):
                v.wait_ge(hi_ready, 1 + PJ * b + i + 1)
                dst = (qf, kf)[which][u]
                for j in range(2):
                    g = 2 * pair + j
                    last = nc.vector.scalar_tensor_tensor(dst[:, g, :], qk_ps[i % 2][:, j * L:(j + 1) * L],
                                                          bqk[:, which, g:g + 1], hi[i % 2][:, j, :].bitcast(F32),
                                                          ALU.add, ALU.subtract)
                last.then_inc(proj_used, 1)

            def batch(b, u, before):
                if b is not None:
                    for i, (which, pair) in enumerate(((1, 0), (1, 1), (0, 0), (0, 1))):
                        split(b, i, u, which, pair)
                    v.wait_ge(v_ready, 1 + b + 1)
                    nc.vector.tensor_copy(va[u][:, :, :, 0:HD],
                                          v_ps[:, 0:2 * C].rearrange("p (t h d) -> p t h d", t=2, h=NH))\
                        .then_inc(v_used, 1)
                    for h in range(NH):
                        v.wait_ge(s_ready, 1 + 16 * b + h + 1)
                        nc.vector.tensor_reduce(mx[:, :, h:h + 1], s_ps[h % 2][:].rearrange("p (t k) -> p t k", t=2),
                                                AX, ALU.max).then_inc(s_used, 1)
                    v.wait_ge(s_used, 1 + 16 * b + 16)
                    for t in range(2):
                        for c in range(2):
                            last = nc.vector.tensor_scalar(
                                mxx[:, t, :, :, 3 * HD + c:3 * HD + c + 1].rearrange("p g s c -> p (g s) c"),
                                bc(mx[:, t, :], 2, 1), -1.0, None, ALU.mult)
                    last.then_inc(max_ready, 1)
                if b is not None:
                    split(b, 4, u, 0, 0)
                    split(b, 5, u, 0, 1)
                if before is not None:
                    v.wait_ge(ob_ready, 1 + before + 1)
                    link = loop_link(dve, v, before, 1)
                    heads = [qk_ps[t][:].rearrange("p (h d) -> p h d", h=NH) for t in range(2)]
                    for t in range(2):
                        ins = nc.vector.reciprocal(den[:, t, :],
                                                   heads[t][:, :, HD:HD + 1].rearrange("p h d -> p (h d)"))
                    link(ins)
                    for t in range(2):
                        last = nc.vector.tensor_tensor(o[:, t, :].rearrange("p (h d) -> p h d", h=NH),
                                                       heads[t][:, :, 0:HD], bc(den[:, t, :], 2, HD), ALU.mult)
                    last.then_inc(o_ready, 1)
                    v.wait_ge(ot_ready, 1 + before + 1)
                    nc.vector.tensor_copy(oT[:], tail_ps[:, 0:L]).then_inc(oT_done, 1)
                    v.wait_ge(pj_ready, 1 + before + 1)
                    x2 = xs_all[:, bass.ds(before * 2, 2), :]
                    nc.vector.tensor_tensor(x2, tail_ps[:, L:L + 2 * C].rearrange("p (t c) -> p t c", t=2), x2, ALU.add)\
                        .then_inc(pj_used, 1)

            in_turn(v, batch)

    with ExitStack() as ctx:
        sb, ps, sem = alloc(ctx)
        wgs = sb("wgs", [P, E])
        wa = sb("wa", [P, E, HID])
        wb = sb("wb", [P, E, HID])
        wc = sb("wc", [P, E, 2, C])
        it8 = sb("it86", [P, E])
        xc = sb("xc", [P, CH])
        lg = sb("lg6", [P, TC, E])
        m8 = sb("m86", [P, TC, 8])
        i8 = sb("i86", [P, TC, 8], U32)
        i8f = sb("i8f6", [P, TC, 2])
        dd = sb("dd6", [P, TC, 2])
        wd = sb("wd6", [P, TC, E])
        act_h = [sb(f"act_h{u}", [P, 2, CH]) for u in range(2)]
        hid = [sb(f"hid{u}", [P, 2, CH]) for u in range(2)]
        moe = sb("moe6", [P, TC, C])
        y = sb("y6", [P, TC, C])
        stats = sb("stats6", [P, TC, 6])
        mv = sb("mv6", [P, TC, 2])
        std = sb("std6", [P, TC])
        lps = ps("lps6", [P, 512])
        tps = ps("tps6", [P, 512])
        xin = sb("xin6", [P, TC, C])
        x3 = sb("x36", [P, TC, C])
        h_ps = [ps(f"h_ps{u}", [P, 512]) for u in range(2)]
        g_ps = [ps(f"g_ps{u}", [P, 512]) for u in range(2)]
        eo = [ps(f"eo6{u}", [P, 512]) for u in range(2)]
        names = ("wl6 it8_set staged6 lg_ready6 exp_go6 exp_done6 h_ready6 g_ready6 silu_done hid_done e_ready6 e_used6 "
                 "sq_go6 sq_done6 y_ready6 stored dve6 x3_ready t_ready6").split()
        S = {k: sem(k) for k in names}
        block = ctx.enter_context(nc.Block())

        @block.sync
        def _(sp):
            start_at_one(sp)
            for dst, src in ((wgs[:], wg), (wa[:], w31.rearrange("e d f -> d e f")),
                             (wb[:], w32.rearrange("e d f -> d e f")),
                             (wc[:], w33.rearrange("e (k f) d -> f e k d", f=P))):
                sp.dma_start(dst, src).then_inc(S["wl6"], 16)
            sp.wait_ge(S["wl6"], 1 + 64)
            with sp.Fori(0, TOK // CH) as q:
                sp.wait_ge(S["y_ready6"], 1 + q + 1)
                sp.dma_start(out[bass.ds(q * CH, CH), :].rearrange("(t p) c -> p t c", p=P), y[:])\
                    .then_inc(S["stored"], 16)
            sp.wait_ge(S["stored"], 1 + 16 * (TOK // CH))

        @block.gpsimd
        def _(pool):
            nc.gpsimd.iota(it8[:], pattern=[[1, E]], base=0, channel_multiplier=0,
                           allow_small_or_imprecise_dtypes=True).then_inc(S["it8_set"], 1)

        @block.tensor
        def _(pe):
            pe.wait_ge(S["wl6"], 1 + 64)
            with pe.Fori(0, TOK // CH) as q:
                pe.wait_ge(S["x3_ready"], 1 + q + 1)
                for t in range(TC):
                    last = nc.tensor.transpose(tps[:, t * P:(t + 1) * P], x3[:, t, :], ident[:])
                last.then_inc(S["t_ready6"], 1)
                pe.wait_ge(S["staged6"], 1 + q + 1)
                for t in range(TC):
                    last = nc.tensor.matmul(lps[:, t * E:(t + 1) * E], xc[:, t * P:(t + 1) * P], wgs[:],
                                            start=True, stop=True)
                last.then_inc(S["lg_ready6"], 1)

                def up(e):
                    for k in range(2):
                        pe.wait_ge(S["hid_done"], 1 + q * 16 + 2 * e + k - 1) if e + k >= 1 else \
                            pe.wait_ge(S["hid_done"], 1 + q * 16)
                        nc.tensor.matmul(h_ps[k][:], wa[:, e, k * P:(k + 1) * P], xc[:], start=True, stop=True)\
                            .then_inc(S["h_ready6"], 1)
                        nc.tensor.matmul(g_ps[k][:], wb[:, e, k * P:(k + 1) * P], xc[:], start=True, stop=True)\
                            .then_inc(S["g_ready6"], 1)

                def down(e):
                    pe.wait_ge(S["hid_done"], 1 + q * 16 + 2 * e + 2)
                    pe.wait_ge(S["e_used6"], 1 + q * E + e - 1) if e >= 1 else pe.wait_ge(S["e_used6"], 1 + q * E)
                    for t in range(TC):
                        for k in range(2):
                            last = nc.tensor.matmul(eo[e % 2][:, t * C:(t + 1) * C], hid[e % 2][:, k, t * P:(t + 1) * P],
                                                    wc[:, e, k, :], start=(k == 0), stop=(k == 1))
                    last.then_inc(S["e_ready6"], 1)

                up(0)
                for e in range(1, E):
                    up(e)
                    down(e - 1)
                down(E - 1)

        @block.scalar
        def _(act):
            with act.Fori(0, TOK // CH) as q:
                def root(n):
                    act.wait_ge(S["sq_go6"], 1 + 2 * q + n + 1)
                    nc.scalar.activation(std[:], mv[:, :, 1], ACT.Sqrt, bias=eps_t[:], scale=1.0 / C)\
                        .then_inc(S["sq_done6"], 1)
                root(0)
                act.wait_ge(S["exp_go6"], 1 + q + 1)
                nc.scalar.activation(dd[:, :, 0:1], dd[:, :, 0:1], ACT.Exp).then_inc(S["exp_done6"], 1)
                for m in range(16):
                    e, k = m // 2, m % 2
                    act.wait_ge(S["h_ready6"], 1 + q * 16 + m + 1)
                    if m >= 4:
                        act.wait_ge(S["hid_done"], 1 + q * 16 + m - 3)
                    nc.scalar.activation(act_h[e % 2][:, k, :], h_ps[k][:], ACT.Silu).then_inc(S["silu_done"], 1)
                root(1)

        @block.vector
        def _(v):
            v.wait_ge(S["it8_set"], 1 + 1)
            with v.Fori(0, TOK // CH) as q:
                link = loop_link(S["dve6"], v, q, FFN1_LINKS)
                nc.vector.memset(dd[:, 0, 0:1], 0.0)
                link(nc.vector.tensor_copy(xin[:], xs_all[:, bass.ds(q * TC, TC), :]))
                norm_link(link, v, xin, x3, mv, stats, std, S["sq_go6"], S["sq_done6"], 2 * q, TC, S["x3_ready"])
                v.wait_ge(S["t_ready6"], 1 + q + 1)
                v.wait_ge(S["e_ready6"], 1 + q * E)
                nc.vector.tensor_copy(xc[:], tps[:]).then_inc(S["staged6"], 1)
                v.wait_ge(S["lg_ready6"], 1 + q + 1)
                route_link(link, v, lps[:, 0:TC * E].rearrange("p (t e) -> p t e", t=TC), lg, m8, i8, i8f, dd, wd,
                           it8, S["exp_go6"], S["exp_done6"], q)
                link(nc.vector.tensor_copy(moe[:], x3[:]))

                def gated(e):
                    for k in range(2):
                        m = 2 * e + k
                        v.wait_ge(S["silu_done"], 1 + q * 16 + m + 1)
                        v.wait_ge(S["g_ready6"], 1 + q * 16 + m + 1)
                        if e >= 1:
                            v.wait_ge(S["e_ready6"], 1 + q * E + e - 1)
                        nc.vector.tensor_tensor(hid[e % 2][:, k, :], act_h[e % 2][:, k, :], g_ps[k][:], ALU.mult)\
                            .then_inc(S["hid_done"], 1)

                def combine(e):
                    v.wait_ge(S["e_ready6"], 1 + q * E + e + 1)
                    for t in range(TC):
                        ins = nc.vector.scalar_tensor_tensor(moe[:, t, :], eo[e % 2][:, t * C:(t + 1) * C],
                                                             wd[:, t, e:e + 1], moe[:, t, :], ALU.mult, ALU.add)
                        if t < TC - 1:
                            link(ins)
                        else:
                            ins.then_inc(S["e_used6"], 1)
                            v.wait_ge(S["e_used6"], 1 + q * E + e + 1)
                gated(0)
                for e in range(1, E):
                    gated(e)
                    combine(e - 1)
                combine(E - 1)
                v.wait_ge(S["stored"], 1 + 16 * q)
                norm_link(link, v, moe, y, mv, stats, std, S["sq_go6"], S["sq_done6"], 2 * q + 1, TC, S["y_ready6"])
                assert link.state[0] == FFN1_LINKS, link.state[0]


FFN0_LINKS, FFN1_LINKS = 81, 56


def kernel(**inputs):
    import numpy as np
    import concourse.bacc as bacc
    from concourse.bass_utils import run_bass_kernel_spmd

    a = {k: np.asarray(v) for k, v in inputs.items()}
    x = a["L0_attn_x"].reshape(TOK, C)
    f32 = np.float32
    ar = {}
    ar["x_tok"] = x
    ar["x_T"] = x.T
    ar["x_conv"] = x.reshape(2, GB, A32, R8, C).transpose(3, 0, 4, 1, 2).reshape(NT, C, P)
    ww = a["L0_attn_wave_w"].reshape(H0, 2, C).transpose(2, 1, 0).reshape(C, 2 * H0)
    ar["kw"] = np.concatenate([a["L0_attn_kernel_w"].T, ww], axis=1)
    ar["kbias"] = np.concatenate([a["L0_attn_kernel_b"],
                                  a["L0_attn_wave_b"].reshape(H0, 2).T.reshape(-1)]).reshape(1, -1)
    ar["outwT"] = a["L0_attn_out_w"].T
    cst = np.zeros((P, VW + 1), f32)
    cst[:, :VW] = np.arange(VW) - R8
    cst[:, VW] = R8 * (np.arange(P) % A32)
    ar["cst"] = cst
    edges = np.zeros((P, R8, NE_), f32)
    edges[:, :, :BINS + 1] = np.arange(BINS + 1) * R8 - L
    edges[:, :, 0], edges[:, :, BINS] = -1e6, 1e6
    pos = R8 * (np.arange(P) % A32)[:, None] + np.arange(R8)[None, :]
    edges[:, :, BINS + 1] = -pos
    edges[:, :, BINS + 2] = L - 1 - pos
    ar["edges"] = edges
    ar["ident_d"] = np.eye(P, dtype=f32)
    ar["ln_gb"] = np.stack([a["L0_ffn_ln_g"], a["L0_ffn_ln_b"]], axis=1)
    ar["abel_w"], ar["abel_b"] = a["L0_ffn_abel_w"], a["L0_ffn_abel_b"].reshape(1, C)
    ar["gate_w"], ar["gate_b"] = a["L0_ffn_gate_w_moe"], a["L0_ffn_gate_b_moe"].reshape(1, E)
    ar["w1"], ar["b1"] = a["L0_ffn_w1"], a["L0_ffn_b1"].reshape(E * 4, P).T
    ar["w2"], ar["b2"] = a["L0_ffn_w2"], a["L0_ffn_b2"]
    gens = a["L0_ffn_gens"]
    ar["gens"] = np.concatenate([gens, gens.transpose(0, 2, 1)], axis=0)
    ar["mix_w"] = np.broadcast_to(a["L0_ffn_mix_w"].reshape(1, 2 * C), (P, 2 * C))
    ar["mix_b"] = np.broadcast_to(a["L0_ffn_mix_b"].reshape(1, 1), (P, 1))
    wq = a["L1_attn_qkv_w"][:2 * C].reshape(2, 4, 4, HD, C).transpose(4, 0, 1, 2, 3)
    bq = a["L1_attn_qkv_b"][:2 * C].reshape(2, 4, 4, HD).transpose(2, 3, 0, 1)
    wqk = np.zeros((C, 2, 4, 4, 32), f32)
    bqk = np.zeros((4, 32, 2, 4), f32)
    for k in range(3):
        wqk[..., k * HD:(k + 1) * HD] = wq
        bqk[:, k * HD:(k + 1) * HD] = bq
    bqk[:, 3 * HD:3 * HD + 2, 1, :] = 1.0
    lo = np.zeros((4, 32, 2), f32)
    lo[:, HD:2 * HD, 0] = lo[:, 3 * HD + 1, 0] = lo[:, 2 * HD:3 * HD, 1] = 1.0
    lo_bias = np.where(lo[..., None] > 0, bqk, f32(0))
    ar["wqkv"] = wqk.reshape(C, 2 * 4 * P)
    ar["bqkv"] = np.concatenate([bqk.reshape(P, 8), lo_bias.reshape(P, 8), lo.reshape(P, 2)], axis=1)
    ar["wv"], ar["bv"] = a["L1_attn_qkv_w"][2 * C:].T, a["L1_attn_qkv_b"][2 * C:].reshape(1, C)
    ar["proj_w"], ar["proj_b"] = a["L1_attn_proj_w"].T, a["L1_attn_proj_b"].reshape(1, C)
    ar["wg"], ar["w31"], ar["w32"], ar["w33"] = (a[f"L1_ffn_{k}"] for k in ("Wg", "W1", "W2", "W3"))

    nc = bacc.Bacc("TRN2", target_bir_lowering=False, num_devices=1)
    args, arrays = {}, {}
    for name, arr in ar.items():
        arrays[f"in_{name}"] = np.ascontiguousarray(arr)
        args[name] = nc.dram_tensor(f"in_{name}", arr.shape, F32, kind="ExternalInput").ap()
    kd = nc.dram_tensor("kd", (NT, P, H0 * BINS), F32, kind="Internal").ap()
    out = nc.dram_tensor("out_0", (TOK, C), F32, kind="ExternalOutput").ap()
    build(nc, kd=kd, out=out, **args)
    r = run_bass_kernel_spmd(nc, [arrays], core_ids=[0])
    return r.results[0]["out_0"].reshape(B, L, C)
```

```python
from contextlib import ExitStack

import concourse.bass as bass
from concourse import mybir

F32 = mybir.dt.float32
F32R = mybir.dt.float32r
U32 = mybir.dt.uint32
ALU = mybir.AluOpType
ACT = mybir.ActivationFunctionType
AX = mybir.AxisListType.X

P = 128
B, L, C = 8, 256, 128
TOK = B * L
NT = TOK // P
H0, D0, BINS, TAPS = 8, 16, 64, 32
R8 = 8
A32 = L // R8
GB = 4
NBLK = L // R8 + 1
VW = NBLK * R8
AW = VW + R8
E = 8
DF = 512
HID = 256
NH, HD = 16, 8
CH = 512
TC = CH // P
EPS = 1e-5
MAGIC = 12582912.0
DELTA = 2.0 ** -17
SQUARINGS, DEGREE = 8, 8
NE_ = BINS + 1 + 2


def V(nc, own, eng):
    sem, state = own

    def link(ins):
        state[0] += 1
        ins.then_inc(sem, 1)
        eng.wait_ge(sem, state[0])
    return link


def loop_link(sem, eng, it, per):
    state = [0]

    def link(ins):
        state[0] += 1
        ins.then_inc(sem, 1)
        eng.wait_ge(sem, it * per + state[0])
    link.state = state
    return link


def bc(ap, axis, n):
    d = [list(x) for x in ap.ap]
    d.insert(axis, [0, n])
    return bass.AP(ap.tensor, ap.offset, d)


def build(nc, x_tok, x_T, x_conv, kw, kbias, outwT, head_rows, cst, edges, ident_d, ln_gb, abel_w, abel_b, gate_w, gate_b,
          w1, b1, w2, b2, gens, mix_w, mix_b, wqkv, bqkv, wv, bv, proj_w, proj_b, wg, w31, w32, w33, kd, out):
    top = ExitStack()

    def alloc(ctx):
        def sb(name, shape, dt=F32):
            return ctx.enter_context(nc.sbuf_tensor(name, shape, dt))

        def ps(name, shape):
            return ctx.enter_context(nc.psum_tensor(name, shape, F32))

        def sem(name):
            s = ctx.enter_context(nc.semaphore(name))
            if "dve" not in name:
                started.append(s)
            return s
        return sb, ps, sem

    started = []

    def start_at_one(eng):
        for s in started:
            eng.sem_inc(s, 1)
        started.clear()

    with top:
        sb, _, _ = alloc(top)
        ident = sb("ident", [P, P])
        ones_row = sb("ones_row", [1, P])
        eps_t = sb("eps_t", [P, 1])
        sT = sb("sT", [P, TOK])
        rot = sb("rot", [P, P])

        par_ctx = ExitStack()
        psb, _, _ = alloc(par_ctx)
        wave = psb("wave", [P, NT, 2 * H0])
        par = psb("par", [P, 8, NT, H0])
        FR, INV, INV2, CE, CO, F2, O0, TMP = range(8)
        cst_s = psb("cst_s", [P, VW + 1])
        edges_s = psb("edges_s", [P, R8, NE_])
        W1 = A32 + 1
        dls = psb("dls", [P, NT, 2, H0, W1])
        ea = psb("ea", [P, NT, 2, H0, 2])
        gens_ctx = ExitStack()
        gsb, _, _ = alloc(gens_ctx)
        gs = gsb("gs", [P, 6, P])
        with ExitStack() as ctx:
            sb, ps, sem = alloc(ctx)
            kw_s = sb("kw_s", [P, H0 * BINS + 2 * H0])
            kb_s = sb("kb_s", [P, H0 * BINS + 2 * H0])
            xs = [sb(f"xs{u}", [P, P]) for u in range(2)]
            kst = [sb(f"kst{u}", [P, H0 * BINS]) for u in range(2)]
            kps = [ps(f"kps{u}", [P, 512]) for u in range(2)]
            wps = [ps(f"wps{u}", [P, 512]) for u in range(2)]
            g_in = sem("g_in")
            loaded, x_in = sem("loaded"), [sem(f"x_in{u}") for u in range(2)]
            mm = [sem(f"mm{u}") for u in range(2)]
            k_out = [sem(f"k_out{u}") for u in range(2)]
            k_dma = [sem(f"k_dma{u}") for u in range(2)]
            wave_done, act_done, dve = sem("wave_done"), sem("act_done"), sem("dve")
            block = ctx.enter_context(nc.Block())
            NK = H0 * BINS

            @block.sync
            def _(sp):
                start_at_one(sp)
                for dst, src in ((kw_s, kw), (kb_s, kbias), (ident, ident_d), (cst_s, cst), (edges_s, edges)):
                    sp.dma_start(dst[:], src).then_inc(loaded, 16)
                with sp.Fori(0, NT // 2) as r:
                    for u in range(2):
                        sp.wait_ge(mm[u], 1 + r)
                        sp.dma_start(xs[u][:], x_conv[bass.ds(r * 2 + u, 1), :, :].rearrange("o c p -> (o c) p"))\
                            .then_inc(x_in[u], 16)
                for m in range(6):
                    sp.dma_start(gs[:, m, :], gens[m]).then_inc(g_in, 16)
                sp.wait_ge(g_in, 1 + 96)
                sp.wait_ge(loaded, 1 + 80)

            @block.tensor
            def _(pe):
                pe.wait_ge(loaded, 1 + 80)
                with pe.Fori(0, NT // 2) as r:
                    for u in range(2):
                        pe.wait_ge(x_in[u], 1 + r * 16 + 16)
                        pe.wait_ge(k_out[u], 1 + r)
                        nc.tensor.matmul(kps[u][:, 0:NK], xs[u][:], kw_s[:, 0:NK], start=True, stop=True)
                        nc.tensor.matmul(wps[u][:, 0:16], xs[u][:], kw_s[:, NK:NK + 16], start=True, stop=True)\
                            .then_inc(mm[u], 1)

            @block.scalar
            def _(act):
                with act.Fori(0, NT // 2) as r:
                    for u in range(2):
                        act.wait_ge(k_out[u], 1 + r + 1)
                        act.dma_start(kd[bass.ds(r * 2 + u, 1), :, :].rearrange("o p n -> (o p) n"), kst[u][:])\
                            .then_inc(k_dma[u], 16)
                act.wait_ge(wave_done, 1 + 1)
                nc.scalar.activation(par[:, FR], wave[:, :, 0:H0], ACT.Sigmoid).then_inc(act_done, 1)
                nc.scalar.activation(par[:, TMP], wave[:, :, H0:], ACT.Tanh).then_inc(act_done, 1)
                for u in range(2):
                    act.wait_ge(k_dma[u], 1 + 8 * 16)

            @block.gpsimd
            def _(pool):
                nc.gpsimd.memset(eps_t[:], EPS)
                nc.gpsimd.memset(ones_row[:], 1.0)

            @block.vector
            def _(v):
                v.wait_ge(loaded, 1 + 80)
                with v.Fori(0, NT // 2) as r:
                    for u in range(2):
                        v.wait_ge(mm[u], 1 + r + 1)
                        nc.vector.tensor_tensor(wave[:, bass.ds(r * 2 + u, 1), :], bc(wps[u][:, 0:16], 1, 1),
                                                bc(kb_s[:, NK:NK + 16], 1, 1), ALU.add)
                        v.wait_ge(k_dma[u], 1 + r * 16)
                        nc.vector.tensor_tensor(kst[u][:], kps[u][:], kb_s[:, 0:NK], ALU.add).then_inc(k_out[u], 1)
                for u in range(2):
                    v.wait_ge(k_out[u], 1 + NT // 2)
                nc.vector.memset(sT[:, 0:1], 0.0).then_inc(wave_done, 1)
                v.wait_ge(act_done, 1 + 2)
                link = V(nc, (dve, [0]), v)
                G = lambda k: par[:, k].rearrange("p n h -> p (n h)")
                link(nc.vector.tensor_scalar(G(FR), G(FR), 15.0, 1.0, ALU.mult, ALU.add))
                link(nc.vector.tensor_tensor(G(TMP), G(TMP), G(FR), ALU.mult))
                link(nc.vector.reciprocal(G(INV), G(FR)))
                link(nc.vector.tensor_scalar(G(INV2), G(INV), 0.5, None, ALU.mult))
                link(nc.vector.tensor_scalar(G(F2), G(FR), 2.0, None, ALU.mult))
                link(nc.vector.scalar_tensor_tensor(G(O0), G(FR), -(TAPS // 2 - 0.5), G(TMP), ALU.mult, ALU.add))
                link(nc.vector.tensor_scalar(G(CE), G(O0), cst_s[:, VW:VW + 1], -1.0, ALU.add, ALU.mult))
                link(nc.vector.tensor_tensor(G(CE), G(CE), G(INV2), ALU.mult))
                link(nc.vector.tensor_scalar(G(CO), G(CE), -0.5, None, ALU.add))

        with ExitStack() as ctx:
            sb, ps, sem = alloc(ctx)
            Rk = sb("Rk", [P, 3, P])
            Y = sb("Y", [P, 6, P])
            r01 = sb("r01", [P, P])
            r01T = sb("r01T", [P, P])
            cnt = sb("cnt", [P, NT * H0, NE_])
            nls = sb("nls", [P, 2, NT * H0, A32 + 2])
            sm = sb("sm", [P, 2, NT * H0])
            gp = ps("gp", [P, 2, 512])
            gp2 = ps("gp2", [P, 2, 512])
            pe_done, dve = sem("e_pe"), sem("e_dve")
            raw_half, raw_ready, nl_ready, dl_done, dve_counts = (
                sem(k) for k in ("raw_half", "raw_ready", "nl_ready", "dl_done", "c_dve"))
            block = ctx.enter_context(nc.Block())
            x2d = lambda t, a, b: t[:, a:b, :].rearrange("p m n -> p (m n)")

            started.clear()

            pair = lambda r: slice(r * 2 * H0, (r + 1) * 2 * H0)
            param = lambda k, r: par[:, k, 2 * r:2 * r + 2, :].rearrange("p n h -> p (n h)")

            @block.gpsimd
            def _(pool):
                nc.gpsimd.memset(ea[:, :, 1].rearrange("p n h s -> p n (h s)"), 2.0)
                for r in range(R8):
                    part = cnt[:, pair(r), :]
                    nc.gpsimd.tensor_tensor(part, bc(edges_s[:, r, :], 1, 2 * H0), bc(param(O0, r), 2, NE_),
                                            ALU.subtract).then_inc(raw_half, 1)
                    pool.wait_ge(raw_half, r + 1)
                    nc.gpsimd.tensor_tensor(part, part, bc(param(INV, r), 2, NE_), ALU.mult).then_inc(raw_ready, 1)
                for r in range(R8):
                    pool.wait_ge(nl_ready, r + 1)
                    for side in range(2):
                        for g in range(2):
                            rows = slice((2 * r + g) * H0, (2 * r + g + 1) * H0)
                            last = nc.gpsimd.tensor_tensor(dls[:, 2 * r + g, side], nls[:, side, rows, 1:],
                                                           nls[:, side, rows, 0:W1], ALU.subtract)
                last.then_inc(dl_done, 1)
                pool.wait_ge(dl_done, 1)

            @block.vector
            def _(v):
                link = V(nc, (dve, [0]), v)
                counted = V(nc, (dve_counts, [0]), v)

                def counts(r):
                    v.wait_ge(raw_ready, r + 1)
                    part = cnt[:, pair(r), :]
                    flat_part = part.rearrange("p n e -> p (n e)")
                    counted(nc.vector.tensor_scalar(flat_part, flat_part, 0.5 - DELTA, 0.0, ALU.add, ALU.max))
                    counted(nc.vector.tensor_scalar(flat_part, flat_part, float(TAPS), MAGIC, ALU.min, ALU.add))
                    at = lambda k: bc(part[:, :, k:k + 1].rearrange("p n e -> p (n e)"), 2, A32 + 2)
                    nc.vector.tensor_tensor(nls[:, 0, pair(r), :], part[:, :, 0:A32 + 2], at(BINS + 1), ALU.min)
                    nc.vector.tensor_tensor(nls[:, 1, pair(r), :], part[:, :, A32 - 1:BINS + 1], at(BINS + 2),
                                            ALU.max).then_inc(nl_ready, 1)

                link(nc.vector.tensor_scalar(x2d(gs, 0, 6), x2d(gs, 0, 6), 2.0 ** -SQUARINGS, None, ALU.mult))
                link(nc.vector.tensor_copy(x2d(Rk, 0, 3), x2d(gs, 0, 3)))
                n = 0
                for k in range(DEGREE, 1, -1):
                    n += 1
                    v.wait_ge(pe_done, n)
                    link(nc.vector.scalar_tensor_tensor(x2d(Rk, 0, 3), gp[:, 0, 0:384], 1.0 / k, x2d(gs, 0, 3),
                                                        ALU.mult, ALU.add))
                n += 1
                v.wait_ge(pe_done, n)
                link(nc.vector.tensor_copy(x2d(Y, 0, 3), x2d(Rk, 0, 3)))
                link(nc.vector.tensor_copy(x2d(Y, 3, 6), gp[:, 1, 0:384]))
                assert SQUARINGS == R8
                for step in range(SQUARINGS):
                    n += 1
                    v.wait_ge(pe_done, n)
                    for half in range(2):
                        link(nc.vector.scalar_tensor_tensor(x2d(Y, 3 * half, 3 * half + 3),
                                                            x2d(Y, 3 * half, 3 * half + 3), 2.0,
                                                            gp2[:, half, 0:384], ALU.mult, ALU.add))
                    counts(step)
                n += 1
                v.wait_ge(pe_done, n)
                link(nc.vector.tensor_tensor(r01[:], gp[:, 0, 0:P], Y[:, 0, :], ALU.add))
                link(nc.vector.tensor_tensor(r01[:], r01[:], Y[:, 1, :], ALU.add))
                n += 1
                v.wait_ge(pe_done, n)
                link(nc.vector.tensor_copy(r01T[:], gp[:, 1, 0:P]))
                n += 1
                v.wait_ge(pe_done, n)
                link(nc.vector.tensor_tensor(rot[:], gp2[:, 0, 0:P], r01[:], ALU.add))
                link(nc.vector.tensor_tensor(rot[:], rot[:], Y[:, 2, :], ALU.add))
                link(nc.vector.tensor_tensor(rot[:], rot[:], ident[:], ALU.add))
                whole = lambda k: par[:, k].rearrange("p n h -> p (n h)")
                for side, add, cmp, lim in ((0, 0.0, ALU.is_ge, float(TAPS)), (1, -1.0, ALU.is_le, 0.0)):
                    count = cnt[:, :, BINS + 1 + side:BINS + 2 + side].rearrange("p n e -> p (n e)")
                    edge = bc(edges_s[:, :, BINS + 1 + side:BINS + 2 + side].rearrange("p r e -> p (r e)"), 2, 2 * H0)
                    s0, s1 = sm[:, 0], sm[:, 1]
                    counted(nc.vector.scalar_tensor_tensor(s0, count, add - MAGIC, whole(FR), ALU.add, ALU.mult))
                    counted(nc.vector.tensor_tensor(s1.rearrange("p (r m) -> p r m", r=R8),
                                                    s0.rearrange("p (r m) -> p r m", r=R8), edge, ALU.subtract))
                    counted(nc.vector.tensor_tensor(s1, s1, whole(O0), ALU.add))
                    counted(nc.vector.scalar_tensor_tensor(s1, s1, -1.0, s1, ALU.mult, ALU.max))
                    counted(nc.vector.tensor_scalar(s0, count, lim + MAGIC, 4.0, cmp, ALU.mult))
                    counted(nc.vector.tensor_tensor(
                        ea[:, :, 0, :, side], s1.rearrange("p (n h) -> p n h", n=NT),
                        s0.rearrange("p (n h) -> p n h", n=NT), ALU.add))

            @block.tensor
            def _(pe):
                d = 2
                for k in range(DEGREE, 1, -1):
                    pe.wait_ge(dve, d)
                    for m in range(3):
                        last = nc.tensor.matmul(gp[:, 0, m * P:(m + 1) * P], gs[:, 3 + m, :], Rk[:, m, :],
                                                start=True, stop=True)
                    last.then_inc(pe_done, 1)
                    d += 1
                pe.wait_ge(dve, d)
                for m in range(3):
                    last = nc.tensor.transpose(gp[:, 1, m * P:(m + 1) * P], Rk[:, m, :], ident[:])
                last.then_inc(pe_done, 1)
                d += 2
                for _ in range(SQUARINGS):
                    pe.wait_ge(dve, d)
                    for m in range(3):
                        nc.tensor.matmul(gp2[:, 0, m * P:(m + 1) * P], Y[:, 3 + m, :], Y[:, m, :],
                                         start=True, stop=True)
                    for m in range(3):
                        last = nc.tensor.matmul(gp2[:, 1, m * P:(m + 1) * P], Y[:, m, :], Y[:, 3 + m, :],
                                                start=True, stop=True)
                    last.then_inc(pe_done, 1)
                    d += 2
                pe.wait_ge(dve, d)
                nc.tensor.matmul(gp[:, 0, 0:P], Y[:, 3, :], Y[:, 1, :], start=True, stop=True).then_inc(pe_done, 1)
                d += 2
                pe.wait_ge(dve, d)
                nc.tensor.transpose(gp[:, 1, 0:P], r01[:], ident[:]).then_inc(pe_done, 1)
                d += 1
                pe.wait_ge(dve, d)
                nc.tensor.matmul(gp2[:, 0, 0:P], r01T[:], Y[:, 2, :], start=True, stop=True).then_inc(pe_done, 1)

        gens_ctx.close()

        with ExitStack() as ctx:
            sb, ps, sem = alloc(ctx)
            xn = sb("xn", [P, NT, P])
            XT = sb("XT", [P, TOK])
            ow = sb("ow", [P, P])
            own_rows = sb("own_rows", [P, H0])
            owh = sb("owh", [P, H0, P])
            Ks = [sb(f"Ks{u}", [P, H0, NBLK]) for u in range(2)]
            Kr = [sb(f"Kr{u}", [P, H0, BINS]) for u in range(2)]
            tts = [sb(f"tt{u}", [P, 2, H0, VW]) for u in range(2)]
            cls = [sb(f"cl{u}", [P, 2, H0, VW]) for u in range(2)]
            Ams = [sb(f"Am{u}", [P, H0, AW]) for u in range(2)]
            AT = sb("AT", [P, 2 * H0, P])
            yS = sb("yS", [P, GB, H0, A32])
            dl = sb("dl", [P, 2, H0, W1])
            ends2 = [sb(f"ends{u}", [P, 2, H0]) for u in range(2)]
            eg = sb("eg", [P, H0, 2])
            sm = sb("sm3", [P, 1])
            map_s = sb("map_s", [P, 2, 3, H0])
            spare = sb("spare", [P, 2])
            map_set, w_ready, A_parts = sem("map_set"), sem("w_ready"), sem("A_parts")
            q1s = [sb(f"q1{u}", [P, 2, H0, NBLK]) for u in range(2)]
            q2 = sb("q2", [P, 2, H0, NBLK])
            dW = sb("dW", [P, H0, NBLK])
            tp = [ps(f"tp{k}", [P, 512]) for k in range(4)]
            yps = ps("yps", [P, GB // 2, 512])
            ops = ps("ops", [P, 512])
            ld, kin = sem("ld"), [sem(f"kin{u}") for u in range(2)]
            owh_set, const_set = sem("owh_set"), sem("const_set")
            t_ready, c_ready, g_ready, a_ready = sem("t_ready"), sem("c_ready"), sem("g_ready"), sem("a_ready")
            tp_ready, at_ready, y_ready, ys_ready = sem("tp_ready"), sem("at_ready"), sem("y_ready"), sem("ys_ready")
            o_ready, o_used, A_ready = sem("o_ready"), sem("o_used"), sem("A_ready")
            dve = sem("g_dve")
            block = ctx.enter_context(nc.Block())
            flat = lambda ap: ap.rearrange("p a h v -> p (a h v)")

            def in_turn(eng, tile):
                tile(0, 0, 0, None)
                with eng.Fori(0, R8 - 1) as k:
                    tile(2 * k + 1, k, 1, (2 * k, k, 0))
                    tile(2 * k + 2, k + 1, 0, (2 * k + 1, k, 1))
                tile(NT - 1, R8 - 1, 1, (NT - 2, R8 - 1, 0))

            @block.sync
            def _(sp):
                start_at_one(sp)
                sp.dma_start(xn[:], x_tok.rearrange("(n p) c -> p n c", p=P)).then_inc(ld, 16)
                sp.dma_start(XT[:], x_T).then_inc(ld, 16)
                sp.dma_start(ow[:], outwT).then_inc(ld, 16)
                sp.dma_start(own_rows[:], head_rows).then_inc(ld, 16)

                def tile(n, r, g, before):
                    if before:
                        sp.wait_ge(A_ready, n)
                    row = H0 * BINS
                    base = kd[0:1, 0:1, 0:1]
                    off = n * (P * row)
                    for b in range(GB):
                        sp.dma_start(
                            Ks[g][b * A32:(b + 1) * A32, :, :],
                            bass.AP(base.tensor, off + b * A32 * row + A32 - 1,
                                    [[row - 1, A32], [BINS, H0], [1, NBLK]])).then_inc(kin[g], 16)
                    sp.dma_start(Kr[g][:].rearrange("p h k -> p (h k)"),
                                 bass.AP(base.tensor, off, [[row, P], [1, row]])).then_inc(kin[g], 16)

                in_turn(sp, tile)
                sp.wait_ge(ld, 1 + 64)

            @block.gpsimd
            def _(pool):
                nc.gpsimd.memset(spare[:], 0.0)

                def takes_wait(g):
                    nc.gpsimd.tensor_tensor(spare[:, g:g + 1], spare[:, g:g + 1], spare[:, g:g + 1], ALU.add)

                def numbers(n, g):
                    nc.gpsimd.tensor_copy(map_s[:, g], par[:, INV2:CO + 1, bass.ds(n, 1), :].rearrange(
                        "p k a h -> p k (a h)")).then_inc(map_set, 1)
                    pool.wait_ge(map_set, 1 + n + 1)
                    takes_wait(g)
                    for h in range(H0):
                        for odd in range(2):
                            last = nc.gpsimd.tensor_scalar(tts[g][:, odd, h, :], cst_s[:, 0:VW],
                                                           map_s[:, g, 0, h:h + 1], map_s[:, g, 1 + odd, h:h + 1],
                                                           ALU.mult, ALU.add)
                    last.then_inc(t_ready, 1)

                def tile(n, r, g, before):
                    if not (isinstance(n, int) and n == NT - 1):
                        pool.wait_ge(A_ready, 1 + n)
                        numbers(n + 1, 1 - g)
                    Am = Ams[g]
                    pool.wait_ge(w_ready, 1 + n + 1)
                    if before:
                        pool.wait_ge(tp_ready, n)
                    takes_wait(g)
                    nc.gpsimd.tensor_tensor(
                        Am[:, :, bass.ds(r, VW)].rearrange("p h (c q) -> p h c q", q=R8),
                        tts[g][:, 0].rearrange("p h (c q) -> p h c q", q=R8),
                        bc(Ks[g][:], 3, R8), ALU.mult).then_inc(A_parts, 1)
                    pool.wait_ge(A_parts, 1 + 2 * n + 1)
                    takes_wait(g)
                    a8 = Am[:, :, bass.ds(r + R8, 1)]
                    d3 = [list(x) for x in a8.ap]
                    a8 = bass.AP(a8.tensor, a8.offset, d3[:-1] + [[R8, NBLK - 1]])
                    nc.gpsimd.tensor_tensor(a8, a8, q1s[g][:, 1, :, 1:], ALU.add).then_inc(A_parts, 1)
                    pool.wait_ge(A_parts, 1 + 2 * n + 2)
                    ab = Am[:, :, R8:R8 + 1]
                    ab = bass.AP(ab.tensor, ab.offset, [list(x) for x in ab.ap][:-1] + [[L - 1, 2]])
                    nc.gpsimd.tensor_tensor(ab, ab, ends2[g][:].rearrange("p s h -> p h s"), ALU.subtract)\
                        .then_inc(A_ready, 1)

                numbers(0, 0)
                for u in range(2):
                    nc.gpsimd.memset(Ams[u][:].rearrange("p h v -> p (h v)"), 0.0)
                nc.gpsimd.memset(eg[:, :, 0:1], 1.0)
                nc.gpsimd.memset(eg[:, :, 1:2], -1.0).then_inc(const_set, 1)
                pool.wait_ge(const_set, 1 + 1)
                in_turn(pool, tile)

            @block.scalar
            def _(act):
                def transposed(n, r, g):
                    act.wait_ge(tp_ready, 1 + n + 1)
                    act.wait_ge(y_ready, 1 + n)
                    for k in range(4):
                        last = nc.scalar.copy(AT[:, 4 * k:4 * k + 4, :].rearrange("p a b -> p (a b)"), tp[k][:])
                    last.then_inc(at_ready, 1)

                def mixed(n, r, g):
                    act.wait_ge(y_ready, 1 + n + 1)
                    act.wait_ge(o_ready, 1 + n)
                    for k in range(GB // 2):
                        last = nc.scalar.copy(yS[:, 2 * k:2 * k + 2].rearrange("p b h a -> p (b h a)"), yps[:, k, :])
                    last.then_inc(ys_ready, 1)

                def clamp(n, g):
                    act.wait_ge(t_ready, 1 + n + 1)
                    nc.scalar.activation(flat(cls[g][:]), flat(tts[g][:]), ACT.Relu).then_inc(c_ready, 1)

                def output(n, r, g):
                    act.wait_ge(o_ready, 1 + n + 1)
                    dst = sT[:, g * GB * L:(g + 1) * GB * L].rearrange("p (b a e) -> p b a e", b=GB, e=R8)
                    nc.scalar.copy(dst[:, :, :, bass.ds(r, 1)].rearrange("p b a e -> p b (a e)"),
                                   ops[:, 0:P].rearrange("p (b a) -> p b a", b=GB)).then_inc(o_used, 1)

                def tile(n, r, g, before):
                    act.wait_ge(g_ready, 1 + 2 * n + 1)
                    for h in range(H0):
                        if h == H0 // 2:
                            act.wait_ge(g_ready, 1 + 2 * n + 2)
                        last = nc.scalar.activation(
                            tts[g][:, :, h, :], cls[g][:, :, h, :], ACT.Abs,
                            scale=par[:, F2, bass.ds(n, 1), h:h + 1].rearrange("p a b -> p (a b)"))
                    last.then_inc(a_ready, 1)
                    if before:
                        transposed(*before)
                    if not (isinstance(n, int) and n == NT - 1):
                        act.wait_ge(A_ready, 1 + n)
                        clamp(n + 1, 1 - g)
                    if before:
                        mixed(*before)
                        output(*before)

                clamp(0, 0)
                in_turn(act, tile)
                transposed(NT - 1, R8 - 1, 1)
                mixed(NT - 1, R8 - 1, 1)
                output(NT - 1, R8 - 1, 1)

            @block.tensor
            def _(pe):
                pe.wait_ge(owh_set, 1 + 1)
                pe.wait_ge(ld, 1 + 64)
                with pe.Fori(0, R8) as r:
                    for g in range(2):
                        n = r * 2 + g
                        pe.wait_ge(A_ready, 1 + n + 1)
                        pe.wait_ge(at_ready, 1 + n)
                        for k in range(4):
                            for j in range(4):
                                h, jc = (4 * k + j) // 2, j % 2
                                last = nc.tensor.transpose(tp[k][:, j * P:(j + 1) * P],
                                                           Ams[g][:, h, R8 + jc * P:R8 + (jc + 1) * P], ident[:])
                        last.then_inc(tp_ready, 1)
                        pe.wait_ge(at_ready, 1 + n + 1)
                        pe.wait_ge(ys_ready, 1 + n)
                        for b in range(GB):
                            for jc in range(2):
                                last = nc.tensor.matmul(
                                    yps[:, b // 2, (b % 2) * L:(b % 2 + 1) * L], xn[:, (g * GB + b) * 2 + jc, :],
                                    AT[:].rearrange("p (h j) t -> p j h t", j=2)[:, jc, :, b * A32:(b + 1) * A32],
                                    start=(jc == 0), stop=(jc == 1))
                        last.then_inc(y_ready, 1)
                        pe.wait_ge(ys_ready, 1 + n + 1)
                        pe.wait_ge(o_used, 1 + n)
                        for h in range(H0):
                            last = nc.tensor.matmul(ops[:, 0:P], owh[:, h, :], yS[:, :, h, :],
                                                    start=(h == 0), stop=(h == H0 - 1))
                        last.then_inc(o_ready, 1)

            @block.vector
            def _(v):
                v.wait_ge(ld, 1 + 64)
                PER = 12
                for h in range(H0):
                    last = nc.vector.tensor_scalar(owh[:, h, :], ow[:], own_rows[:, h:h + 1], None, ALU.mult)
                last.then_inc(owh_set, 1)

                def tile(n, r, g, before):
                    tt_, cl, ends, q1 = tts[g], cls[g], ends2[g], q1s[g]
                    link = loop_link(dve, v, n, PER)
                    pr = lambda k: par[:, k, bass.ds(n, 1), :].rearrange("p a h -> p (a h)")

                    v.wait_ge(c_ready, 1 + n + 1)
                    for half in range(2):
                        heads = slice(half * H0 // 2, (half + 1) * H0 // 2)
                        c, t = (x[:, :, heads, :].rearrange("p a h v -> p a (h v)") for x in (cl, tt_))
                        link(nc.vector.tensor_scalar(c, c, float(TAPS // 2 - 1), MAGIC, ALU.min, ALU.add))
                        nc.vector.scalar_tensor_tensor(c, c, MAGIC, t, ALU.subtract, ALU.subtract)\
                            .then_inc(g_ready, 1)
                    v.wait_ge(kin[g], 1 + (r + 1) * 80)
                    kr = Kr[g][:, :, 0:W1]
                    kr = bass.AP(kr.tensor, kr.offset, [list(kr.ap[0]), [A32 - 1, 2], [BINS, H0], [1, W1]])
                    link(nc.vector.tensor_tensor(dl[:], dls[:, bass.ds(n, 1)].rearrange("p a s h e -> p (a s) h e"),
                                                 kr, ALU.mult))
                    link(nc.vector.tensor_reduce(ends[:].rearrange("p s h -> p (s h)"),
                                                 dl[:].rearrange("p s h e -> p (s h) e"), AX, ALU.add))
                    link(nc.vector.tensor_tensor(dW[:, :, 1:], Ks[g][:, :, 0:NBLK - 1], Ks[g][:, :, 1:],
                                                 ALU.subtract))
                    v.wait_ge(a_ready, 1 + n + 1)
                    if before is None:
                        v.wait_ge(const_set, 1 + 1)
                    ta = tt_[:, :, :, bass.ds(R8 - r, 1)]
                    tg = cl[:, 0, :, bass.ds(R8 - r, 1)]
                    d4 = [list(x) for x in ta.ap]
                    d3 = [list(x) for x in tg.ap]
                    nc.vector.memset(sm[:], 0.0)
                    link(nc.vector.tensor_copy(bass.AP(ta.tensor, ta.offset, d4[:-1] + [[L - 1, 2]]),
                                               ea[:, bass.ds(n, 1)].rearrange("p a k h s -> p (a k) h s")))
                    nc.vector.memset(sm[:], 0.0)
                    link(nc.vector.tensor_copy(bass.AP(tg.tensor, tg.offset, d3[:-1] + [[L - 1, 2]]), eg[:]))
                    blk = lambda t: t[:].rearrange("p a h (c q) -> p (a h c) q", q=R8)[:, :, 0:1]\
                        .rearrange("p c q -> p (c q)")
                    q1f, q2f = (t[:].rearrange("p a h c -> p (a h c)") for t in (q1, q2))
                    link(nc.vector.tensor_scalar(q1f, blk(tt_), 1.0, -1.0, ALU.min, ALU.add))
                    link(nc.vector.scalar_tensor_tensor(q2f, blk(cl), 0.0, q1f, ALU.is_lt, ALU.mult))
                    link(nc.vector.tensor_tensor(q1[:, 0], q2[:, 0], q2[:, 1], ALU.add))
                    link(nc.vector.tensor_tensor(q1[:, 1, :, 1:], q1[:, 0, :, 1:], dW[:, :, 1:], ALU.mult))
                    tE = tt_[:, 0].rearrange("p h v -> p (h v)")
                    tO = tt_[:, 1].rearrange("p h v -> p (h v)")
                    link(nc.vector.tensor_scalar(tO, tO, 1.0, -2.0, ALU.min, ALU.add))
                    nc.vector.scalar_tensor_tensor(tE, tE, 1.0, tO, ALU.min, ALU.add).then_inc(w_ready, 1)
                    assert link.state[0] == PER, link.state[0]

                in_turn(v, tile)
                v.wait_ge(o_used, 1 + NT)
                nc.vector.tensor_tensor(sT[:], XT[:], sT[:], ALU.subtract)

        par_ctx.close()
        sb, _, _ = alloc(top)
        xs_all = sb("xs_all", [P, NT, P])
        xT_all = sb("xT_all", [P, TOK])
        return finish(nc, top, alloc, start_at_one, ident, ones_row, eps_t, sT, rot, xs_all, xT_all, ln_gb, abel_w, abel_b, gate_w, gate_b,
                      w1, b1, w2, b2, mix_w, mix_b, wqkv, bqkv, wv, bv, proj_w, proj_b, wg, w31, w32, w33, out)


def finish(nc, top, alloc, start_at_one, ident, ones_row, eps_t, sT, rot, xs_all, xT_all, ln_gb, abel_w, abel_b, gate_w, gate_b,
           w1, b1, w2, b2, mix_w, mix_b, wqkv, bqkv, wv, bv, proj_w, proj_b, wg, w31, w32, w33, out):
    def norm_link(link, v, src, dst, mv, stats, std, sqrt_go, sqrt_done, n, count, done=None, parts=1):
        for t in range(count):
            ins = nc.vector.bn_stats(stats[:, t, :], src[:, t, :])
        link(ins)
        one = lambda k: stats[:, 0:count, k:k + 1]
        link(nc.vector.tensor_tensor(mv[:, 0:count, 0:1], one(1), one(4), ALU.add))
        link(nc.vector.tensor_tensor(one(0), one(1), one(4), ALU.subtract))
        link(nc.vector.tensor_tensor(one(2), one(2), one(5), ALU.add))
        link(nc.vector.scalar_tensor_tensor(one(0), one(0), C / 4.0, one(0), ALU.mult, ALU.mult))
        link(nc.vector.tensor_scalar(mv[:, 0:count, 0:1], mv[:, 0:count, 0:1], 0.5, None, ALU.mult))
        nc.vector.tensor_tensor(mv[:, 0:count, 1:2], one(2), one(0), ALU.add).then_inc(sqrt_go, 1)
        v.wait_ge(sqrt_done, 1 + n + 1)
        link(nc.vector.reciprocal(std[:, 0:count], std[:, 0:count]))
        for t in range(count):
            ins = nc.vector.tensor_scalar(dst[:, t, :], src[:, t, :], mv[:, t, 0:1], std[:, t:t + 1],
                                          ALU.subtract, ALU.mult)
            if done is not None and (t + 1) % (count // parts) == 0:
                ins.then_inc(done, 1)
        if done is None:
            link(ins)

    def route_link(link, v, lg_ps, lg, m8, i8, i8f, dd, wd, it8, exp_go, exp_done, bias=None):
        if bias is None:
            link(nc.vector.tensor_copy(lg[:], lg_ps))
        else:
            link(nc.vector.tensor_tensor(lg[:], lg_ps, bc(bias, 1, NT), ALU.add))
        for t in range(NT):
            ins = nc.vector.max(m8[:, t, :], lg[:, t, :])
        link(ins)
        for t in range(NT):
            ins = nc.vector.max_index(i8[:, t, :], m8[:, t, :], lg[:, t, :])
        link(ins)
        link(nc.vector.tensor_copy(i8f[:], i8[:, :, 0:2]))
        nc.vector.tensor_tensor(dd[:, :, 0:1], m8[:, :, 1:2], m8[:, :, 0:1], ALU.subtract).then_inc(exp_go, 1)
        v.wait_ge(exp_done, 1 + 1)
        link(nc.vector.tensor_scalar(dd[:, :, 1:2], dd[:, :, 0:1], 1.0, None, ALU.add))
        link(nc.vector.reciprocal(dd[:, :, 1:2], dd[:, :, 1:2]))
        link(nc.vector.tensor_tensor(dd[:, :, 0:1], dd[:, :, 0:1], dd[:, :, 1:2], ALU.mult))
        for t in range(NT):
            nc.vector.tensor_scalar(wd[:, t, :], it8[:], i8f[:, t, 0:1], dd[:, t, 1:2], ALU.is_equal, ALU.mult)
            last = nc.vector.tensor_scalar(lg[:, t, :], it8[:], i8f[:, t, 1:2], dd[:, t, 0:1],
                                           ALU.is_equal, ALU.mult)
        link(last)
        link(nc.vector.tensor_tensor(wd[:], wd[:], lg[:], ALU.add))

    flat2 = lambda ap: ap.rearrange("p a b -> p (a b)")

    sb, _, _ = alloc(top)
    wqk = sb("wqk", [P, 2, 4, P])
    bqk = sb("bqk", [P, 2, 4])
    lo_bias = sb("lo_bias", [P, 2, 4])
    lo_row = sb("lo_row", [P, 2])
    wvs = sb("wvs", [P, C])
    bvr = sb("bvr", [1, C])
    pw = sb("pw", [P, C])
    pbr = sb("pbr", [1, C])
    with ExitStack() as ctx:
        sb, ps, sem = alloc(ctx)
        w1s = sb("w1s", [P, E, DF])
        w2s = sb("w2s", [P, E, 4, C])
        b1s = sb("b1s", [P, E * 4])
        b2s = sb("b2s", [E, C])
        aw = sb("aw", [P, C])
        abr = sb("abr", [1, C])
        gw = sb("gw", [P, E])
        gbr = sb("gbr", [P, E])
        gb = sb("gb", [P, 2])
        mixs = sb("mixs", [P, 2, C])
        mb = sb("mb", [P, 1])
        it8 = sb("it8", [P, E])
        x1 = sb("x1", [P, NT, C])
        xh = sb("xh", [P, NT, C])
        xnT = sb("xnT", [P, TOK])
        w1h, w1l = sb("w1h", [P, E, DF], F32R), sb("w1l", [P, E, DF], F32R)
        xnh, xnl = sb("xnh", [P, TOK], F32R), sb("xnl", [P, TOK], F32R)
        stats = sb("stats", [P, NT, 6])
        mv = sb("mv", [P, NT, 2])
        std = sb("std", [P, NT])
        lg = sb("lg", [P, NT, E])
        m8 = sb("m8", [P, NT, 8])
        i8 = sb("i8", [P, NT, 8], U32)
        i8f = sb("i8f", [P, NT, 2])
        dd = sb("dd", [P, NT, 2])
        wd = sb("wd", [P, NT, E])
        wT = sb("wT", [E, TOK])
        abel = sb("abel", [P, NT, C])
        hT = [sb(f"hT{u}", [P, 4, CH]) for u in range(2)]
        moe = sb("moe", [P, NT, C])
        moeT = xnT
        nona = sb("nona", [P, NT, C])
        junk = sb("junk", [P, C])
        z = sb("z", [P, NT, 2])
        wide, work = ps("wide", [P, TC, 512]), ps("work", [P, TC, 512])
        hps = [work[:, u, :] for u in range(2)]
        eo = [work[:, 2 + u, :] for u in range(2)]
        wl_iota = sem("wl_iota")
        weights_in = sem("weights_in")
        wl, dve, dve_loop = sem("wl"), sem("f_dve"), sem("f_dve_loop")
        tp_s, tp_x, tp_w, tp_m, tp_y = (sem(f"tp_{k}") for k in "sxwmy")
        sqrt_go, sqrt_done, exp_go, exp_done = sem("sqrt_go"), sem("sqrt_done"), sem("exp_go"), sem("exp_done")
        xh_ready, xn_ready, lg_ready, wd_ready, wT_ready, ab_ready, ab_act = (
            sem(k) for k in ("xh_ready", "xn_ready", "lg_ready", "wd_ready", "wT_ready", "ab_ready", "ab_act"))
        h_ps, h_ready, e_ready, e_used = (sem(k) for k in ("h_ps", "h_ready", "e_ready", "e_used"))
        moeT_ready, rot_ready, z_go, z_done = (sem(k) for k in ("moeT_ready", "rot_ready", "z_go", "z_done"))
        x2_ready, x2T_done = sem("x2_ready"), sem("x2T_done")
        w_high, w_low, x_high, x_low = sem("w_high"), sem("w_low"), sem("x_high"), sem("x_low")
        begun = sem("begun")
        block = ctx.enter_context(nc.Block())

        @block.sync
        def _(sp):
            start_at_one(sp)
            for dst, src in ((w1s[:], w1.rearrange("e d f -> d e f")),
                             (w2s[:], w2.rearrange("e (k f) d -> f e k d", f=P)),
                             (b1s[:], b1), (b2s[:], b2), (aw[:], abel_w), (abr[:], abel_b), (gw[:], gate_w),
                             (gbr[:], gate_b), (gb[:], ln_gb), (mixs[:].rearrange("p a c -> p (a c)"), mix_w),
                             (mb[:], mix_b)):
                sp.dma_start(dst, src).then_inc(wl, 16)
            for dst, src in ((wqk[:].rearrange("p a b c -> p (a b c)"), wqkv),
                             (bqk[:].rearrange("p a b -> p (a b)"), bqkv[:, 0:8]),
                             (lo_bias[:].rearrange("p a b -> p (a b)"), bqkv[:, 8:16]), (lo_row[:], bqkv[:, 16:18]),
                             (wvs[:], wv), (bvr[:], bv), (pw[:], proj_w), (pbr[:], proj_b)):
                sp.dma_start(dst, src).then_inc(weights_in, 16)
            sp.wait_ge(weights_in, 1 + 128)
            sp.wait_ge(wl, 1 + 176)

        @block.gpsimd
        def _(pool):
            nc.gpsimd.iota(it8[:], pattern=[[1, E]], base=0, channel_multiplier=0,
                           allow_small_or_imprecise_dtypes=True).then_inc(wl_iota, 1)
            pool.wait_ge(wl, 1 + 176)
            pool.wait_ge(w_high, 1 + 1)
            nc.gpsimd.tensor_tensor(flat2(w1l[:]), flat2(w1s[:]), flat2(w1h[:]).bitcast(F32), ALU.subtract)\
                .then_inc(w_low, 1)
            for b in range(NT // TC):
                part = slice(b * CH, (b + 1) * CH)
                pool.wait_ge(x_high, 1 + b + 1)
                nc.gpsimd.tensor_tensor(xnl[:, part], xnT[:, part], xnh[:, part].bitcast(F32), ALU.subtract)\
                    .then_inc(x_low, 1)

        bank = lambda t: wide[:, t // TC, (t % TC) * P:(t % TC + 1) * P]
        chunks = wide[:].rearrange("p b (t c) -> p (b t) c", t=TC)

        @block.tensor
        def _(pe):
            pe.wait_ge(begun, 1)
            for t in range(NT):
                last = nc.tensor.transpose(bank(t), sT[:, t * P:(t + 1) * P], ident[:])
            last.then_inc(tp_s, 1)
            pe.wait_ge(xh_ready, 1 + 1)
            for t in range(NT):
                last = nc.tensor.transpose(bank(t), xh[:, t, :], ident[:])
                if t % TC == TC - 1:
                    last.then_inc(tp_x, 1)
            pe.wait_ge(wl, 1 + 176)
            pe.wait_ge(xn_ready, 1 + NT // TC)
            for t in range(NT):
                last = nc.tensor.matmul(eo[1][:, t * E:(t + 1) * E], xnT[:, t * P:(t + 1) * P], gw[:],
                                        start=True, stop=True)
            last.then_inc(lg_ready, 1)
            for t in range(NT):
                nc.tensor.matmul(bank(t), xnT[:, t * P:(t + 1) * P], aw[:], start=True, stop=False)
                last = nc.tensor.matmul(bank(t), ones_row[:], abr[:], start=False, stop=True)
                if t % TC == TC - 1:
                    last.then_inc(ab_ready, 1)

            pe.wait_ge(w_low, 1 + 1)
            pe.wait_ge(x_low, 1 + NT // TC)
            with pe.Fori(0, TOK // CH) as q:
                def up(e):
                    for k in range(4):
                        m = e * 4 + k
                        if m >= 2:
                            pe.wait_ge(h_ready, 1 + q * 32 + m - 1)
                        else:
                            pe.wait_ge(h_ready, 1 + q * 32)
                        for w, x in ((w1h, xnh), (w1h, xnl), (w1l, xnh)):
                            last = nc.tensor.matmul(hps[m % 2], w[:, e, k * P:(k + 1) * P], x[:, bass.ds(q * CH, CH)],
                                                    start=(x is xnh and w is w1h), stop=(w is w1l))
                        last.then_inc(h_ps, 1)

                def down(e):
                    pe.wait_ge(h_ready, 1 + q * 32 + 4 * e + 4)
                    pe.wait_ge(e_used, 1 + q * E + e - 1) if e >= 1 else pe.wait_ge(e_used, 1 + q * E)
                    for t in range(TC):
                        for k in range(4):
                            last = nc.tensor.matmul(eo[e % 2][:, t * C:(t + 1) * C], hT[e % 2][:, k, t * P:(t + 1) * P],
                                                    w2s[:, e, k, :], start=(k == 0), stop=(k == 3))
                    last.then_inc(e_ready, 1)

                up(0)
                for e in range(1, E):
                    up(e)
                    down(e - 1)
                down(E - 1)

            pe.wait_ge(ab_act, 1 + NT // TC)
            pe.wait_ge(wd_ready, 1 + 1)
            for t in range(NT):
                last = nc.tensor.matmul(bank(t)[0:E, :], wd[:, t, :], ident[:], start=True, stop=True)
            last.then_inc(tp_w, 1)
            pe.wait_ge(wT_ready, 1 + NT // TC)
            pe.wait_ge(e_used, 1 + E * (NT // TC))
            for b in range(NT // TC):
                nc.tensor.matmul(wide[:, b, :], b2s[:], wT[:, b * CH:(b + 1) * CH], start=True, stop=False)
                for t in range(b * TC, b * TC + TC):
                    last = nc.tensor.matmul(bank(t), moe[:, t, :], ident[:], start=False, stop=(t % TC == TC - 1))
                last.then_inc(tp_m, 1)
            for b in range(NT // TC):
                pe.wait_ge(moeT_ready, 1 + b + 1)
                for t in range(b * TC, b * TC + TC):
                    last = nc.tensor.matmul(work[:, b, (t % TC) * C:(t % TC + 1) * C], moeT[:, t * P:(t + 1) * P],
                                            rot[:], start=True, stop=True)
                last.then_inc(rot_ready, 1)
            pe.wait_ge(x2_ready, 1 + 1)
            for t in range(NT):
                last = nc.tensor.transpose(bank(t), xs_all[:, t, :], ident[:])
                if t % TC == TC - 1:
                    last.then_inc(tp_y, 1)

        @block.scalar
        def _(act):
            act.wait_ge(begun, 1)

            def root(n):
                act.wait_ge(sqrt_go, 1 + n + 1)
                nc.scalar.activation(std[:], mv[:, :, 1], ACT.Sqrt, bias=eps_t[:], scale=1.0 / C).then_inc(sqrt_done, 1)
            root(0)
            root(1)
            act.wait_ge(wl, 1 + 176)
            nc.scalar.copy(flat2(w1h[:]), flat2(w1s[:])).then_inc(w_high, 1)
            for b in range(NT // TC):
                act.wait_ge(xn_ready, 1 + b + 1)
                nc.scalar.copy(xnh[:, b * CH:(b + 1) * CH], xnT[:, b * CH:(b + 1) * CH]).then_inc(x_high, 1)
            act.wait_ge(exp_go, 1 + 1)
            nc.scalar.activation(dd[:, :, 0:1], dd[:, :, 0:1], ACT.Exp).then_inc(exp_done, 1)
            for b in range(NT // TC):
                act.wait_ge(ab_ready, 1 + b + 1)
                nc.scalar.activation(flat2(abel[:, b * TC:(b + 1) * TC, :]), wide[:, b, :], ACT.Gelu).then_inc(ab_act, 1)
            act.wait_ge(wl, 1 + 176)
            with act.Fori(0, TOK // CH) as q:
                for m in range(32):
                    e, k = m // 4, m % 4
                    act.wait_ge(h_ps, 1 + q * 32 + m + 1)
                    if k == 0:
                        act.wait_ge(e_ready, 1 + q * E + e - 1) if e >= 1 else act.wait_ge(e_ready, 1 + q * E)
                    nc.scalar.activation(hT[e % 2][:, k, :], hps[m % 2], ACT.Gelu, bias=b1s[:, m:m + 1])\
                        .then_inc(h_ready, 1)
            act.wait_ge(tp_w, 1 + 1)
            for b in range(NT // TC):
                nc.scalar.copy(wT[:, b * CH:(b + 1) * CH], wide[0:E, b, :]).then_inc(wT_ready, 1)
            for b in range(NT // TC):
                act.wait_ge(tp_m, 1 + b + 1)
                nc.scalar.copy(moeT[:, b * CH:(b + 1) * CH], wide[:, b, :]).then_inc(moeT_ready, 1)
            act.wait_ge(z_go, 1 + 1)
            nc.scalar.activation(z[:, :, 0:1], z[:, :, 0:1], ACT.Exp, scale=-1.0).then_inc(z_done, 1)
            root(2)
            for b in range(NT // TC):
                act.wait_ge(tp_y, 1 + b + 1)
                nc.scalar.copy(xT_all[:, b * CH:(b + 1) * CH], wide[:, b, :]).then_inc(x2T_done, 1)
            act.wait_ge(x2T_done, 1 + NT // TC)

        @block.vector
        def _(v):
            v.wait_ge(wl_iota, 1 + 1)
            link = V(nc, (dve, [0]), v)
            v.wait_ge(begun, 1)
            v.wait_ge(tp_s, 1 + 1)
            norm_link(link, v, chunks, x1, mv, stats, std, sqrt_go, sqrt_done, 0, NT)
            norm_link(link, v, x1, xh, mv, stats, std, sqrt_go, sqrt_done, 1, NT, xh_ready)
            v.wait_ge(wl, 1 + 176)
            for b in range(NT // TC):
                v.wait_ge(tp_x, 1 + b + 1)
                nc.vector.tensor_scalar(xnT[:, b * CH:(b + 1) * CH], wide[:, b, :], gb[:, 0:1], gb[:, 1:2],
                                        ALU.mult, ALU.add).then_inc(xn_ready, 1)
            v.wait_ge(lg_ready, 1 + 1)
            route_link(link, v, eo[1][:, 0:NT * E].rearrange("p (t e) -> p t e", t=NT), lg, m8, i8, i8f, dd, wd,
                       it8, exp_go, exp_done, gbr[:])
            nc.vector.memset(junk[:, 0:1], 0.0).then_inc(wd_ready, 1)
            v.wait_ge(wd_ready, 1 + 1)

            with v.Fori(0, TOK // CH) as q:
                linked = loop_link(dve_loop, v, q, E * (TC - 1))
                for e in range(E):
                    v.wait_ge(e_ready, 1 + q * E + e + 1)
                    for t in range(TC):
                        tile = bass.ds(q * TC + t, 1)
                        acc = moe[:, tile, :].rearrange("p a c -> p (a c)")
                        part = eo[e % 2][:, t * C:(t + 1) * C]
                        weight = wd[:, tile, e:e + 1].rearrange("p a c -> p (a c)")
                        if e == 0:
                            ins = nc.vector.tensor_scalar(acc, part, weight, None, ALU.mult)
                        else:
                            ins = nc.vector.scalar_tensor_tensor(acc, part, weight, acc, ALU.mult, ALU.add)
                        if t < TC - 1:
                            linked(ins)
                        else:
                            ins.then_inc(e_used, 1)
                            v.wait_ge(e_used, 1 + q * E + e + 1)

            v.wait_ge(ab_act, 1 + NT // TC)
            for t in range(NT):
                link(nc.vector.scalar_tensor_tensor(junk[:], abel[:, t, :], 1.0, mixs[:, 0, :], ALU.mult,
                                                    ALU.mult, accum_out=z[:, t, 0:1]))
            for b in range(NT // TC):
                v.wait_ge(rot_ready, 1 + b + 1)
                link(nc.vector.tensor_copy(flat2(nona[:, b * TC:(b + 1) * TC, :]), work[:, b, :]))
                for t in range(b * TC, b * TC + TC):
                    link(nc.vector.scalar_tensor_tensor(junk[:], nona[:, t, :], 1.0, mixs[:, 1, :], ALU.mult,
                                                        ALU.mult, accum_out=z[:, t, 1:2]))
            link(nc.vector.tensor_tensor(z[:, :, 0:1], z[:, :, 0:1], z[:, :, 1:2], ALU.add))
            nc.vector.tensor_scalar(z[:, :, 0:1], z[:, :, 0:1], mb[:], None, ALU.add).then_inc(z_go, 1)
            link(nc.vector.tensor_tensor(flat2(nona[:]), flat2(nona[:]), flat2(abel[:]), ALU.subtract))
            link(nc.vector.scalar_tensor_tensor(flat2(x1[:]), flat2(x1[:]), 2.0, flat2(abel[:]), ALU.mult, ALU.add))
            v.wait_ge(z_done, 1 + 1)
            link(nc.vector.tensor_scalar(z[:, :, 1:2], z[:, :, 0:1], 1.0, None, ALU.add))
            link(nc.vector.reciprocal(z[:, :, 1:2], z[:, :, 1:2]))
            for t in range(NT):
                ins = nc.vector.scalar_tensor_tensor(xh[:, t, :], nona[:, t, :], z[:, t, 1:2], x1[:, t, :],
                                                     ALU.mult, ALU.add)
            link(ins)
            norm_link(link, v, xh, xs_all, mv, stats, std, sqrt_go, sqrt_done, 2, NT, x2_ready)

    sb, _, _ = alloc(top)
    wgs = sb("wgs", [P, E])
    wa = sb("wa", [P, E, HID])
    wb = sb("wb", [P, E, HID])
    wc = sb("wc", [P, E, 2, C])
    wah, wal, wbh, wbl = (sb(k, [P, E, HID], F32R) for k in ("wah", "wal", "wbh", "wbl"))
    with ExitStack() as ctx:
        sb, ps, sem = alloc(ctx)
        xb = sb("xb", [P, L])
        hi = [sb(f"hi{u}", [P, 2, L], F32R) for u in range(2)]
        qf = [sb(f"qf{u}", [P, 4, L], F32R) for u in range(2)]
        kf = [sb(f"kf{u}", [P, 4, L], F32R) for u in range(2)]
        va = [sb(f"va{u}", [P, 2, NH, 32]) for u in range(2)]
        mx = sb("mx", [P, 2, NH])
        mxx = sb("mxx", [P, 2, 4, 4, 32])
        pt = [sb(f"pt{u}", [P, 2, L]) for u in range(4)]
        os_ = sb("os_", [P, 2, 512])
        o = sb("o", [P, 2, C])
        den = sb("den", [P, 2, NH])
        oT = sb("oT", [P, L])
        qk_ps = [ps(f"qk_ps{u}", [P, 512]) for u in range(2)]
        s_ps = [ps(f"s_ps{u}", [P, 512]) for u in range(2)]
        st_ps = [ps(f"st_ps{u}", [P, 512]) for u in range(2)]
        o_ps = [ps(f"o_ps{u}", [P, 512]) for u in range(2)]
        v_ps, tail_ps = s_ps
        staged, ffn1_in, ffn1_high = sem("staged5"), sem("ffn1_in"), sem("ffn1_high")
        proj_ready, hi_ready, proj_used = sem("proj_ready"), sem("hi_ready"), sem("proj_used")
        v_ready, v_used, s_ready, s_used, max_ready = (sem(k) for k in ("v_ready", "v_used", "s_ready", "s_used",
                                                                         "max_ready"))
        st_ready, p_ready, pv_ready = sem("st_ready"), sem("p_ready"), sem("pv_ready")
        o_ready, ot_ready, oT_done, pj_ready, pj_used = (sem(k) for k in ("o_ready5", "ot_ready", "oT_done",
                                                                          "pj_ready", "pj_used"))
        os_ready, ob_ready = sem("os_ready"), sem("ob_ready")
        dve, pool_set = sem("dve5"), sem("pool_set")
        begun5 = sem("begun5")
        block = ctx.enter_context(nc.Block())
        SCALE = float(HD) ** -0.5
        PJ = 6

        def in_turn(eng, batch):
            batch(0, 0, None)
            with eng.Fori(0, B // 2 - 1) as k:
                batch(2 * k + 1, 1, 2 * k)
                batch(2 * k + 2, 0, 2 * k + 1)
            batch(B - 1, 1, B - 2)
            batch(None, 0, B - 1)

        @block.sync
        def _(sp):
            start_at_one(sp)
            for dst, src in ((wgs[:], wg), (wa[:], w31.rearrange("e d f -> d e f")),
                             (wb[:], w32.rearrange("e d f -> d e f")),
                             (wc[:], w33.rearrange("e (k f) d -> f e k d", f=P))):
                sp.dma_start(dst, src).then_inc(ffn1_in, 16)
            sp.wait_ge(ffn1_in, 1 + 64)

        @block.gpsimd
        def _(pool):
            nc.gpsimd.memset(mxx[:].rearrange("p t g s c -> p (t g s c)"), 0.0)
            for u in range(2):
                nc.gpsimd.memset(va[u][:].rearrange("p t h d -> p (t h d)"), 0.0).then_inc(pool_set, 1)
            pool.wait_ge(pool_set, 1 + 2)
            for u in range(2):
                nc.gpsimd.memset(va[u][:, :, :, HD:HD + 1], 1.0).then_inc(pool_set, 1)
            with pool.Fori(0, B) as b:
                pool.wait_ge(proj_ready, 1 + PJ * b)
                nc.gpsimd.tensor_copy(xb[:], xT_all[:, bass.ds(b * L, L)]).then_inc(staged, 1)
            pool.wait_ge(ffn1_in, 1 + 64)
            for high, whole in ((wah, wa), (wbh, wb)):
                last = nc.gpsimd.tensor_copy(flat2(high[:]), flat2(whole[:]))
            last.then_inc(ffn1_high, 1)
            pool.wait_ge(ffn1_high, 1 + 1)
            for low, high, whole in ((wal, wah, wa), (wbl, wbh, wb)):
                nc.gpsimd.tensor_tensor(flat2(low[:]), flat2(whole[:]), flat2(high[:]).bitcast(F32), ALU.subtract)

        @block.tensor
        def _(pe):
            pe.wait_ge(begun5, 1)

            def project(b, i, which, pair, waits=True):
                pe.wait_ge(proj_used, PJ * b + i) if waits else None
                for j in range(2):
                    g = 2 * pair + j
                    last = nc.tensor.matmul(qk_ps[i % 2][:, j * L:(j + 1) * L], wqk[:, which, g, :], xb[:],
                                            start=True, stop=(i < 4))
                    if i >= 4:
                        for t in range(2):
                            last = nc.tensor.matmul(qk_ps[i % 2][:, j * L + t * P:j * L + (t + 1) * P],
                                                    mxx[:, t, g, :, :].rearrange("p s c -> p (s c)"), ident[:],
                                                    start=False, stop=(t == 1))
                last.then_inc(proj_ready, 1)

            def scores(b, u, h, out_ps, stat, mov, ready):
                rows = slice(32 * (h % 4), 32 * (h % 4) + 32)
                for t in range(2):
                    last = nc.tensor.matmul(out_ps[h % 2][:, t * L:(t + 1) * L],
                                            stat[u][rows, h // 4, t * P:(t + 1) * P], mov[u][rows, h // 4, :],
                                            start=True, stop=True, tile_position=(32 * (h % 4), 0))
                last.then_inc(ready, 1)

            def values(b, u, h):
                pe.wait_ge(p_ready, 1 + 16 * b + h + 1)
                if h == 0:
                    pe.wait_ge(os_ready, 1 + b)
                slot = slice(32 * (h % 4), 32 * (h % 4) + 32)
                g = h // 4
                for tk in range(2):
                    last = nc.tensor.matmul(o_ps[g // 2][slot, (g % 2) * L:(g % 2 + 1) * L], va[u][:, tk, h, :],
                                            pt[h % 4][:, tk, :], start=(tk == 0), stop=(tk == 1),
                                            tile_position=(0, 32 * (h % 4)))
                last.then_inc(pv_ready, 1)

            def batch(b, u, before):
                if b is not None:
                    pe.wait_ge(staged, 1 + b + 1)
                    if before is not None:
                        pe.wait_ge(o_ready, 1 + before)
                    for i, (which, pair) in enumerate(((1, 0), (1, 1), (0, 0), (0, 1))):
                        project(b, i, which, pair, before is not None or i >= 2)
                    if before is not None:
                        pe.wait_ge(s_used, 1 + 16 * b)
                    for t in range(2):
                        nc.tensor.matmul(v_ps[:, t * C:(t + 1) * C], xb[:, t * P:(t + 1) * P], wvs[:],
                                         start=True, stop=False)
                        last = nc.tensor.matmul(v_ps[:, t * C:(t + 1) * C], ones_row[:], bvr[:],
                                                start=False, stop=True)
                    last.then_inc(v_ready, 1)
                if before is not None:
                    pe.wait_ge(proj_used, 1 + PJ * before + PJ)
                for h in range(NH + 2):
                    if before is not None and h < NH:
                        if h >= 2:
                            pe.wait_ge(p_ready, 1 + 16 * before + h - 1)
                        scores(before, 1 - u, h, st_ps, kf, qf, st_ready)
                    if b is not None and h < NH:
                        if h == 0:
                            pe.wait_ge(proj_used, 1 + PJ * b + 4)
                            pe.wait_ge(v_used, 1 + b + 1)
                        if h == 1 and before is not None:
                            pe.wait_ge(pj_used, 1 + before)
                        if h >= 2:
                            pe.wait_ge(s_used, 1 + 16 * b + h - 1)
                        scores(b, u, h, s_ps, qf, kf, s_ready)
                    if before is not None and h >= 2:
                        values(before, 1 - u, h - 2)
                if b is not None:
                    pe.wait_ge(max_ready, 1 + b + 1)
                    project(b, 4, 0, 0)
                    project(b, 5, 0, 1)
                if before is not None:
                    pe.wait_ge(os_ready, 1 + before + 1)
                    if b is not None:
                        pe.wait_ge(proj_used, 1 + PJ * b + 6)
                    for t in range(2):
                        for g in range(4):
                            last = nc.tensor.transpose(qk_ps[t][:, g * P:(g + 1) * P],
                                                       os_[:, g // 2, (g % 2) * L + t * P:(g % 2) * L + (t + 1) * P],
                                                       ident[:])
                    last.then_inc(ob_ready, 1)
                    pe.wait_ge(o_ready, 1 + before + 1)
                    for t in range(2):
                        last = nc.tensor.transpose(tail_ps[:, t * P:(t + 1) * P], o[:, t, :], ident[:])
                    last.then_inc(ot_ready, 1)
                    pe.wait_ge(oT_done, 1 + before + 1)
                    for t in range(2):
                        nc.tensor.matmul(tail_ps[:, L + t * C:L + (t + 1) * C], oT[:, t * P:(t + 1) * P], pw[:],
                                         start=True, stop=False)
                        last = nc.tensor.matmul(tail_ps[:, L + t * C:L + (t + 1) * C], ones_row[:], pbr[:],
                                                start=False, stop=True)
                    last.then_inc(pj_ready, 1)

            in_turn(pe, batch)

        @block.scalar
        def _(act):
            act.wait_ge(begun5, 1)

            def high(b, i, which, pair):
                act.wait_ge(proj_ready, 1 + PJ * b + i + 1)
                for j in range(2):
                    g = 2 * pair + j
                    last = nc.scalar.activation(hi[i % 2][:, j, :], qk_ps[i % 2][:, j * L:(j + 1) * L], ACT.Identity,
                                                bias=lo_bias[:, which, g:g + 1], scale=lo_row[:, which:which + 1])
                last.then_inc(hi_ready, 1)

            def batch(b, u, before):
                if b is not None:
                    for i, (which, pair) in enumerate(((1, 0), (1, 1), (0, 0), (0, 1))):
                        high(b, i, which, pair)
                if before is not None:
                    for h in range(NH):
                        act.wait_ge(st_ready, 1 + 16 * before + h + 1)
                        if h >= 4:
                            act.wait_ge(pv_ready, 1 + 16 * before + h - 3)
                        nc.scalar.activation(pt[h % 4][:].rearrange("p t q -> p (t q)"), st_ps[h % 2][:],
                                             ACT.Exp, scale=SCALE).then_inc(p_ready, 1)
                    act.wait_ge(pv_ready, 1 + 16 * before + 16)
                    for j in range(2):
                        last = nc.scalar.copy(os_[:, j, :], o_ps[j][:])
                    last.then_inc(os_ready, 1)
                if b is not None:
                    high(b, 4, 0, 0)
                    high(b, 5, 0, 1)

            in_turn(act, batch)

        @block.vector
        def _(v):
            v.wait_ge(begun5, 1)
            v.wait_ge(pool_set, 1 + 4)

            def split(b, i, u, which, pair):
                v.wait_ge(hi_ready, 1 + PJ * b + i + 1)
                dst = (qf, kf)[which][u]
                for j in range(2):
                    g = 2 * pair + j
                    last = nc.vector.scalar_tensor_tensor(dst[:, g, :], qk_ps[i % 2][:, j * L:(j + 1) * L],
                                                          bqk[:, which, g:g + 1], hi[i % 2][:, j, :].bitcast(F32),
                                                          ALU.add, ALU.subtract)
                last.then_inc(proj_used, 1)

            def batch(b, u, before):
                if b is not None:
                    for i, (which, pair) in enumerate(((1, 0), (1, 1), (0, 0), (0, 1))):
                        split(b, i, u, which, pair)
                    v.wait_ge(v_ready, 1 + b + 1)
                    nc.vector.tensor_copy(va[u][:, :, :, 0:HD],
                                          v_ps[:, 0:2 * C].rearrange("p (t h d) -> p t h d", t=2, h=NH))\
                        .then_inc(v_used, 1)
                    for h in range(NH):
                        v.wait_ge(s_ready, 1 + 16 * b + h + 1)
                        nc.vector.tensor_reduce(mx[:, :, h:h + 1], s_ps[h % 2][:].rearrange("p (t k) -> p t k", t=2),
                                                AX, ALU.max).then_inc(s_used, 1)
                    v.wait_ge(s_used, 1 + 16 * b + 16)
                    for t in range(2):
                        for c in range(2):
                            last = nc.vector.tensor_scalar(
                                mxx[:, t, :, :, 3 * HD + c:3 * HD + c + 1].rearrange("p g s c -> p (g s) c"),
                                bc(mx[:, t, :], 2, 1), -1.0, None, ALU.mult)
                    last.then_inc(max_ready, 1)
                if b is not None:
                    split(b, 4, u, 0, 0)
                    split(b, 5, u, 0, 1)
                if before is not None:
                    v.wait_ge(ob_ready, 1 + before + 1)
                    link = loop_link(dve, v, before, 1)
                    heads = [qk_ps[t][:].rearrange("p (h d) -> p h d", h=NH) for t in range(2)]
                    for t in range(2):
                        ins = nc.vector.reciprocal(den[:, t, :],
                                                   heads[t][:, :, HD:HD + 1].rearrange("p h d -> p (h d)"))
                    link(ins)
                    for t in range(2):
                        last = nc.vector.tensor_tensor(o[:, t, :].rearrange("p (h d) -> p h d", h=NH),
                                                       heads[t][:, :, 0:HD], bc(den[:, t, :], 2, HD), ALU.mult)
                    last.then_inc(o_ready, 1)
                    v.wait_ge(ot_ready, 1 + before + 1)
                    nc.vector.tensor_copy(oT[:], tail_ps[:, 0:L]).then_inc(oT_done, 1)
                    v.wait_ge(pj_ready, 1 + before + 1)
                    x2 = xs_all[:, bass.ds(before * 2, 2), :]
                    nc.vector.tensor_tensor(x2, tail_ps[:, L:L + 2 * C].rearrange("p (t c) -> p t c", t=2), x2, ALU.add)\
                        .then_inc(pj_used, 1)

            in_turn(v, batch)

    with ExitStack() as ctx:
        sb, ps, sem = alloc(ctx)
        it8 = sb("it86", [P, E])
        xc = sb("xc", [P, TOK])
        xch, xcl = sb("xch", [P, TOK], F32R), sb("xcl", [P, TOK], F32R)
        lg = sb("lg6", [P, NT, E])
        m8 = sb("m86", [P, NT, 8])
        i8 = sb("i86", [P, NT, 8], U32)
        i8f = sb("i8f6", [P, NT, 2])
        dd = sb("dd6", [P, NT, 2])
        wd = sb("wd6", [P, NT, E])
        act_h = [sb(f"act_h{u}", [P, 2, CH]) for u in range(2)]
        hid = [sb(f"hid{u}", [P, 2, CH]) for u in range(2)]
        y = sb("y6", [P, NT, C])
        stats = sb("stats6", [P, NT, 6])
        mv = sb("mv6", [P, NT, 2])
        std = sb("std6", [P, NT])
        moe = sb("moe6", [P, NT, C])
        work = ps("work6", [P, TC, 512])
        h_ps = [work[:, u, :] for u in range(2)]
        g_ps = [work[:, 2 + u, :] for u in range(2)]
        eo = [ps(f"eo6{u}", [P, 512]) for u in range(2)]
        names = ("it8_set staged6 lg_ready6 exp_go6 exp_done6 h_ready6 g_ready6 silu_done hid_done e_ready6 e_used6 "
                 "sq_go6 sq_done6 y_ready6 stored dve6 dve_loop6 x3_ready t_ready6 "
                 "x_high6 x_low6 begun6").split()
        S = {k: sem(k) for k in names}
        block = ctx.enter_context(nc.Block())

        @block.sync
        def _(sp):
            start_at_one(sp)
            for b in range(NT // TC):
                sp.wait_ge(S["y_ready6"], 1 + b + 1)
                sp.dma_start(out[b * CH:(b + 1) * CH, :].rearrange("(t p) c -> p t c", p=P),
                             y[:, b * TC:(b + 1) * TC, :]).then_inc(S["stored"], 16)
            sp.wait_ge(S["stored"], 1 + 16 * (NT // TC))

        @block.gpsimd
        def _(pool):
            nc.gpsimd.iota(it8[:], pattern=[[1, E]], base=0, channel_multiplier=0,
                           allow_small_or_imprecise_dtypes=True).then_inc(S["it8_set"], 1)
            for b in range(NT // TC):
                part = slice(b * CH, (b + 1) * CH)
                pool.wait_ge(S["x_high6"], 1 + b + 1)
                nc.gpsimd.tensor_tensor(xcl[:, part], xc[:, part], xch[:, part].bitcast(F32), ALU.subtract)\
                    .then_inc(S["x_low6"], 1)

        @block.tensor
        def _(pe):
            pe.wait_ge(S["begun6"], 1)
            pe.wait_ge(S["x3_ready"], 1 + 1)
            for t in range(NT):
                last = nc.tensor.transpose(work[:, t // TC, (t % TC) * P:(t % TC + 1) * P], moe[:, t, :], ident[:])
                if t % TC == TC - 1:
                    last.then_inc(S["t_ready6"], 1)
            pe.wait_ge(S["staged6"], 1 + NT // TC)
            for t in range(NT):
                last = nc.tensor.matmul(eo[1][:, t * E:(t + 1) * E], xc[:, t * P:(t + 1) * P], wgs[:],
                                        start=True, stop=True)
            last.then_inc(S["lg_ready6"], 1)
            pe.wait_ge(S["x_low6"], 1 + NT // TC)
            with pe.Fori(0, TOK // CH) as q:
                def up(e):
                    for k in range(2):
                        pe.wait_ge(S["hid_done"], 1 + q * 16 + 2 * e + k - 1) if e + k >= 1 else \
                            pe.wait_ge(S["hid_done"], 1 + q * 16)
                        for dst, high, low, ready in ((h_ps[k], wah, wal, S["h_ready6"]),
                                                      (g_ps[k], wbh, wbl, S["g_ready6"])):
                            for i, (w, x) in enumerate(((high, xch), (high, xcl), (low, xch))):
                                last = nc.tensor.matmul(dst, w[:, e, k * P:(k + 1) * P], x[:, bass.ds(q * CH, CH)],
                                                        start=(i == 0), stop=(i == 2))
                            last.then_inc(ready, 1)

                def down(e):
                    pe.wait_ge(S["hid_done"], 1 + q * 16 + 2 * e + 2)
                    pe.wait_ge(S["e_used6"], 1 + q * E + e - 1) if e >= 1 else pe.wait_ge(S["e_used6"], 1 + q * E)
                    for t in range(TC):
                        for k in range(2):
                            last = nc.tensor.matmul(eo[e % 2][:, t * C:(t + 1) * C], hid[e % 2][:, k, t * P:(t + 1) * P],
                                                    wc[:, e, k, :], start=(k == 0), stop=(k == 1))
                    last.then_inc(S["e_ready6"], 1)

                up(0)
                for e in range(1, E):
                    up(e)
                    down(e - 1)
                down(E - 1)

        @block.scalar
        def _(act):
            act.wait_ge(S["begun6"], 1)

            def root(n):
                act.wait_ge(S["sq_go6"], 1 + n + 1)
                nc.scalar.activation(std[:], mv[:, :, 1], ACT.Sqrt, bias=eps_t[:], scale=1.0 / C)\
                    .then_inc(S["sq_done6"], 1)
            root(0)
            for b in range(NT // TC):
                act.wait_ge(S["staged6"], 1 + b + 1)
                nc.scalar.copy(xch[:, b * CH:(b + 1) * CH], xc[:, b * CH:(b + 1) * CH]).then_inc(S["x_high6"], 1)
            act.wait_ge(S["exp_go6"], 1 + 1)
            nc.scalar.activation(dd[:, :, 0:1], dd[:, :, 0:1], ACT.Exp).then_inc(S["exp_done6"], 1)
            with act.Fori(0, TOK // CH) as q:
                for m in range(16):
                    e, k = m // 2, m % 2
                    act.wait_ge(S["h_ready6"], 1 + q * 16 + m + 1)
                    if m >= 4:
                        act.wait_ge(S["hid_done"], 1 + q * 16 + m - 3)
                    nc.scalar.activation(act_h[e % 2][:, k, :], h_ps[k], ACT.Silu).then_inc(S["silu_done"], 1)
            root(1)

        @block.vector
        def _(v):
            v.wait_ge(S["it8_set"], 1 + 1)
            v.wait_ge(S["begun6"], 1)
            link = V(nc, (S["dve6"], [0]), v)
            norm_link(link, v, xs_all, moe, mv, stats, std, S["sq_go6"], S["sq_done6"], 0, NT, S["x3_ready"])
            for b in range(NT // TC):
                v.wait_ge(S["t_ready6"], 1 + b + 1)
                nc.vector.tensor_copy(xc[:, b * CH:(b + 1) * CH], work[:, b, :]).then_inc(S["staged6"], 1)
            v.wait_ge(S["lg_ready6"], 1 + 1)
            route_link(link, v, eo[1][:, 0:NT * E].rearrange("p (t e) -> p t e", t=NT), lg, m8, i8, i8f, dd, wd,
                       it8, S["exp_go6"], S["exp_done6"])
            with v.Fori(0, TOK // CH) as q:
                linked = loop_link(S["dve_loop6"], v, q, E * (TC - 1))

                def gated(e):
                    for k in range(2):
                        m = 2 * e + k
                        v.wait_ge(S["silu_done"], 1 + q * 16 + m + 1)
                        v.wait_ge(S["g_ready6"], 1 + q * 16 + m + 1)
                        if e >= 1:
                            v.wait_ge(S["e_ready6"], 1 + q * E + e - 1)
                        nc.vector.tensor_tensor(hid[e % 2][:, k, :], act_h[e % 2][:, k, :], g_ps[k], ALU.mult)\
                            .then_inc(S["hid_done"], 1)

                def combine(e):
                    v.wait_ge(S["e_ready6"], 1 + q * E + e + 1)
                    for t in range(TC):
                        tile = bass.ds(q * TC + t, 1)
                        acc = moe[:, tile, :].rearrange("p a c -> p (a c)")
                        ins = nc.vector.scalar_tensor_tensor(acc, eo[e % 2][:, t * C:(t + 1) * C],
                                                             wd[:, tile, e:e + 1].rearrange("p a c -> p (a c)"), acc,
                                                             ALU.mult, ALU.add)
                        if t < TC - 1:
                            linked(ins)
                        else:
                            ins.then_inc(S["e_used6"], 1)
                            v.wait_ge(S["e_used6"], 1 + q * E + e + 1)
                gated(0)
                for e in range(1, E):
                    gated(e)
                    combine(e - 1)
                combine(E - 1)
            norm_link(link, v, moe, y, mv, stats, std, S["sq_go6"], S["sq_done6"], 1, NT, S["y_ready6"], NT // TC)


def kernel(**inputs):
    import numpy as np
    import concourse.bacc as bacc
    from concourse.bass_utils import run_bass_kernel_spmd

    a = {k: np.asarray(v) for k, v in inputs.items()}
    x = a["L0_attn_x"].reshape(TOK, C)
    f32 = np.float32
    ar = {}
    ar["x_tok"] = x
    ar["x_T"] = x.T
    ar["x_conv"] = x.reshape(2, GB, A32, R8, C).transpose(3, 0, 4, 1, 2).reshape(NT, C, P)
    ww = a["L0_attn_wave_w"].reshape(H0, 2, C).transpose(2, 1, 0).reshape(C, 2 * H0)
    ar["kw"] = np.concatenate([a["L0_attn_kernel_w"].T, ww], axis=1)
    ar["kbias"] = np.concatenate([a["L0_attn_kernel_b"],
                                  a["L0_attn_wave_b"].reshape(H0, 2).T.reshape(-1)])
    ar["kbias"] = np.broadcast_to(ar["kbias"].reshape(1, -1), (P, H0 * (BINS + 2)))
    ar["outwT"] = a["L0_attn_out_w"].T
    ar["head_rows"] = np.repeat(np.eye(H0, dtype=f32), D0, axis=0)
    cst = np.zeros((P, VW + 1), f32)
    cst[:, :VW] = np.arange(VW) - R8
    cst[:, VW] = R8 * (np.arange(P) % A32)
    ar["cst"] = cst
    edges = np.zeros((P, R8, NE_), f32)
    edges[:, :, :BINS + 1] = np.arange(BINS + 1) * R8 - L
    edges[:, :, 0], edges[:, :, BINS] = -1e6, 1e6
    pos = R8 * (np.arange(P) % A32)[:, None] + np.arange(R8)[None, :]
    edges[:, :, BINS + 1] = -pos
    edges[:, :, BINS + 2] = L - 1 - pos
    ar["edges"] = edges
    ar["ident_d"] = np.eye(P, dtype=f32)
    ar["ln_gb"] = np.stack([a["L0_ffn_ln_g"], a["L0_ffn_ln_b"]], axis=1)
    ar["abel_w"], ar["abel_b"] = a["L0_ffn_abel_w"], a["L0_ffn_abel_b"].reshape(1, C)
    ar["gate_w"], ar["gate_b"] = a["L0_ffn_gate_w_moe"], np.broadcast_to(
        a["L0_ffn_gate_b_moe"].reshape(1, E), (P, E))
    ar["w1"], ar["b1"] = a["L0_ffn_w1"], a["L0_ffn_b1"].reshape(E * 4, P).T
    ar["w2"], ar["b2"] = a["L0_ffn_w2"], a["L0_ffn_b2"]
    gens = a["L0_ffn_gens"]
    ar["gens"] = np.concatenate([gens, gens.transpose(0, 2, 1)], axis=0)
    ar["mix_w"] = np.broadcast_to(a["L0_ffn_mix_w"].reshape(1, 2 * C), (P, 2 * C))
    ar["mix_b"] = np.broadcast_to(a["L0_ffn_mix_b"].reshape(1, 1), (P, 1))
    wq = a["L1_attn_qkv_w"][:2 * C].reshape(2, 4, 4, HD, C).transpose(4, 0, 1, 2, 3)
    bq = a["L1_attn_qkv_b"][:2 * C].reshape(2, 4, 4, HD).transpose(2, 3, 0, 1)
    wqk = np.zeros((C, 2, 4, 4, 32), f32)
    bqk = np.zeros((4, 32, 2, 4), f32)
    for k in range(3):
        wqk[..., k * HD:(k + 1) * HD] = wq
        bqk[:, k * HD:(k + 1) * HD] = bq
    bqk[:, 3 * HD:3 * HD + 2, 1, :] = 1.0
    lo = np.zeros((4, 32, 2), f32)
    lo[:, HD:2 * HD, 0] = lo[:, 3 * HD + 1, 0] = lo[:, 2 * HD:3 * HD, 1] = 1.0
    lo_bias = np.where(lo[..., None] > 0, bqk, f32(0))
    ar["wqkv"] = wqk.reshape(C, 2 * 4 * P)
    ar["bqkv"] = np.concatenate([bqk.reshape(P, 8), lo_bias.reshape(P, 8), lo.reshape(P, 2)], axis=1)
    ar["wv"], ar["bv"] = a["L1_attn_qkv_w"][2 * C:].T, a["L1_attn_qkv_b"][2 * C:].reshape(1, C)
    ar["proj_w"], ar["proj_b"] = a["L1_attn_proj_w"].T, a["L1_attn_proj_b"].reshape(1, C)
    ar["wg"], ar["w31"], ar["w32"], ar["w33"] = (a[f"L1_ffn_{k}"] for k in ("Wg", "W1", "W2", "W3"))

    nc = bacc.Bacc("TRN2", target_bir_lowering=False, num_devices=1)
    args, arrays = {}, {}
    for name, arr in ar.items():
        arrays[f"in_{name}"] = np.ascontiguousarray(arr)
        args[name] = nc.dram_tensor(f"in_{name}", arr.shape, F32, kind="ExternalInput").ap()
    kd = nc.dram_tensor("kd", (NT, P, H0 * BINS), F32, kind="Internal").ap()
    out = nc.dram_tensor("out_0", (TOK, C), F32, kind="ExternalOutput").ap()
    build(nc, kd=kd, out=out, **args)
    r = run_bass_kernel_spmd(nc, [arrays], core_ids=[0])
    return r.results[0]["out_0"].reshape(B, L, C)
```
